# Optimizing a Trainium2 kernel written in Bass

```python
import numpy as np
import jax
import jax.numpy as jnp

def _softmax(x, axis=-1):
    return jax.nn.softmax(x, axis=axis)

def _gelu(x):
    return jax.nn.gelu(x, approximate=True)

def _silu(x):
    return jax.nn.silu(x)

def _sigmoid(x):
    return jax.nn.sigmoid(x)

def _layernorm(x, axis=-1, eps=1e-05):
    m = jnp.mean(x, axis=axis, keepdims=True)
    v = jnp.var(x, axis=axis, keepdims=True)
    return (x - m) / jnp.sqrt(v + eps)

def _scatter_add(tgt, idx, src, axis=0):
    return tgt.at[idx].add(src)

def _segment_sum(src, seg, n):
    return jax.ops.segment_sum(src, seg, n)
kernel_name = 'mk_decoder_preln_d2_seqx_r4_2ef29a'

def setup_inputs(seed: int=0):
    np.random.seed(seed)
    _w = jnp.asarray

    def _rec_inputs():
        import jax
        import jax.numpy as jnp
        _rk = jax.random.key(seed)
        x = -0.0005146 + 1 * jax.random.normal(jax.random.fold_in(_rk, 1), (4, 1024, 256), jnp.float32)
        _lenS = 1024 - jax.random.randint(jax.random.fold_in(_rk, 7), (4,), 0, max(1, 1024 // 4) + 1, jnp.int32)
        _lenS2 = 77 - jax.random.randint(jax.random.fold_in(_rk, 8), (4,), 0, max(1, 77 // 4) + 1, jnp.int32)
        _ctx_1024P = jax.random.normal(jax.random.fold_in(_rk, 11), (4, 16, 256), jnp.float32)
        _ctx_1024c = jax.random.dirichlet(jax.random.fold_in(_rk, 511), 0.3 * jnp.ones((16,), jnp.float32), (4, 77))
        _ctx_1024t = jnp.einsum('bsk,bkd->bsd', _ctx_1024c, _ctx_1024P)
        _ctx_1024t = _ctx_1024t * jax.lax.rsqrt(jnp.mean(jnp.square(_ctx_1024t)) + 1e-12) * 0.953939
        ctx_1024 = -7.10856e-05 + 0.999911 * (_ctx_1024t + 0.3 * jax.random.normal(jax.random.fold_in(_rk, 611), (4, 77, 256), jnp.float32))
        _validS = jnp.arange(1024)[None, :] < _lenS[:, None]
        _validS2 = jnp.arange(77)[None, :] < _lenS2[:, None]
        _causal = jnp.tril(jnp.ones((1024, 1024), dtype=bool))
        mask_BxS2_if1 = jnp.where(jnp.ones((4, 77), dtype=bool), 1, 0).astype(jnp.int32)
        return (x, ctx_1024, mask_BxS2_if1)
    x, ctx_1024, mask_BxS2_if1 = _rec_inputs()

    def _L0_attn_setup():
        import jax, jax.numpy as jnp
        import numpy as np
        D_MODEL, D_STATE, D_CONV, D_INNER, DT_RANK = (256, 16, 4, 512, 64)
        BATCH, LENGTH = (4, 512)

        def _mamba_fwd(x, W_in, conv_w, conv_b, W_x, W_dt, b_dt, A_raw, D, W_out):
            b, l, _ = x.shape
            d_inner = W_in.shape[0] // 2
            d_state = A_raw.shape[0]
            dt_rank = W_dt.shape[1]
            xz = jnp.einsum('bld,ed->ble', x, W_in)
            xc, z = jnp.split(xz, 2, axis=-1)
            xc = xc.transpose(0, 2, 1)
            k = conv_w.shape[-1]
            xc = jax.lax.conv_general_dilated(xc, conv_w, (1,), [(k - 1, 0)], dimension_numbers=('NCH', 'OIH', 'NCH'), feature_group_count=d_inner) + conv_b[None, :, None]
            xc = jax.nn.silu(xc).transpose(0, 2, 1)
            dbc = jnp.einsum('bld,ed->ble', xc, W_x)
            dt, B, C = jnp.split(dbc, [dt_rank, dt_rank + d_state], axis=-1)
            delta = jax.nn.softplus(jnp.einsum('blr,dr->bld', dt, W_dt) + b_dt)
            A = -jnp.exp(A_raw)

            def step(h, inp):
                x_t, dlt, B_t, C_t = inp
                dA = jnp.exp(dlt[:, None, :] * A[None])
                h = dA * h + dlt[:, None, :] * B_t[:, :, None] * x_t[:, None, :]
                y_t = jnp.einsum('bn,bnd->bd', C_t, h) + D * x_t
                return (h, y_t)
            h0 = jnp.zeros((b, d_state, d_inner), x.dtype)
            xs = (xc.transpose(1, 0, 2), delta.transpose(1, 0, 2), B.transpose(1, 0, 2), C.transpose(1, 0, 2))
            _, ys = jax.lax.scan(step, h0, xs)
            y = ys.transpose(1, 0, 2) * jax.nn.silu(z)
            return jnp.einsum('bld,md->blm', y, W_out)
        key = jax.random.key(seed)
        ks = jax.random.split(key, 10)
        dt_init_std = DT_RANK ** (-0.5)
        dt_min, dt_max, dt_floor = (0.001, 0.1, 0.0001)
        u = jax.random.uniform(ks[9], (D_INNER,))
        dt = jnp.clip(jnp.exp(u * (np.log(dt_max) - np.log(dt_min)) + np.log(dt_min)), dt_floor, None)
        b_dt = dt + jnp.log(-jnp.expm1(-dt))
        return {'x': jax.random.normal(ks[0], (BATCH, LENGTH, D_MODEL), jnp.float32), 'W_in': jax.random.normal(ks[1], (2 * D_INNER, D_MODEL), jnp.float32) * D_MODEL ** (-0.5), 'conv_w': jax.random.normal(ks[2], (D_INNER, 1, D_CONV), jnp.float32) * D_CONV ** (-0.5), 'conv_b': jax.random.normal(ks[3], (D_INNER,), jnp.float32) * 0.01, 'W_x': jax.random.normal(ks[4], (DT_RANK + 2 * D_STATE, D_INNER), jnp.float32) * D_INNER ** (-0.5), 'W_dt': jax.random.uniform(ks[5], (D_INNER, DT_RANK), jnp.float32, -dt_init_std, dt_init_std), 'b_dt': b_dt.astype(jnp.float32), 'A_raw': jax.random.normal(ks[6], (D_STATE, D_INNER), jnp.float32), 'D': jax.random.normal(ks[7], (D_INNER,), jnp.float32), 'W_out': jax.random.normal(ks[8], (D_MODEL, D_INNER), jnp.float32) * D_INNER ** (-0.5)}
    _L0_attn_all = _L0_attn_setup()
    _L0_attn_in = {k: v for k, v in _L0_attn_all.items() if k in ('W_in', 'conv_w', 'conv_b', 'W_x', 'W_dt', 'b_dt', 'A_raw', 'D', 'W_out')}
    del _L0_attn_all

    def _L0_xattn_setup():
        import jax, jax.numpy as jnp
        import numpy as np
        B, L, P, D = (32, 512, 64, 256)
        MAX_HOP = 2
        key = jax.random.key(seed)
        k1, k2, k3, k4 = jax.random.split(key, 4)
        return {'context': jax.random.normal(k1, (B, L, D), dtype=jnp.float32), 'mem0': jax.random.normal(k2, (B, P, D), dtype=jnp.float32), 'W0': jax.random.normal(k3, (D, D), dtype=jnp.float32) * 0.02, 'W1': jax.random.normal(k4, (D, D), dtype=jnp.float32) * 0.02, 'mask': jnp.ones((B, L), dtype=jnp.int32)}
    _L0_xattn_all = _L0_xattn_setup()
    _L0_xattn_in = {k: v for k, v in _L0_xattn_all.items() if k in ('W0', 'W1')}
    del _L0_xattn_all

    def _L0_ffn_setup():
        import jax, jax.numpy as jnp
        import numpy as np
        B, T, D = (2, 512, 256)
        DCD = 1024
        RET = 128
        NEXP = 1024
        NKEYS = 64
        H = 4
        KPH = 8
        key = jax.random.key(seed)
        ks = jax.random.split(key, 10)
        s = lambda k, shape, scale: jax.random.normal(k, shape, jnp.float32) * scale
        return {'hidden_states': jax.random.normal(ks[0], (B, T, D), jnp.float32), 'Wg': s(ks[1], (D, DCD), 0.02), 'bg': jnp.zeros((DCD,), jnp.float32), 'Wu': s(ks[2], (D, DCD), 0.02), 'bu': jnp.zeros((DCD,), jnp.float32), 'Wd': s(ks[3], (DCD, D), 0.02), 'bd': jnp.zeros((D,), jnp.float32), 'Wq': s(ks[4], (D, RET * H), 0.02), 'keys': s(ks[5], (H, NKEYS, 2, RET // 2), 0.02), 'down_embed': s(ks[6], (NEXP, D), 0.02), 'up_embed': s(ks[7], (NEXP, D), 0.02)}
    _L0_ffn_all = _L0_ffn_setup()
    _L0_ffn_in = {k: v for k, v in _L0_ffn_all.items() if k in ('Wg', 'bg', 'Wu', 'bu', 'Wd', 'bd', 'Wq', 'keys', 'down_embed', 'up_embed')}
    del _L0_ffn_all

    def _L1_attn_setup():
        import jax, jax.numpy as jnp
        import numpy as np
        from jax import lax
        NUM_LEVELS = 2
        NUM_HEADS = 16
        LN_EPS = 1e-05
        ATTN_EPS = 1e-06

        def dwconv(x, filt):
            C = x.shape[-1]
            return lax.conv_general_dilated(x, filt[:, None, :], window_strides=(1,), padding='SAME', dimension_numbers=('NWC', 'WIO', 'NWC'), feature_group_count=C)

        def linear_attention(x, num_heads):
            B, N, C = x.shape
            d = C // num_heads
            h = x.reshape(B, N, num_heads, d)
            q = jax.nn.elu(h) + 1.0
            k = q
            v = h
            kv = jnp.einsum('bnhd,bnhe->bhde', k, v)
            z = k.sum(axis=1)
            num = jnp.einsum('bnhd,bhde->bnhe', q, kv)
            den = jnp.einsum('bnhd,bhd->bnh', q, z)[..., None] + ATTN_EPS
            return (num / den).reshape(B, N, C)

        def layer_norm(x, gamma, beta):
            mu = jnp.mean(x, axis=-1, keepdims=True)
            var = jnp.mean(jnp.square(x - mu), axis=-1, keepdims=True)
            return (x - mu) * lax.rsqrt(var + LN_EPS) * gamma + beta
        key = jax.random.key(seed)
        ks = jax.random.split(key, 7)
        B, S, C, K = (8, 1024, 256, 4)
        x = jax.random.normal(ks[0], (B, S, C), dtype=jnp.float32)
        scale = 1.0 / np.sqrt(K)
        h_filter = jax.random.normal(ks[1], (K, C), dtype=jnp.float32) * scale
        g_filter = jax.random.normal(ks[2], (K, C), dtype=jnp.float32) * scale
        h_synth = jax.random.normal(ks[3], (K, C), dtype=jnp.float32) * scale
        g_synth = jax.random.normal(ks[4], (K, C), dtype=jnp.float32) * scale
        norm_gamma = jnp.ones((C,), dtype=jnp.float32)
        norm_beta = jnp.zeros((C,), dtype=jnp.float32)
        return {'x': x, 'h_filter': h_filter, 'g_filter': g_filter, 'h_synth': h_synth, 'g_synth': g_synth, 'norm_gamma': norm_gamma, 'norm_beta': norm_beta}
    _L1_attn_all = _L1_attn_setup()
    _L1_attn_in = {k: v for k, v in _L1_attn_all.items() if k in ('h_filter', 'g_filter', 'h_synth', 'g_synth', 'norm_gamma', 'norm_beta')}
    del _L1_attn_all

    def _L1_xattn_setup():
        import jax, jax.numpy as jnp
        import numpy as np
        EPS = 1e-05

        def layer_norm(x, g, b):
            mu = jnp.mean(x, axis=-1, keepdims=True)
            var = jnp.var(x, axis=-1, keepdims=True)
            return (x - mu) * jax.lax.rsqrt(var + EPS) * g + b
        key = jax.random.key(seed)
        ks = jax.random.split(key, 8)
        dim, heads, dim_head = (256, 16, 64)
        inner = heads * dim_head
        b, n, m = (8, 1024, 64)
        s = dim ** (-0.5)
        return {'x': jax.random.normal(ks[0], (b, n, dim), jnp.float32), 'latents': jax.random.normal(ks[1], (b, m, dim), jnp.float32), 'ln_m_g': jnp.ones((dim,), jnp.float32), 'ln_m_b': jnp.zeros((dim,), jnp.float32), 'ln_l_g': jnp.ones((dim,), jnp.float32), 'ln_l_b': jnp.zeros((dim,), jnp.float32), 'Wq': jax.random.normal(ks[2], (dim, inner), jnp.float32) * s, 'Wkv': jax.random.normal(ks[3], (dim, 2 * inner), jnp.float32) * s, 'Wout': jax.random.normal(ks[4], (inner, dim), jnp.float32) * s}
    _L1_xattn_all = _L1_xattn_setup()
    _L1_xattn_in = {k: v for k, v in _L1_xattn_all.items() if k in ('ln_m_g', 'ln_m_b', 'ln_l_g', 'ln_l_b', 'Wq', 'Wkv', 'Wout')}
    del _L1_xattn_all

    def _L1_ffn_setup():
        import jax, jax.numpy as jnp
        import numpy as np
        FP8_MAX = 448.0

        def quant_fp8(x):
            amax = jnp.max(jnp.abs(x)).astype(jnp.float32)
            scale = jnp.minimum(FP8_MAX / jnp.maximum(amax, 1e-12), FP8_MAX)
            x_fp8 = jnp.clip(x * scale, -FP8_MAX, FP8_MAX).astype(jnp.float8_e4m3fn)
            return (x_fp8, 1.0 / scale)
        key = jax.random.key(seed)
        k1, k2, k3 = jax.random.split(key, 3)
        B, S, IN, OUT = (4, 2048, 256, 256)
        input = jax.random.normal(k1, (B, S, IN), dtype=jnp.float32)
        bound = 1.0 / np.sqrt(IN)
        weight = jax.random.uniform(k2, (OUT, IN), dtype=jnp.float32, minval=-bound, maxval=bound)
        bias = jax.random.uniform(k3, (OUT,), dtype=jnp.float32, minval=-bound, maxval=bound)
        return {'input': input, 'weight': weight, 'bias': bias}
    _L1_ffn_all = _L1_ffn_setup()
    _L1_ffn_in = {k: v for k, v in _L1_ffn_all.items() if k in ('weight', 'bias')}
    del _L1_ffn_all
    return {'x': x, 'ctx_1024': ctx_1024, 'mask_BxS2_if1': mask_BxS2_if1, 'L0_attn_W_in': _L0_attn_in['W_in'], 'L0_attn_conv_w': _L0_attn_in['conv_w'], 'L0_attn_conv_b': _L0_attn_in['conv_b'], 'L0_attn_W_x': _L0_attn_in['W_x'], 'L0_attn_W_dt': _L0_attn_in['W_dt'], 'L0_attn_b_dt': _L0_attn_in['b_dt'], 'L0_attn_A_raw': _L0_attn_in['A_raw'], 'L0_attn_D': _L0_attn_in['D'], 'L0_attn_W_out': _L0_attn_in['W_out'], 'L0_xattn_W0': _L0_xattn_in['W0'], 'L0_xattn_W1': _L0_xattn_in['W1'], 'L0_ffn_Wg': _L0_ffn_in['Wg'], 'L0_ffn_bg': _L0_ffn_in['bg'], 'L0_ffn_Wu': _L0_ffn_in['Wu'], 'L0_ffn_bu': _L0_ffn_in['bu'], 'L0_ffn_Wd': _L0_ffn_in['Wd'], 'L0_ffn_bd': _L0_ffn_in['bd'], 'L0_ffn_Wq': _L0_ffn_in['Wq'], 'L0_ffn_keys': _L0_ffn_in['keys'], 'L0_ffn_down_embed': _L0_ffn_in['down_embed'], 'L0_ffn_up_embed': _L0_ffn_in['up_embed'], 'L1_attn_h_filter': _L1_attn_in['h_filter'], 'L1_attn_g_filter': _L1_attn_in['g_filter'], 'L1_attn_h_synth': _L1_attn_in['h_synth'], 'L1_attn_g_synth': _L1_attn_in['g_synth'], 'L1_attn_norm_gamma': _L1_attn_in['norm_gamma'], 'L1_attn_norm_beta': _L1_attn_in['norm_beta'], 'L1_xattn_ln_m_g': _L1_xattn_in['ln_m_g'], 'L1_xattn_ln_m_b': _L1_xattn_in['ln_m_b'], 'L1_xattn_ln_l_g': _L1_xattn_in['ln_l_g'], 'L1_xattn_ln_l_b': _L1_xattn_in['ln_l_b'], 'L1_xattn_Wq': _L1_xattn_in['Wq'], 'L1_xattn_Wkv': _L1_xattn_in['Wkv'], 'L1_xattn_Wout': _L1_xattn_in['Wout'], 'L1_ffn_weight': _L1_ffn_in['weight'], 'L1_ffn_bias': _L1_ffn_in['bias']}

def reference(x, ctx_1024, mask_BxS2_if1, L0_attn_W_in, L0_attn_conv_w, L0_attn_conv_b, L0_attn_W_x, L0_attn_W_dt, L0_attn_b_dt, L0_attn_A_raw, L0_attn_D, L0_attn_W_out, L0_xattn_W0, L0_xattn_W1, L0_ffn_Wg, L0_ffn_bg, L0_ffn_Wu, L0_ffn_bu, L0_ffn_Wd, L0_ffn_bd, L0_ffn_Wq, L0_ffn_keys, L0_ffn_down_embed, L0_ffn_up_embed, L1_attn_h_filter, L1_attn_g_filter, L1_attn_h_synth, L1_attn_g_synth, L1_attn_norm_gamma, L1_attn_norm_beta, L1_xattn_ln_m_g, L1_xattn_ln_m_b, L1_xattn_ln_l_g, L1_xattn_ln_l_b, L1_xattn_Wq, L1_xattn_Wkv, L1_xattn_Wout, L1_ffn_weight, L1_ffn_bias):
    import jax
    import jax.numpy as jnp

    def _L0_attn_ref(x, W_in, conv_w, conv_b, W_x, W_dt, b_dt, A_raw, D, W_out):
        import jax, jax.numpy as jnp
        import numpy as np
        D_MODEL, D_STATE, D_CONV, D_INNER, DT_RANK = (256, 16, 4, 512, 64)
        BATCH, LENGTH = (4, 512)

        def _mamba_fwd(x, W_in, conv_w, conv_b, W_x, W_dt, b_dt, A_raw, D, W_out):
            b, l, _ = x.shape
            d_inner = W_in.shape[0] // 2
            d_state = A_raw.shape[0]
            dt_rank = W_dt.shape[1]
            xz = jnp.einsum('bld,ed->ble', x, W_in)
            xc, z = jnp.split(xz, 2, axis=-1)
            xc = xc.transpose(0, 2, 1)
            k = conv_w.shape[-1]
            xc = jax.lax.conv_general_dilated(xc, conv_w, (1,), [(k - 1, 0)], dimension_numbers=('NCH', 'OIH', 'NCH'), feature_group_count=d_inner) + conv_b[None, :, None]
            xc = jax.nn.silu(xc).transpose(0, 2, 1)
            dbc = jnp.einsum('bld,ed->ble', xc, W_x)
            dt, B, C = jnp.split(dbc, [dt_rank, dt_rank + d_state], axis=-1)
            delta = jax.nn.softplus(jnp.einsum('blr,dr->bld', dt, W_dt) + b_dt)
            A = -jnp.exp(A_raw)

            def step(h, inp):
                x_t, dlt, B_t, C_t = inp
                dA = jnp.exp(dlt[:, None, :] * A[None])
                h = dA * h + dlt[:, None, :] * B_t[:, :, None] * x_t[:, None, :]
                y_t = jnp.einsum('bn,bnd->bd', C_t, h) + D * x_t
                return (h, y_t)
            h0 = jnp.zeros((b, d_state, d_inner), x.dtype)
            xs = (xc.transpose(1, 0, 2), delta.transpose(1, 0, 2), B.transpose(1, 0, 2), C.transpose(1, 0, 2))
            _, ys = jax.lax.scan(step, h0, xs)
            y = ys.transpose(1, 0, 2) * jax.nn.silu(z)
            return jnp.einsum('bld,md->blm', y, W_out)
        return _mamba_fwd(x, W_in, conv_w, conv_b, W_x, W_dt, b_dt, A_raw, D, W_out)

    def _L0_xattn_ref(context, mem0, W0, W1, mask):
        import jax, jax.numpy as jnp
        import numpy as np
        B, L, P, D = (32, 512, 64, 256)
        MAX_HOP = 2
        m = (mask == 0)[:, None, :]
        neg_inf = jnp.finfo(context.dtype).min
        u = mem0
        for W in (W0, W1):
            key_ = jnp.einsum('bpd,md->bpm', u, W)
            attn = jnp.einsum('bpm,blm->bpl', key_, context)
            attn = jnp.where(m, neg_inf, attn)
            w = jax.nn.softmax(attn, axis=-1)
            o = jnp.einsum('bpl,bld->bpd', w, context)
            u = u + o
        return u

    def _L0_ffn_ref(hidden_states, Wg, bg, Wu, bu, Wd, bd, Wq, keys, down_embed, up_embed):
        import jax, jax.numpy as jnp
        import numpy as np
        B, T, D = (2, 512, 256)
        DCD = 1024
        RET = 128
        NEXP = 1024
        NKEYS = 64
        H = 4
        KPH = 8
        b, t, d = hidden_states.shape
        q = (hidden_states @ Wq).reshape(b, t, 2, H, RET // 2)
        sim = jnp.einsum('btphn,hkpn->pbthk', q, keys)
        sc, ix = jax.lax.top_k(sim, KPH)
        sx, sy = (sc[0], sc[1])
        ixx, ixy = (ix[0], ix[1])
        all_sc = (sx[..., :, None] + sy[..., None, :]).reshape(b, t, H, KPH * KPH)
        all_ix = (ixx[..., :, None] * NKEYS + ixy[..., None, :]).reshape(b, t, H, KPH * KPH)
        scores, pk = jax.lax.top_k(all_sc, KPH)
        idx = jnp.take_along_axis(all_ix, pk, axis=-1)
        de = down_embed[idx]
        ue = up_embed[idx]
        w = jnp.einsum('btd,bthkd->bthk', hidden_states, de)
        w = jax.nn.silu(w) * jax.nn.softmax(scores, axis=-1)
        experts_states = jnp.einsum('bthk,bthkd->btd', w, ue)
        mlp = jax.nn.silu(hidden_states @ Wg + bg) * (hidden_states @ Wu + bu) @ Wd + bd
        return mlp + experts_states

    def _L1_attn_ref(x, h_filter, g_filter, h_synth, g_synth, norm_gamma, norm_beta):
        import jax, jax.numpy as jnp
        import numpy as np
        from jax import lax
        NUM_LEVELS = 2
        NUM_HEADS = 16
        LN_EPS = 1e-05
        ATTN_EPS = 1e-06

        def dwconv(x, filt):
            C = x.shape[-1]
            return lax.conv_general_dilated(x, filt[:, None, :], window_strides=(1,), padding='SAME', dimension_numbers=('NWC', 'WIO', 'NWC'), feature_group_count=C)

        def linear_attention(x, num_heads):
            B, N, C = x.shape
            d = C // num_heads
            h = x.reshape(B, N, num_heads, d)
            q = jax.nn.elu(h) + 1.0
            k = q
            v = h
            kv = jnp.einsum('bnhd,bnhe->bhde', k, v)
            z = k.sum(axis=1)
            num = jnp.einsum('bnhd,bhde->bnhe', q, kv)
            den = jnp.einsum('bnhd,bhd->bnh', q, z)[..., None] + ATTN_EPS
            return (num / den).reshape(B, N, C)

        def layer_norm(x, gamma, beta):
            mu = jnp.mean(x, axis=-1, keepdims=True)
            var = jnp.mean(jnp.square(x - mu), axis=-1, keepdims=True)
            return (x - mu) * lax.rsqrt(var + LN_EPS) * gamma + beta
        low = x
        highs = []
        lens = []
        for _ in range(NUM_LEVELS):
            lens.append(low.shape[1])
            l = dwconv(low, h_filter)[:, ::2]
            h = dwconv(low, g_filter)[:, ::2]
            highs.append(h)
            low = l
        low = linear_attention(low, NUM_HEADS)
        for h, L in zip(reversed(highs), reversed(lens)):
            up_l = jnp.repeat(low, 2, axis=1)[:, :L]
            up_h = jnp.repeat(h, 2, axis=1)[:, :L]
            low = dwconv(up_l, h_synth) + dwconv(up_h, g_synth)
        return layer_norm(x + low, norm_gamma, norm_beta)

    def _L1_xattn_ref(x, latents, ln_m_g, ln_m_b, ln_l_g, ln_l_b, Wq, Wkv, Wout):
        import jax, jax.numpy as jnp
        import numpy as np
        EPS = 1e-05

        def layer_norm(x, g, b):
            mu = jnp.mean(x, axis=-1, keepdims=True)
            var = jnp.var(x, axis=-1, keepdims=True)
            return (x - mu) * jax.lax.rsqrt(var + EPS) * g + b
        heads, dim_head = (16, 64)
        scale = dim_head ** (-0.5)
        x = layer_norm(x, ln_m_g, ln_m_b)
        lat = layer_norm(latents, ln_l_g, ln_l_b)
        b, m, _ = lat.shape
        q = lat @ Wq
        kv_input = jnp.concatenate([x, lat], axis=1)
        kv = kv_input @ Wkv
        k, v = jnp.split(kv, 2, axis=-1)

        def split_heads(t):
            return t.reshape(t.shape[0], t.shape[1], heads, dim_head).transpose(0, 2, 1, 3)
        q, k, v = (split_heads(q), split_heads(k), split_heads(v))
        dots = jnp.einsum('bhid,bhjd->bhij', q, k) * scale
        attn = jax.nn.softmax(dots, axis=-1)
        out = jnp.einsum('bhij,bhjd->bhid', attn, v)
        out = out.transpose(0, 2, 1, 3).reshape(b, m, heads * dim_head)
        return out @ Wout

    def _L1_ffn_ref(input, weight, bias):
        import jax, jax.numpy as jnp
        import numpy as np
        FP8_MAX = 448.0

        def quant_fp8(x):
            amax = jnp.max(jnp.abs(x)).astype(jnp.float32)
            scale = jnp.minimum(FP8_MAX / jnp.maximum(amax, 1e-12), FP8_MAX)
            x_fp8 = jnp.clip(x * scale, -FP8_MAX, FP8_MAX).astype(jnp.float8_e4m3fn)
            return (x_fp8, 1.0 / scale)
        prev_shape = input.shape
        x2d = input.reshape(-1, weight.shape[1])
        w_fp8, w_scale = quant_fp8(weight)
        x_fp8, x_scale = quant_fp8(x2d)
        acc = jnp.matmul(x_fp8.astype(jnp.float32), w_fp8.astype(jnp.float32).T)
        out2d = (acc * (x_scale * w_scale) + bias).astype(jnp.bfloat16)
        out = out2d.reshape(*prev_shape[:-1], weight.shape[0]).astype(input.dtype)
        return out
    x = x + _L0_attn_ref(_layernorm(x, axis=-1), L0_attn_W_in, L0_attn_conv_w, L0_attn_conv_b, L0_attn_W_x, L0_attn_W_dt, L0_attn_b_dt, L0_attn_A_raw, L0_attn_D, L0_attn_W_out)
    x = x + _L0_xattn_ref(ctx_1024, _layernorm(x, axis=-1), L0_xattn_W0, L0_xattn_W1, mask_BxS2_if1)
    x = x + _L0_ffn_ref(_layernorm(x, axis=-1), L0_ffn_Wg, L0_ffn_bg, L0_ffn_Wu, L0_ffn_bu, L0_ffn_Wd, L0_ffn_bd, L0_ffn_Wq, L0_ffn_keys, L0_ffn_down_embed, L0_ffn_up_embed)
    x = x + _L1_attn_ref(_layernorm(x, axis=-1), L1_attn_h_filter, L1_attn_g_filter, L1_attn_h_synth, L1_attn_g_synth, L1_attn_norm_gamma, L1_attn_norm_beta)
    x = x + _L1_xattn_ref(ctx_1024, _layernorm(x, axis=-1), L1_xattn_ln_m_g, L1_xattn_ln_m_b, L1_xattn_ln_l_g, L1_xattn_ln_l_b, L1_xattn_Wq, L1_xattn_Wkv, L1_xattn_Wout)
    x = x + _L1_ffn_ref(_layernorm(x, axis=-1), L1_ffn_weight, L1_ffn_bias)
    return x

_drawn_inputs = setup_inputs


def setup_inputs(seed=0):
    import zlib

    import numpy as np

    out = dict(_drawn_inputs(seed))
    spreads = {'L0_ffn_bg': (0.0, 0.8),
     'L0_ffn_bu': (0.0, 0.8),
     'L0_ffn_bd': (0.0, 0.372),
     'L1_attn_norm_gamma': (1.0, 0.2),
     'L1_attn_norm_beta': (0.0, 0.434),
     'L1_xattn_ln_m_g': (1.0, 0.6),
     'L1_xattn_ln_m_b': (0.0, 0.8),
     'L1_xattn_ln_l_g': (1.0, 0.2),
     'L1_xattn_ln_l_b': (0.0, 0.284)}
    factors = {'L0_attn_conv_b': 8.0,
     'L0_ffn_Wg': 4.286,
     'L0_ffn_Wu': 4.224,
     'L0_ffn_Wd': 3.969,
     'L0_ffn_Wq': 8.0,
     'L0_ffn_keys': 8.0,
     'L0_ffn_down_embed': 8.0,
     'L0_ffn_up_embed': 8.0,
     'L1_ffn_bias': 5.279}
    for name, (base, spread) in spreads.items():
        noise = np.random.default_rng([zlib.crc32(name.encode()), seed]).standard_normal(out[name].shape)
        drawn = base * np.exp(spread * noise) if base else spread * noise
        out[name] = jnp.asarray(drawn.astype(out[name].dtype))
    for name, factor in factors.items():
        out[name] = (out[name] * factor).astype(out[name].dtype)
    return out
```

```python
from contextlib import ExitStack

import concourse.bass as bass
from concourse import mybir

ALU = mybir.AluOpType
ACT = mybir.ActivationFunctionType
AXIS = mybir.AxisListType
F32 = mybir.dt.float32
BF16 = mybir.dt.bfloat16
I32 = mybir.dt.int32
P = 128
BANK = 512
LN_EPS = 1e-5

BATCH, SEQ, DM = 4, 1024, 256
TILES = SEQ // P
DK = DM // P
HALVES = SEQ // BANK

LAST_STAGE = 6


class Signal:

    def __init__(self, ctx, nc, name):
        self.sem = ctx.enter_context(nc.semaphore(name))


class Chain:

    def __init__(self, steps):
        self.steps, self.count = steps, 0

    def link(self, engine, instruction):
        self.count += 1
        instruction.then_inc(self.steps.sem, 1)
        engine.wait_ge(self.steps.sem, self.count)


class BatchSignals:

    def __init__(self, ctx, nc, prefix):
        self.ctx, self.nc, self.prefix, self.all = ctx, nc, prefix, []

    def __call__(self, name):
        self.all.append(Signal(self.ctx, self.nc, self.prefix + name))
        return self.all[-1]

    def clear(self):
        for signal in self.all:
            self.nc.sync.sem_clear(signal.sem)
        self.nc.all_engine_barrier()


class Prologue(ExitStack):

    def __init__(self, nc):
        super().__init__()
        self.nc, self.semaphores = nc, []

    def semaphore(self, name):
        self.semaphores.append(self.enter_context(self.nc.semaphore(name)))
        return self.semaphores[-1]

    def counter(self, name):
        counter = Signal(self, self.nc, name)
        self.semaphores.append(counter.sem)
        return counter

    def block(self):
        self.callback(self.clear)
        return self.enter_context(self.nc.Block())

    def clear(self):
        for semaphore in self.semaphores:
            self.nc.sync.sem_clear(semaphore)
        self.nc.all_engine_barrier()


class Kernel:

    def __init__(self, nc, ctx, dram):
        self.nc, self.ctx, self.dram = nc, ctx, dram
        self.X = ctx.enter_context(nc.sbuf_tensor("X", [P, BATCH * TILES, DM], F32))
        self.ident = ctx.enter_context(nc.sbuf_tensor("ident", [P, P], F32))
        self.ones = ctx.enter_context(nc.sbuf_tensor("ones", [P, P], F32))


def load_residual(k):
    nc = k.nc
    with Prologue(nc) as pre:
        x_loaded = pre.semaphore("x_loaded")
        ident_filled = pre.semaphore("ident_filled")
        block = pre.block()

        @block.sync
        def _(sp):
            view = k.dram["x"].rearrange("b (j p) d -> b p j d", p=P)
            for b in range(BATCH):
                sp.dma_start(k.X[:, b * TILES:(b + 1) * TILES, :], view[b]).then_inc(x_loaded, 16)
            sp.wait_ge(x_loaded, 16 * BATCH)

        @block.gpsimd
        def _(pool):
            pool.memset(k.ones[:], 1.0).then_inc(ident_filled, 1)
            pool.wait_ge(ident_filled, 1)
            pool.affine_select(out=k.ident[:], in_=k.ones[:], compare_op=ALU.is_equal, fill=0.0,
                               base=0, pattern=[[-1, P]], channel_multiplier=1).then_inc(ident_filled, 1)
            pool.wait_ge(ident_filled, 2)


def store_residual(k):
    nc = k.nc
    with ExitStack() as ctx:
        stored = ctx.enter_context(nc.semaphore("stored"))
        block = ctx.enter_context(nc.Block())

        @block.sync
        def _(sp):
            view = k.dram["out"].rearrange("b (j p) d -> b p j d", p=P)
            for b in range(BATCH):
                sp.dma_start(view[b], k.X[:, b * TILES:(b + 1) * TILES, :]).then_inc(stored, 16)
            sp.wait_ge(stored, 16 * BATCH)



class NormBuffers:
    def __init__(self, sb, name):
        self.stats = sb(f"{name}_stats", [P, TILES, 6], F32)
        self.moments = sb(f"{name}_moments", [P, TILES, 2], F32)
        self.std = sb(f"{name}_std", [P, TILES], F32)
        self.rstd = sb(f"{name}_rstd", [P, TILES], F32)
        self.eps = sb(f"{name}_eps", [P, 1], F32)


def norm_on_vector(dve, n, source, out, chain, std_ready, moments_ready, normed):
    chain.link(dve, dve.memset(n.eps[:], LN_EPS))
    for j in range(TILES):
        last = dve.bn_stats(n.stats[:, j, :], source(j))
    chain.link(dve, last)
    for j in range(TILES):
        last = dve.bn_aggr(n.moments[:, j, :], n.stats[:, j, :])
    last.then_inc(moments_ready.sem, 1)
    dve.wait_ge(std_ready.sem, 1)
    chain.link(dve, dve.reciprocal(n.rstd[:], n.std[:]))
    for j in range(TILES):
        dve.tensor_scalar(out[:, j, :], source(j), n.moments[:, j, 0:1], n.rstd[:, j:j + 1],
                          ALU.subtract, ALU.mult).then_inc(normed.sem, 1)


def roots_on_scalar(act, n, moments_ready, std_ready):
    act.wait_ge(moments_ready.sem, 1)
    act.activation(n.std[:], n.moments[:, :, 1], ACT.Sqrt, bias=n.eps[:, 0:1]).then_inc(std_ready.sem, 1)


def transpose_on_tensor(pe, k, tiles, banks, tiles_ready, ready_at, turned):
    for half in range(HALVES):
        pe.wait_ge(tiles_ready.sem, ready_at + 4 * (half + 1))
        for c in range(DK):
            for i in range(4):
                last = pe.transpose(banks[:, half * DK + c, i * P:(i + 1) * P],
                                    tiles[:, half * 4 + i, c * P:(c + 1) * P], k.ident[:])
            last.then_inc(turned.sem, 1)


def columns_of(turned_tile, q, pad=0):
    half, c = divmod(q, DK)
    return turned_tile[:, c, pad + half * BANK:pad + (half + 1) * BANK]



D_INNER, D_STATE, D_CONV, DT_RANK = 512, 16, 4, 64
DI = D_INNER // P


def mamba_stage(k):
    nc, d = k.nc, k.dram
    with ExitStack() as ctx:
        def sb(name, shape, dt=F32):
            return ctx.enter_context(nc.sbuf_tensor(name, shape, dt))

        w_in = sb("w_in", [P, DK, 2 * D_INNER])
        w_x = sb("w_x", [P, DI, DT_RANK + 2 * D_STATE])
        w_dt = sb("w_dt", [DT_RANK, D_INNER])
        w_out = sb("w_out", [P, DI, DM])
        conv_w = sb("conv_w", [P, DI, D_CONV])
        conv_b = sb("conv_b", [P, DI])
        b_dt = sb("b_dt", [P, DI])
        skip = sb("skip", [P, DI])
        a_neg = sb("a_neg", [P, D_STATE, DI])
        conv_diag = sb("conv_diag", [P, DI * D_CONV, P])
        skip_diag = sb("skip_diag", [P, DI, P])
        n = NormBuffers(sb, "mamba")
        xs = sb("xs", [P, DI, SEQ])
        gate = sb("gate", [P, DI, SEQ])
        delta = sb("delta", [P, DI, SEQ])
        du = sb("du", [P, DI, SEQ])
        decay = sb("decay", [P, DI, SEQ])
        drive = sb("drive", [P, DI, SEQ])
        h = sb("h", [P, DI, SEQ])
        b_row = sb("b_row", [P, 2, SEQ])
        c_row = sb("c_row", [P, 2, SEQ])
        z = h[:, 0:2, :].rearrange("p a (b d) -> p (a b) d", d=DM)
        zT = h[:, 2:4, :]
        xc = decay
        dt_low = drive[0:DT_RANK, 0, :]
        bc = drive[0:2 * D_STATE, 1, :]
        soft = h
        bank = ctx.enter_context(nc.psum_tensor("mamba_psum", [P, 8, BANK], F32))
        bc_dram = nc.dram_tensor("bc_scratch", [2 * D_STATE, SEQ], F32, kind="Internal").ap()

        with Prologue(nc) as pre:
            loaded = pre.semaphore("mamba_loaded")
            a_ready = pre.semaphore("mamba_a_ready")
            diag_ready = pre.semaphore("mamba_diag_ready")
            block = pre.block()

            @block.sync
            def _(sp):
                loads = [
                    (w_in[:], d["L0_attn_W_in"].rearrange("(c p) n -> p c n", p=P)),
                    (w_x[:], d["L0_attn_W_x"].rearrange("(c p) n -> p c n", p=P)),
                    (w_dt[:], d["L0_attn_W_dt"]),
                    (w_out[:], d["L0_attn_W_out"].rearrange("(c p) n -> p c n", p=P)),
                    (conv_w[:], d["L0_attn_conv_w"].rearrange("(c p) o n -> p c (o n)", p=P)),
                    (conv_b[:], d["L0_attn_conv_b"].rearrange("(c p) -> p c", p=P)),
                    (b_dt[:], d["L0_attn_b_dt"].rearrange("(c p) -> p c", p=P)),
                    (skip[:], d["L0_attn_D"].rearrange("(c p) -> p c", p=P)),
                    (a_neg[:], d["L0_attn_A_raw"].rearrange("n (c p) -> p n c", p=P)),
                ]
                for dst, src in loads:
                    sp.dma_start(dst, src, allow_slow_non_contiguous=True).then_inc(loaded, 16)
                sp.wait_ge(loaded, 16 * len(loads))

            @block.scalar
            def _(act):
                act.wait_ge(loaded, 16 * 9)
                act.activation(a_neg[:], a_neg[:], ACT.Exp).then_inc(a_ready, 1)

            @block.vector
            def _(dve):
                dve.wait_ge(a_ready, 1)
                dve.tensor_scalar(a_neg[:], a_neg[:], -1.0, None, ALU.mult)
                for c in range(DI):
                    for t in range(D_CONV):
                        dve.tensor_scalar(conv_diag[:, c * D_CONV + t, :], k.ident[:], conv_w[:, c, t:t + 1],
                                          None, ALU.mult)
                    last = dve.tensor_scalar(skip_diag[:, c, :], k.ident[:], skip[:, c:c + 1], None, ALU.mult)
                last.then_inc(diag_ready, 1)
                dve.wait_ge(diag_ready, 1)

        with ExitStack() as run, nc.Fori(0, BATCH) as b:
            signal = BatchSignals(run, nc, "mamba_")
            chain = Chain(signal("chain"))
            moments_ready = signal("moments_ready")
            std_ready = signal("std_ready")
            normed = signal("normed")
            turned = signal("turned")
            zT_ready = signal("zT_ready")
            projected = signal("projected")
            taken = signal("taken")
            convolved = signal("convolved")
            xs_ready = signal("xs_ready")
            low_ranked = signal("low_ranked")
            low_ready = signal("low_ready")
            bc_stored = signal("bc_stored")
            raised = signal("raised")
            delta_biased = signal("delta_biased")
            clamped = signal("clamped")
            exp_taken = signal("exp_taken")
            log_taken = signal("log_taken")
            delta_ready = signal("delta_ready")
            du_ready = signal("du_ready")
            b_loaded = [signal(f"b_loaded{r}") for r in range(2)]
            c_loaded = [signal(f"c_loaded{r}") for r in range(2)]
            steps = D_STATE * DI
            decay_ready = signal("decay_ready")
            drive_ready = signal("drive_ready")
            scanned = signal("scanned")
            weighted = signal("weighted")
            summed = signal("summed")
            gated = signal("gated")
            out_summed = signal("out_summed")
            added = signal("added")
            block_ctx = ExitStack()
            block = block_ctx.enter_context(nc.Block())

            @block.vector
            def _(dve):
                dve.sem_inc(scanned.sem, DI)
                dve.sem_inc(weighted.sem, DI + 1)
                norm_on_vector(dve, n, lambda j: k.X[:, b * TILES + j, :], z, chain, std_ready,
                               moments_ready, normed)
                for half in range(HALVES):
                    dve.wait_ge(low_ranked.sem, 2 * half + 2)
                    cols = slice(half * BANK, (half + 1) * BANK)
                    dve.tensor_copy(dt_low[:, cols], bank[0:DT_RANK, 4 + 2 * half, :]).then_inc(low_ready.sem, 1)
                    dve.tensor_copy(bc[:, cols], bank[0:2 * D_STATE, 5 + 2 * half, :]).then_inc(low_ready.sem, 1)
                for r in range(8):
                    c, half = divmod(r, HALVES)
                    dve.wait_ge(raised.sem, r + 1)
                    dve.tensor_scalar(delta[:, c, half * BANK:(half + 1) * BANK], bank[:, r % 4, :],
                                      b_dt[:, c:c + 1], None, ALU.add).then_inc(delta_biased.sem, 1)
                for c in range(DI):
                    dve.wait_ge(log_taken.sem, c + 1)
                    dve.tensor_tensor(delta[:, c, :], delta[:, c, :], soft[:, c, :],
                                      ALU.max).then_inc(delta_ready.sem, 1)
                    dve.wait_ge(delta_ready.sem, c + 1)
                    dve.tensor_tensor(du[:, c, :], delta[:, c, :], xs[:, c, :], ALU.mult).then_inc(du_ready.sem, 1)

                def scan(s, c):
                    dve.wait_ge(decay_ready.sem, s * DI + c + 1)
                    dve.wait_ge(drive_ready.sem, s * DI + c + 1)
                    dve.tensor_tensor_scan(h[:, c, :], decay[:, c, :], drive[:, c, :], 0.0,
                                           ALU.mult, ALU.add).then_inc(scanned.sem, 1)

                def weigh(s, c, r):
                    dve.wait_ge(scanned.sem, DI + s * DI + c + 1)
                    dve.tensor_tensor(h[:, c, :], h[:, c, :], c_row[:, r, :], ALU.mult).then_inc(weighted.sem, 1)

                with dve.Fori(0, D_STATE // 2) as pair:
                    for r in range(2):
                        s = pair * 2 + r
                        dve.wait_ge(c_loaded[r].sem, pair * 16 + 16)
                        for c in range(DI + 1):
                            if c < DI:
                                dve.wait_ge(summed.sem, s * DI + c + 1)
                                scan(s, c)
                            if c >= 1:
                                weigh(s, c - 1, r)
                for c in range(DI):
                    dve.wait_ge(summed.sem, steps + c + 1)
                    dve.tensor_tensor(xs[:, c, :], bank[:, 2 * c:2 * c + 2, :].rearrange("p a b -> p (a b)"),
                                      gate[:, c, :], ALU.mult).then_inc(gated.sem, 1)
                for j in range(TILES):
                    dve.wait_ge(out_summed.sem, j + 1)
                    dve.tensor_tensor(k.X[:, b * TILES + j, :], k.X[:, b * TILES + j, :], bank[:, j, 0:DM],
                                      ALU.add).then_inc(added.sem, 1)
                dve.wait_ge(added.sem, TILES)

            @block.scalar
            def _(act):
                roots_on_scalar(act, n, moments_ready, std_ready)
                for q in range(4):
                    act.wait_ge(turned.sem, q + 1)
                    act.copy(columns_of(zT, q), bank[:, q, :]).then_inc(zT_ready.sem, 1)
                for q in range(8):
                    c, half = divmod(q, HALVES)
                    act.wait_ge(projected.sem, q + 1)
                    act.copy(xc[:, c, half * BANK:(half + 1) * BANK], bank[:, 4 + q % 4, :]).then_inc(taken.sem, 1)
                for q in range(8):
                    c, half = divmod(q, HALVES)
                    act.wait_ge(convolved.sem, q + 1)
                    act.activation(xs[:, c, half * BANK:(half + 1) * BANK], bank[:, q % 4, :], ACT.Silu,
                                   bias=conv_b[:, c:c + 1]).then_inc(xs_ready.sem, 1)
                for q in range(8):
                    c, half = divmod(q, HALVES)
                    act.wait_ge(projected.sem, 8 + q + 1)
                    act.activation(gate[:, c, half * BANK:(half + 1) * BANK], bank[:, 4 + q % 4, :],
                                   ACT.Silu).then_inc(taken.sem, 1)
                for c in range(DI):
                    act.wait_ge(clamped.sem, c + 1)
                    act.activation(soft[:, c, :], soft[:, c, :], ACT.Exp).then_inc(exp_taken.sem, 1)
                for c in range(DI):
                    act.wait_ge(exp_taken.sem, c + 1)
                    act.activation(soft[:, c, :], soft[:, c, :], ACT.Ln, bias=1.0).then_inc(log_taken.sem, 1)
                for c in range(DI):
                    act.wait_ge(delta_ready.sem, c + 1)
                with act.Fori(0, D_STATE) as s:
                    for c in range(DI):
                        act.wait_ge(scanned.sem, s * DI + c + 1)
                        act.activation(decay[:, c, :], delta[:, c, :], ACT.Exp,
                                       scale=a_neg[:, s, c:c + 1]).then_inc(decay_ready.sem, 1)

            @block.gpsimd
            def _(pool):
                for c in range(DI):
                    pool.wait_ge(delta_biased.sem, 2 * c + 2)
                    pool.wait_ge(taken.sem, 16)
                    pool.tensor_scalar(soft[:, c, :], delta[:, c, :], 80.0, None, ALU.min).then_inc(clamped.sem, 1)
                for c in range(DI):
                    pool.wait_ge(du_ready.sem, c + 1)
                with pool.Fori(0, D_STATE // 2) as pair:
                    for r in range(2):
                        s = pair * 2 + r
                        pool.wait_ge(b_loaded[r].sem, pair * 16 + 16)
                        for c in range(DI):
                            pool.wait_ge(scanned.sem, s * DI + c + 1)
                            pool.tensor_tensor(drive[:, c, :], du[:, c, :], b_row[:, r, :],
                                               ALU.mult).then_inc(drive_ready.sem, 1)

            @block.tensor
            def _(pe):
                transpose_on_tensor(pe, k, z, bank, normed, 0, turned)

                def project(q):
                    m, half = divmod(q, HALVES)
                    if q >= 4:
                        pe.wait_ge(taken.sem, q - 3)
                    for c in range(DK):
                        last = pe.matmul(bank[:, 4 + q % 4, :], w_in[:, c, m * P:(m + 1) * P],
                                         zT[:, c, half * BANK:(half + 1) * BANK], start=(c == 0), stop=(c == DK - 1))
                    last.then_inc(projected.sem, 1)

                for q in range(8):
                    pe.wait_ge(zT_ready.sem, 2 * (q % 2) + 2)
                    project(q)
                for q in range(8):
                    c, half = divmod(q, HALVES)
                    pe.wait_ge(taken.sem, q + 1)
                    if q >= 4:
                        pe.wait_ge(xs_ready.sem, q - 3)
                    for t in (3, 2, 1, 0):
                        back = D_CONV - 1 - t
                        first = half * BANK - back
                        w = conv_diag[:, c * D_CONV + t, :]
                        lo = max(first, 0)
                        last = pe.matmul(bank[:, q % 4, lo - first:BANK], w, xc[:, c, lo:first + BANK],
                                         start=(t == 3), stop=(t == 0), skip_group_check=True)
                    last.then_inc(convolved.sem, 1)
                for q in range(8, 16):
                    project(q)
                for half in range(HALVES):
                    pe.wait_ge(xs_ready.sem, 8)
                    pe.wait_ge(taken.sem, 16)
                    for lo, hi, slot in ((0, DT_RANK, 4), (DT_RANK, DT_RANK + 2 * D_STATE, 5)):
                        for c in range(DI):
                            last = pe.matmul(bank[0:hi - lo, slot + 2 * half, :], w_x[:, c, lo:hi],
                                             xs[:, c, half * BANK:(half + 1) * BANK], start=(c == 0), stop=(c == DI - 1))
                        last.then_inc(low_ranked.sem, 1)
                for r in range(8):
                    c, half = divmod(r, HALVES)
                    pe.wait_ge(low_ready.sem, 2 * half + 1)
                    if r >= 4:
                        pe.wait_ge(delta_biased.sem, r - 3)
                    pe.matmul(bank[:, r % 4, :], w_dt[:, c * P:(c + 1) * P], dt_low[:, half * BANK:(half + 1) * BANK],
                              start=True, stop=True).then_inc(raised.sem, 1)
                pe.wait_ge(delta_biased.sem, 8)
                pe.wait_ge(low_ready.sem, 4)
                for c in range(DI):
                    for half in range(HALVES):
                        last = pe.matmul(bank[:, 2 * c + half, :], skip_diag[:, c, :],
                                         xs[:, c, half * BANK:(half + 1) * BANK], start=True, stop=False,
                                         skip_group_check=True)
                    last.then_inc(summed.sem, 1)
                with pe.Fori(0, D_STATE) as s:
                    for c in range(DI):
                        pe.wait_ge(weighted.sem, DI + s * DI + c + 2)
                        for half in range(HALVES):
                            last = pe.matmul(bank[:, 2 * c + half, :], k.ident[:],
                                             h[:, c, half * BANK:(half + 1) * BANK], start=False, stop=False,
                                             skip_group_check=True)
                        last.then_inc(summed.sem, 1)
                pe.wait_ge(gated.sem, DI)
                for j in range(TILES):
                    for c in range(DI):
                        last = pe.matmul(bank[:, j, 0:DM], xs[:, c, j * P:(j + 1) * P], w_out[:, c, :],
                                         start=(c == 0), stop=(c == DI - 1))
                    last.then_inc(out_summed.sem, 1)

            @block.sync
            def _(sp):
                sp.wait_ge(low_ready.sem, 4)
                sp.dma_start(bc_dram, bc).then_inc(bc_stored.sem, 16)
                sp.wait_ge(bc_stored.sem, 16)
                with sp.Fori(0, D_STATE // 2) as pair:
                    for r in range(2):
                        row = pair * 2 + r
                        sp.wait_ge(weighted.sem, row * DI + 1)
                        sp.dma_start(b_row[:, r, :], bc_dram[bass.ds(row, 1), :].broadcast_to([P, SEQ])).then_inc(b_loaded[r].sem, 16)
                        sp.dma_start(c_row[:, r, :], bc_dram[bass.ds(row + D_STATE, 1), :].broadcast_to([P, SEQ])).then_inc(c_loaded[r].sem, 16)
            block_ctx.close()
            signal.clear()



CTX = 77
HOPS = 2
MASKED = -3.4028234663852886e38


def memory_stage(k):
    nc, d = k.nc, k.dram
    with ExitStack() as ctx:
        def sb(name, shape, dt=F32):
            return ctx.enter_context(nc.sbuf_tensor(name, shape, dt))

        context = sb("context", [CTX, BATCH, DM])
        contextT = sb("contextT", [P, DK, BATCH, CTX])
        w_hop = sb("w_hop", [P, HOPS, DK, DM])
        w_context = sb("w_context", [P, HOPS, DK, BATCH, CTX])
        mask_in = sb("mask_in", [P, BATCH, CTX], I32)
        keep = sb("keep", [P, BATCH, CTX])
        fill = sb("fill", [P, BATCH, CTX])
        n = NormBuffers(sb, "memory")
        u = sb("u", [P, TILES, DM])
        uT = sb("uT", [P, DK, SEQ])
        logits = sb("logits", [P, TILES, CTX])
        most = sb("most", [P, TILES])
        total = sb("total", [P, TILES])
        scale = sb("scale", [P, TILES])
        weightT = sb("weightT", [CTX, TILES, P])
        bank = ctx.enter_context(nc.psum_tensor("memory_psum", [P, 8, BANK], F32))

        with Prologue(nc) as pre:
            loaded = pre.semaphore("memory_loaded")
            turned = pre.semaphore("memory_turned")
            contextT_ready = pre.semaphore("memory_contextT_ready")
            folded = pre.semaphore("memory_folded")
            kept = pre.semaphore("memory_kept")
            block = pre.block()

            @block.sync
            def _(sp):
                sp.dma_start(context[:], d["ctx_1024"].rearrange("b l d -> l b d")).then_inc(loaded, 16)
                for i, name in enumerate(("L0_xattn_W0", "L0_xattn_W1")):
                    sp.dma_start(w_hop[:, i], d[name].rearrange("(c p) n -> p c n", p=P)).then_inc(loaded, 16)
                mask = d["mask_BxS2_if1"].rearrange("(o b) l -> o (b l)", o=1)
                sp.dma_start(mask_in[:].rearrange("p b l -> p (b l)"),
                             mask.broadcast_to([P, BATCH * CTX])).then_inc(loaded, 16)
                sp.wait_ge(loaded, 64)

            @block.tensor
            def _(pe):
                pe.wait_ge(loaded, 64)
                for b in range(BATCH):
                    for c in range(DK):
                        last = pe.transpose(bank[:, c, b * P:b * P + CTX], context[:, b, c * P:(c + 1) * P],
                                            k.ident[0:CTX, 0:CTX])
                last.then_inc(turned, 1)
                pe.wait_ge(contextT_ready, 1)
                for i in range(HOPS):
                    for m in range(DK):
                        for c in range(DK):
                            last = pe.matmul(bank[:, 2 + i * DK + m, 0:BATCH * CTX],
                                             w_hop[:, i, c, m * P:(m + 1) * P],
                                             contextT[:, c].rearrange("p b l -> p (b l)"),
                                             start=(c == 0), stop=(c == DK - 1))
                last.then_inc(folded, 1)

            @block.vector
            def _(dve):
                dve.wait_ge(loaded, 64)
                dve.tensor_scalar(keep[:], mask_in[:], 0, None, ALU.not_equal).then_inc(kept, 1)
                dve.wait_ge(kept, 1)
                dve.tensor_scalar(fill[:], keep[:], 1.0, -MASKED, ALU.subtract, ALU.mult)
                dve.wait_ge(turned, 1)
                for c in range(DK):
                    last = dve.tensor_copy(contextT[:, c],
                                           bank[:, c, :].rearrange("p (b l) -> p b l", l=P)[:, :, 0:CTX])
                last.then_inc(contextT_ready, 1)
                dve.wait_ge(folded, 1)
                for i in range(HOPS):
                    for m in range(DK):
                        last = dve.tensor_copy(w_context[:, i, m].rearrange("p b l -> p (b l)"),
                                               bank[:, 2 + i * DK + m, 0:BATCH * CTX])
                last.then_inc(kept, 1)
                dve.wait_ge(kept, 2)

        with ExitStack() as run, nc.Fori(0, BATCH) as b:
            signal = BatchSignals(run, nc, "memory_")
            chain = Chain(signal("chain"))
            moments_ready = signal("moments_ready")
            std_ready = signal("std_ready")
            u_ready = signal("u_ready")
            turned = signal("turned")
            uT_ready = signal("uT_ready")
            scored = signal("scored")
            shifted = signal("shifted")
            exp_taken = signal("exp_taken")
            weight_turned = signal("weight_turned")
            weightT_ready = signal("weightT_ready")
            read = signal("read")
            added = signal("added")
            block_ctx = ExitStack()
            block = block_ctx.enter_context(nc.Block())

            @block.vector
            def _(dve):
                norm_on_vector(dve, n, lambda j: k.X[:, b * TILES + j, :], u, chain, std_ready,
                               moments_ready, u_ready)
                for i in range(HOPS):
                    for half in range(HALVES):
                        js = slice(half * 4, half * 4 + 4)
                        psum = bank[:, 4 + half, :].rearrange("p (j l) -> p j l", l=P)[:, :, 0:CTX]
                        dve.wait_ge(scored.sem, i * HALVES + half + 1)
                        chain.link(dve, dve.tensor_tensor(logits[:, js], psum,
                                                          keep[:, bass.ds(b, 1), :].broadcast_to([P, 4, CTX]), ALU.mult))
                        chain.link(dve, dve.tensor_tensor(logits[:, js], logits[:, js],
                                                          fill[:, bass.ds(b, 1), :].broadcast_to([P, 4, CTX]), ALU.add))
                        chain.link(dve, dve.tensor_reduce(most[:, js], logits[:, js], AXIS.X, ALU.max))
                        dve.tensor_tensor(logits[:, js], logits[:, js],
                                          most[:, js].unsqueeze(2).broadcast_to([P, 4, CTX]),
                                          ALU.subtract).then_inc(shifted.sem, 1)
                    for half in range(HALVES):
                        js = slice(half * 4, half * 4 + 4)
                        dve.wait_ge(exp_taken.sem, i * HALVES + half + 1)
                        chain.link(dve, dve.tensor_reduce(total[:, js], logits[:, js], AXIS.X, ALU.add))
                        chain.link(dve, dve.reciprocal(scale[:, js], total[:, js]))
                    for j in range(TILES):
                        dve.wait_ge(read.sem, i * TILES // 2 + j // 2 + 1)
                        dve.scalar_tensor_tensor(out=u[:, j, :], in0=bank[:, j // 2, (j % 2) * DM:(j % 2 + 1) * DM],
                                                 scalar=scale[:, j:j + 1], in1=u[:, j, :], op0=ALU.mult,
                                                 op1=ALU.add).then_inc(u_ready.sem, 1)
                for j in range(TILES):
                    dve.wait_ge(u_ready.sem, HOPS * TILES + j + 1)
                    dve.tensor_tensor(k.X[:, b * TILES + j, :], k.X[:, b * TILES + j, :], u[:, j, :],
                                      ALU.add).then_inc(added.sem, 1)
                dve.wait_ge(added.sem, TILES)

            @block.scalar
            def _(act):
                roots_on_scalar(act, n, moments_ready, std_ready)
                for i in range(HOPS):
                    for q in range(4):
                        act.wait_ge(turned.sem, i * 4 + q + 1)
                        act.copy(columns_of(uT, q), bank[:, q, :]).then_inc(uT_ready.sem, 1)
                    for half in range(HALVES):
                        js = slice(half * 4, half * 4 + 4)
                        act.wait_ge(shifted.sem, i * HALVES + half + 1)
                        act.activation(logits[:, js], logits[:, js], ACT.Exp).then_inc(exp_taken.sem, 1)
                    for half in range(HALVES):
                        act.wait_ge(weight_turned.sem, i * HALVES + half + 1)
                        act.copy(weightT[:, half * 4:half * 4 + 4, :],
                                 bank[0:CTX, 6 + half, :].rearrange("p (j l) -> p j l", l=P)).then_inc(weightT_ready.sem, 1)

            @block.tensor
            def _(pe):
                for i in range(HOPS):
                    transpose_on_tensor(pe, k, u, bank, u_ready, i * TILES, turned)
                    for half in range(HALVES):
                        pe.wait_ge(uT_ready.sem, i * 4 + 2 * half + 2)
                        for j in range(half * 4, half * 4 + 4):
                            for c in range(DK):
                                last = pe.matmul(bank[:, 4 + half, (j % 4) * P:(j % 4) * P + CTX],
                                                 uT[:, c, j * P:(j + 1) * P],
                                                 w_context[:, i, c, bass.ds(b, 1), :].rearrange("p o l -> p (o l)"),
                                                 start=(c == 0), stop=(c == DK - 1))
                        last.then_inc(scored.sem, 1)
                    for half in range(HALVES):
                        pe.wait_ge(exp_taken.sem, i * HALVES + half + 1)
                        for j in range(half * 4, half * 4 + 4):
                            last = pe.transpose(bank[0:CTX, 6 + half, (j % 4) * P:(j % 4 + 1) * P],
                                                logits[:, j, :], k.ident[:])
                        last.then_inc(weight_turned.sem, 1)
                    for half in range(HALVES):
                        pe.wait_ge(weightT_ready.sem, i * HALVES + half + 1)
                        for j in range(half * 4, half * 4 + 4):
                            last = pe.matmul(bank[:, j // 2, (j % 2) * DM:(j % 2 + 1) * DM], weightT[:, j, :],
                                             context[:, bass.ds(b, 1), :].rearrange("p o l -> p (o l)"),
                                             start=True, stop=True)
                            if j % 2:
                                last.then_inc(read.sem, 1)

            block_ctx.close()
            signal.clear()



FF = 1024
HEADS, KEYS, TOP = 4, 64, 8
EXPERTS = 1024
ROWS = EXPERTS // KEYS
KW = 64
SIDES = 2
FC = FF // P
EC = EXPERTS // P


def expert_stage(k):
    nc, d = k.nc, k.dram
    with ExitStack() as ctx:
        def sb(name, shape, dt=F32):
            return ctx.enter_context(nc.sbuf_tensor(name, shape, dt))

        w_sim = sb("w_sim", [P, DK, SIDES * HEADS * KEYS])
        downT = sb("downT", [P, DK, EXPERTS])
        up = sb("up", [P, EC, DM])
        w_g = sb("w_g", [P, DK, FF])
        w_u = sb("w_u", [P, DK, FF])
        w_d = sb("w_d", [P, FC, DM])
        b_g = sb("b_g", [P, FC])
        b_u = sb("b_u", [P, FC])
        b_d = sb("b_d", [1, DM])
        n = NormBuffers(sb, "expert")
        y = sb("y", [P, TILES, DM])
        yT = sb("yT", [P, DK, SEQ])
        sims = sb("sims", [P, TILES, SIDES * HEADS * KEYS])
        hitT = sb("hitT", [P, EC, SEQ])
        innerT = sb("innerT", [P, FC, SEQ])
        gate = sb("ffn_gate", [P, BANK])
        best = sb("best", [P, SIDES, HEADS, TOP])
        pairs = sb("pairs", [P, HEADS, TOP, TOP])
        score = sb("score", [P, HEADS, TOP])
        escore = sb("escore", [P, HEADS, TOP])
        neg_most = sb("neg_most", [P, 2, HEADS])
        total = sb("expert_total", [P, HEADS])
        inv_total = sb("inv_total", [P, HEADS])
        given = sb("given", [P, 2])
        table = sb("table", [P, 2, ROWS, KEYS])
        picked = sb("picked", [P, 2, ROWS, KEYS])
        weight = sb("weight", [P, 2, EXPERTS])
        mixedT = y[:].rearrange("p (r e) t -> p r (e t)", r=2)
        bank = ctx.enter_context(nc.psum_tensor("expert_psum", [P, 8, BANK], F32))

        with Prologue(nc) as pre:
            loaded = pre.semaphore("expert_loaded")
            folded = pre.semaphore("expert_folded")
            kept = pre.semaphore("expert_kept")
            w_q = hitT[0:KW, 0:2, :].rearrange("p a (s d) -> p (a s) d", d=DM)
            keys = hitT[0:KW, 2, 0:SIDES * HEADS * KEYS].rearrange("p (s h e) -> p s h e", s=SIDES, h=HEADS)
            block = pre.block()
            loads = [
                (w_q[:], d["L0_ffn_Wq"].rearrange("(s n) d -> n s d", n=KW)),
                (keys[:], d["L0_ffn_keys"]),
                (downT[:], d["L0_ffn_down_embed"].rearrange("(c p) n -> p c n", p=P)),
                (up[:], d["L0_ffn_up_embed"].rearrange("(c p) n -> p c n", p=P)),
                (w_g[:], d["L0_ffn_Wg"].rearrange("(c p) n -> p c n", p=P)),
                (w_u[:], d["L0_ffn_Wu"].rearrange("(c p) n -> p c n", p=P)),
                (w_d[:], d["L0_ffn_Wd"].rearrange("(c p) n -> p c n", p=P)),
                (b_g[:], d["L0_ffn_bg"].rearrange("(c p) -> p c", p=P)),
                (b_u[:], d["L0_ffn_bu"].rearrange("(c p) -> p c", p=P)),
                (b_d[:], d["L0_ffn_bd"].rearrange("(o n) -> o n", o=1)),
            ]

            @block.sync
            def _(sp):
                for dst, src in loads:
                    sp.dma_start(dst, src, allow_slow_non_contiguous=True).then_inc(loaded, 16)
                sp.wait_ge(loaded, 16 * len(loads))

            @block.tensor
            def _(pe):
                pe.wait_ge(loaded, 16 * len(loads))
                for m in range(DK):
                    for s in range(SIDES * HEADS):
                        last = pe.matmul(bank[:, m, s * KEYS:(s + 1) * KEYS], w_q[:, s, m * P:(m + 1) * P],
                                         keys[:, s // HEADS, s % HEADS, :], start=True, stop=True)
                last.then_inc(folded, 1)

            @block.vector
            def _(dve):
                dve.wait_ge(folded, 1)
                for m in range(DK):
                    dve.tensor_copy(w_sim[:, m, :], bank[:, m, :]).then_inc(kept, 1)
                dve.wait_ge(kept, DK)

        with ExitStack() as run, nc.Fori(0, BATCH) as b:
            signal = BatchSignals(run, nc, "expert_")
            chain = Chain(signal("chain"))
            moments_ready = signal("moments_ready")
            std_ready = signal("std_ready")
            normed = signal("normed")
            turned = signal("turned")
            yT_ready = signal("yT_ready")
            compared = signal("compared")
            sims_ready = signal("sims_ready")
            hit = signal("hit")
            hitT_ready = signal("hitT_ready")
            gate_done = signal("gate_done")
            up_done = signal("up_done")
            gate_ready = signal("gate_ready")
            innerT_ready = signal("innerT_ready")
            most_ready = signal("most_ready")
            score_shifted = signal("score_shifted")
            escore_ready = signal("escore_ready")
            table_ready = signal("table_ready")
            exp_ready = signal("exp_ready")
            picked_ready = signal("picked_ready")
            head_added = signal("head_added")
            weight_ready = signal("weight_ready")
            weight_turned = signal("weight_turned")
            mixed = signal("mixed")
            out_summed = signal("out_summed")
            added = signal("added")
            block_ctx = ExitStack()
            block = block_ctx.enter_context(nc.Block())

            def pieces_before(j):
                return range(0, FC) if j == 0 else range(FC + 2 * (j - 1), FC + 2 * j) if j <= 4 else range(0)

            @block.vector
            def _(dve):
                norm_on_vector(dve, n, lambda j: k.X[:, b * TILES + j, :], y, chain, std_ready,
                               moments_ready, normed)

                def gate_up(q):
                    half, m = divmod(q, FC)
                    dve.wait_ge(up_done.sem, q + 1)
                    dve.wait_ge(gate_ready.sem, q + 1)
                    dve.scalar_tensor_tensor(out=innerT[:, m, half * BANK:(half + 1) * BANK], in0=bank[:, 7, :],
                                             scalar=b_u[:, m:m + 1], in1=gate[:], op0=ALU.add,
                                             op1=ALU.mult).then_inc(innerT_ready.sem, 1)

                def choose(j):
                    dve.wait_ge(sims_ready.sem, j + 1)
                    sim = sims[:, j, :].rearrange("p (s h e) -> p s h e", s=SIDES, h=HEADS)
                    for s in range(SIDES):
                        for h in range(HEADS):
                            last = dve.max(best[:, s, h, :], sim[:, s, h, :])
                    chain.link(dve, last)
                    chain.link(dve, dve.tensor_tensor(
                        pairs[:], best[:, 0].unsqueeze(3).broadcast_to([P, HEADS, TOP, TOP]),
                        best[:, 1].unsqueeze(2).broadcast_to([P, HEADS, TOP, TOP]), ALU.add))
                    if j >= 1:
                        dve.wait_ge(escore_ready.sem, j)
                    for h in range(HEADS):
                        last = dve.max(score[:, h, :], pairs[:, h].rearrange("p a b -> p (a b)"))
                    chain.link(dve, last)
                    if j >= 2:
                        dve.wait_ge(exp_ready.sem, HEADS * (j - 1))
                    dve.tensor_scalar(neg_most[:, j % 2, :], score[:, :, 0], -1.0, None,
                                      ALU.mult).then_inc(most_ready.sem, 1)
                    dve.tensor_tensor(escore[:], score[:], score[:, :, 0:1].broadcast_to([P, HEADS, TOP]),
                                      ALU.subtract).then_inc(score_shifted.sem, 1)

                def weigh(j):
                    dve.wait_ge(escore_ready.sem, j + 1)
                    chain.link(dve, dve.tensor_reduce(total[:], escore[:], AXIS.X, ALU.add))
                    chain.link(dve, dve.reciprocal(inv_total[:], total[:]))
                    if j >= 2:
                        dve.wait_ge(weight_turned.sem, j - 1)
                    w = weight[:, j % 2, :]
                    for h in range(HEADS):
                        t = j * HEADS + h
                        e = picked[:, t % 2].rearrange("p r e -> p (r e)")
                        dve.wait_ge(exp_ready.sem, t + 1)
                        dve.scalar_tensor_tensor(out=e, in0=table[:, t % 2].rearrange("p r e -> p (r e)"),
                                                 scalar=score[:, h, TOP - 1:TOP], in1=e, op0=ALU.is_ge,
                                                 op1=ALU.mult).then_inc(picked_ready.sem, 1)
                        dve.wait_ge(picked_ready.sem, t + 1)
                        if h == 0:
                            last = dve.tensor_scalar(w, e, inv_total[:, 0:1], None, ALU.mult)
                        elif h < HEADS - 1:
                            last = dve.scalar_tensor_tensor(out=w, in0=e, scalar=inv_total[:, h:h + 1], in1=w,
                                                            op0=ALU.mult, op1=ALU.add)
                        else:
                            last = dve.scalar_tensor_tensor(out=w, in0=e, scalar=inv_total[:, h:h + 1], in1=w,
                                                            op0=ALU.mult, op1=ALU.add, accum_out=given[:, 0:1])
                        last.then_inc(head_added.sem, 1)
                        dve.wait_ge(head_added.sem, t + 1)
                    chain.link(dve, dve.tensor_scalar(given[:, 1:2], given[:, 0:1], -1.0, float(HEADS),
                                                      ALU.mult, ALU.add))
                    dve.tensor_tensor(w[:, EXPERTS - 1:], w[:, EXPERTS - 1:], given[:, 1:2],
                                      ALU.add).then_inc(weight_ready.sem, 1)

                def mix(j):
                    dve.wait_ge(weight_turned.sem, j + 1)
                    dve.wait_ge(hitT_ready.sem, FC * (1 + j // 4))
                    if j >= 2:
                        dve.wait_ge(out_summed.sem, j - 1)
                    dve.tensor_tensor(mixedT[:, j % 2].rearrange("p (e t) -> p e t", t=P),
                                      bank[:, 2:4, :].rearrange("p a (e t) -> p (a e) t", t=P),
                                      hitT[:, :, j * P:(j + 1) * P], ALU.mult).then_inc(mixed.sem, 1)

                def add_out(j):
                    dve.wait_ge(out_summed.sem, j + 1)
                    dve.tensor_tensor(k.X[:, b * TILES + j, :], k.X[:, b * TILES + j, :], bank[:, j % 2, 0:DM],
                                      ALU.add).then_inc(added.sem, 1)

                for j in range(TILES + 1):
                    if j < TILES:
                        choose(j)
                        for q in pieces_before(j):
                            gate_up(q)
                        weigh(j)
                        mix(j)
                    if j >= 1:
                        add_out(j - 1)
                dve.wait_ge(added.sem, TILES)

            @block.gpsimd
            def _(pool):
                for j in range(TILES):
                    pool.wait_ge(sims_ready.sem, j + 1)
                    sim = sims[:, j, :].rearrange("p (s h e) -> p s h e", s=SIDES, h=HEADS)
                    for h in range(HEADS):
                        t = j * HEADS + h
                        if t >= 2:
                            pool.wait_ge(picked_ready.sem, t - 1)
                        pool.tensor_tensor(table[:, t % 2], sim[:, 0, h, 0:ROWS].unsqueeze(2).broadcast_to([P, ROWS, KEYS]),
                                           sim[:, 1, h:h + 1, :].broadcast_to([P, ROWS, KEYS]),
                                           ALU.add).then_inc(table_ready.sem, 1)

            @block.scalar
            def _(act):
                roots_on_scalar(act, n, moments_ready, std_ready)
                for q in range(4):
                    act.wait_ge(turned.sem, q + 1)
                    act.copy(columns_of(yT, q), bank[:, q, :]).then_inc(yT_ready.sem, 1)
                for j in range(TILES):
                    act.wait_ge(compared.sem, j + 1)
                    act.copy(sims[:, j, :], bank[:, 4 + j % 4, :]).then_inc(sims_ready.sem, 1)
                for j in range(TILES):
                    for q in pieces_before(j):
                        half, m = divmod(q, FC)
                        cols = slice(half * BANK, (half + 1) * BANK)
                        act.wait_ge(hit.sem, q + 1)
                        act.activation(hitT[:, m, cols], bank[:, 4 + q % 2, :], ACT.Silu).then_inc(hitT_ready.sem, 1)
                        act.wait_ge(gate_done.sem, q + 1)
                        if q >= 1:
                            act.wait_ge(innerT_ready.sem, q)
                        act.activation(gate[:], bank[:, 6, :], ACT.Silu, bias=b_g[:, m:m + 1]).then_inc(gate_ready.sem, 1)
                    act.wait_ge(score_shifted.sem, j + 1)
                    act.activation(escore[:], escore[:], ACT.Exp).then_inc(escore_ready.sem, 1)
                    act.wait_ge(most_ready.sem, j + 1)
                    for h in range(HEADS):
                        t = j * HEADS + h
                        act.wait_ge(table_ready.sem, t + 1)
                        if t >= 2:
                            act.wait_ge(head_added.sem, t - 1)
                        act.activation(picked[:, t % 2], table[:, t % 2], ACT.Exp,
                                       bias=neg_most[:, j % 2, h:h + 1]).then_inc(exp_ready.sem, 1)

            @block.tensor
            def _(pe):
                transpose_on_tensor(pe, k, y, bank, normed, 0, turned)
                for j in range(TILES):
                    pe.wait_ge(yT_ready.sem, 2 if j < 4 else 4)
                    if j >= 4:
                        pe.wait_ge(sims_ready.sem, j - 3)
                    for c in range(DK):
                        last = pe.matmul(bank[:, 4 + j % 4, :], yT[:, c, j * P:(j + 1) * P], w_sim[:, c, :],
                                         start=(c == 0), stop=(c == DK - 1))
                    last.then_inc(compared.sem, 1)
                pe.wait_ge(sims_ready.sem, TILES)

                def piece(q):
                    half, m = divmod(q, FC)
                    cols = slice(half * BANK, (half + 1) * BANK)
                    for w, slot, done, taken, lag in ((downT, 4 + q % 2, hit, hitT_ready, 2),
                                                      (w_g, 6, gate_done, gate_ready, 1),
                                                      (w_u, 7, up_done, innerT_ready, 1)):
                        if q >= lag:
                            pe.wait_ge(taken.sem, q - lag + 1)
                        for c in range(DK):
                            last = pe.matmul(bank[:, slot, :], w[:, c, m * P:(m + 1) * P], yT[:, c, cols],
                                             start=(c == 0), stop=(c == DK - 1))
                        last.then_inc(done.sem, 1)

                for j in range(TILES):
                    for q in pieces_before(j):
                        piece(q)
                    pe.wait_ge(weight_ready.sem, j + 1)
                    if j >= 1:
                        pe.wait_ge(mixed.sem, j)
                    for e in range(EC):
                        last = pe.transpose(bank[:, 2 + e // 4, (e % 4) * P:(e % 4 + 1) * P],
                                            weight[:, j % 2, e * P:(e + 1) * P], k.ident[:])
                    last.then_inc(weight_turned.sem, 1)
                    out = bank[:, j % 2, 0:DM]
                    if j >= 2:
                        pe.wait_ge(added.sem, j - 1)
                    pe.matmul(out, k.ones[0:1, :], b_d[:], start=True, stop=False)
                    pe.wait_ge(innerT_ready.sem, FC * (1 + j // 4))
                    for c in range(FC):
                        pe.matmul(out, innerT[:, c, j * P:(j + 1) * P], w_d[:, c, :], start=False, stop=False)
                    pe.wait_ge(mixed.sem, j + 1)
                    for c in range(EC):
                        last = pe.matmul(out, mixedT[:, j % 2, c * P:(c + 1) * P], up[:, c, :], start=False,
                                         stop=(c == EC - 1))
                    last.then_inc(out_summed.sem, 1)

            block_ctx.close()
            signal.clear()



FILTER = 4
LOW1, LOW2 = SEQ // 2, SEQ // 4
HEAD_W = 16
ATTN_EPS = 1e-6


def wavelet_stage(k):
    nc, d = k.nc, k.dram
    with ExitStack() as ctx:
        def sb(name, shape, dt=F32):
            return ctx.enter_context(nc.sbuf_tensor(name, shape, dt))

        filters = sb("filters", [P, 4, DK, FILTER])
        even = sb("even", [P, 2, DK, 3])
        odd = sb("odd", [P, 2, DK, 2])
        gamma = sb("gamma", [P, DM])
        beta = sb("beta", [P, DM])
        heads = sb("heads", [P, P])
        n = NormBuffers(sb, "wavelet")
        n2 = NormBuffers(sb, "wavelet2")
        y = sb("wavelet_y", [P, TILES, DM])
        yT = sb("wavelet_yT", [P, DK, SEQ + 3])
        low1 = sb("low1", [P, DK, LOW1 + 3])
        high1 = sb("high1", [P, DK, LOW1 + 2])
        low2 = sb("low2", [P, DK, LOW2])
        high2 = sb("high2", [P, DK, LOW2 + 2])
        below = sb("below", [P, DK, LOW2])
        qT = sb("qT", [P, DK, LOW2])
        v_tokens = sb("v_tokens", [P, 2, DM])
        k_tokens = sb("k_tokens", [P, 2, DM])
        kv = sb("kv", [P, DK, P])
        z_column = sb("z_column", [P, DK])
        z_heads = sb("z_heads", [P, DK, P])
        den = sb("den", [P, DK, LOW2])
        attended = sb("attended", [P, DK, LOW2 + 2])
        back2 = sb("back2", [P, DK, LOW1 + 2])
        back1 = sb("back1", [P, DK, SEQ])
        bank = ctx.enter_context(nc.psum_tensor("wavelet_psum", [P, 8, BANK], F32))

        with Prologue(nc) as pre:
            loaded = pre.semaphore("wavelet_loaded")
            masked = pre.semaphore("wavelet_masked")
            combined = pre.semaphore("wavelet_combined")
            block = pre.block()

            @block.sync
            def _(sp):
                for i, name in enumerate(("h_filter", "g_filter", "h_synth", "g_synth")):
                    for c in range(DK):
                        sp.dma_start(filters[:, i, c, :], d["L1_attn_" + name][:, c * P:(c + 1) * P].rearrange("f p -> p f"),
                                     allow_slow_non_contiguous=True).then_inc(loaded, 16)
                for dst, name in ((gamma, "norm_gamma"), (beta, "norm_beta")):
                    row = d["L1_attn_" + name].rearrange("(o n) -> o n", o=1)
                    sp.dma_start(dst[:], row.broadcast_to([P, DM])).then_inc(loaded, 16)
                sp.wait_ge(loaded, 160)

            @block.gpsimd
            def _(pool):
                blocks = heads[:].rearrange("p (a r) -> p a r", r=HEAD_W)
                pool.affine_select(out=blocks, in_=k.ones[:].rearrange("p (a r) -> p a r", r=HEAD_W),
                                   compare_op=ALU.is_ge, fill=0.0, base=0, pattern=[[-HEAD_W, P // HEAD_W], [0, HEAD_W]],
                                   channel_multiplier=1).then_inc(masked, 1)
                pool.wait_ge(masked, 1)
                pool.affine_select(out=blocks, in_=blocks, compare_op=ALU.is_ge, fill=0.0, base=HEAD_W - 1,
                                   pattern=[[HEAD_W, P // HEAD_W], [0, HEAD_W]],
                                   channel_multiplier=-1).then_inc(masked, 1)
                pool.wait_ge(masked, 2)

            @block.vector
            def _(dve):
                dve.wait_ge(loaded, 160)
                f = filters[:, 2:4]
                dve.tensor_copy(even[:, :, :, 0:1], f[:, :, :, 0:1])
                dve.tensor_tensor(even[:, :, :, 1:2], f[:, :, :, 1:2], f[:, :, :, 2:3], ALU.add)
                dve.tensor_copy(even[:, :, :, 2:3], f[:, :, :, 3:4])
                dve.tensor_tensor(odd[:, :, :, 0:1], f[:, :, :, 0:1], f[:, :, :, 1:2], ALU.add)
                dve.tensor_tensor(odd[:, :, :, 1:2], f[:, :, :, 2:3], f[:, :, :, 3:4], ALU.add)
                for t, w in ((yT, SEQ), (low1, LOW1), (high1, LOW1), (high2, LOW2), (attended, LOW2), (back2, LOW1)):
                    for c in range(DK):
                        dve.memset(t[:, c, 0:1], 0.0)
                        last = dve.memset(t[:, c, w + 1:], 0.0)
                last.then_inc(combined, 1)
                dve.wait_ge(combined, 1)

        with ExitStack() as run, nc.Fori(0, BATCH) as b:
            signal = BatchSignals(run, nc, "wavelet_")
            chain = Chain(signal("chain"))
            moments_ready = signal("moments_ready")
            std_ready = signal("std_ready")
            normed = signal("normed")
            turned = signal("turned")
            yT_ready = signal("yT_ready")
            tapped = signal("tapped")
            below_ready = signal("below_ready")
            exp_taken = signal("exp_taken")
            q_ready = signal("q_ready")
            tokens_turned = signal("tokens_turned")
            tokens_ready = signal("tokens_ready")
            kv_done = signal("kv_done")
            kv_ready = signal("kv_ready")
            num_den = signal("num_den")
            back_turned = signal("back_turned")
            moments2_ready = signal("moments2_ready")
            std2_ready = signal("std2_ready")
            normed2 = signal("normed2")
            scaled = signal("scaled")
            shifted = signal("shifted")
            added = signal("added")
            block_ctx = ExitStack()
            block = block_ctx.enter_context(nc.Block())

            @block.vector
            def _(dve):
                norm_on_vector(dve, n, lambda j: k.X[:, b * TILES + j, :], y, chain, std_ready,
                               moments_ready, normed)
                count = [0]

                def filter_all(outputs):
                    last_of = {}
                    for i in range(max(len(taps) for _, _, taps in outputs)):
                        for o, (out, start, taps) in enumerate(outputs):
                            if i >= len(taps):
                                continue
                            tap, source = taps[i]
                            if i:
                                dve.wait_ge(tapped.sem, last_of[o])
                            acc = out if i else start
                            if acc is None:
                                ins = dve.tensor_scalar(out, source, tap, None, ALU.mult)
                            else:
                                ins = dve.scalar_tensor_tensor(out=out, in0=source, scalar=tap, in1=acc,
                                                               op0=ALU.mult, op1=ALU.add)
                            ins.then_inc(tapped.sem, 1)
                            count[0] += 1
                            last_of[o] = count[0]
                    dve.wait_ge(tapped.sem, count[0])

                def analysis(source, low, high, length):
                    filter_all([(out, None, [(filters[:, i, c, t:t + 1], source[:, c, t:t + 2 * length - 1:2])
                                             for t in range(FILTER)])
                                for c in range(DK) for i, out in ((0, low[c]), (1, high[c]))])

                def synthesis(sources, out, start, length):
                    outputs = []
                    for c in range(DK):
                        for parity, taps in ((0, even), (1, odd)):
                            n_taps = 3 - parity
                            outputs.append((out[c][:, parity:2 * length:2],
                                            start[c][:, parity:2 * length:2] if start else None,
                                            [(taps[:, i, c, t:t + 1], sources[i][:, c, t + parity:t + parity + length])
                                             for i in range(2) for t in range(n_taps)]))
                    filter_all(outputs)

                dve.wait_ge(yT_ready.sem, 4)
                analysis(yT, [low1[:, c, 1:1 + LOW1] for c in range(DK)], [high1[:, c, 1:1 + LOW1] for c in range(DK)], LOW1)
                analysis(low1, [low2[:, c, :] for c in range(DK)], [high2[:, c, 1:1 + LOW2] for c in range(DK)], LOW2)
                dve.tensor_scalar(below[:], low2[:], 0.0, None, ALU.min).then_inc(below_ready.sem, 1)
                dve.wait_ge(exp_taken.sem, 1)
                for c in range(DK):
                    dve.scalar_tensor_tensor(out=qT[:, c, :], in0=low2[:, c, :], scalar=0.0, in1=below[:, c, :],
                                             op0=ALU.max, op1=ALU.add).then_inc(q_ready.sem, 1)
                dve.wait_ge(tokens_turned.sem, 2)
                dve.tensor_copy(v_tokens[:].rearrange("p i n -> p (i n)"), bank[:, 4, :]).then_inc(tokens_ready.sem, 1)
                dve.tensor_copy(k_tokens[:].rearrange("p i n -> p (i n)"), bank[:, 5, :]).then_inc(tokens_ready.sem, 1)
                dve.wait_ge(kv_done.sem, 2)
                chain.link(dve, dve.tensor_copy(z_column[:], bank[:, 7, 0:DK]))
                for c in range(DK):
                    dve.tensor_tensor(kv[:, c, :], bank[:, 6, c * P:(c + 1) * P], heads[:], ALU.mult)
                    dve.tensor_scalar(z_heads[:, c, :], heads[:], z_column[:, c:c + 1], None,
                                      ALU.mult).then_inc(kv_ready.sem, 1)
                dve.wait_ge(num_den.sem, 2)
                chain.link(dve, dve.tensor_scalar(den[:].rearrange("p c t -> p (c t)"), bank[:, 5, :], ATTN_EPS, None,
                                                  ALU.add))
                chain.link(dve, dve.reciprocal(den[:], den[:]))
                chain.link(dve, dve.tensor_tensor(attended[:, :, 1:1 + LOW2],
                                                  bank[:, 4, :].rearrange("p (c t) -> p c t", c=DK), den[:], ALU.mult))
                synthesis([attended, high2], [back2[:, c, 1:1 + LOW1] for c in range(DK)], None, LOW2)
                synthesis([back2, high1], [back1[:, c, :] for c in range(DK)],
                          [yT[:, c, 1:1 + SEQ] for c in range(DK)], LOW1)
                dve.wait_ge(back_turned.sem, 4)
                norm_on_vector(dve, n2, lambda j: bank[:, j // 2, (j % 2) * DM:(j % 2 + 1) * DM], y, chain, std2_ready,
                               moments2_ready, normed2)
                for half in range(HALVES):
                    js = bass.ds(b * TILES + half * 4, 4)
                    dve.wait_ge(shifted.sem, half + 1)
                    dve.tensor_tensor(k.X[:, js, :], k.X[:, js, :], y[:, half * 4:half * 4 + 4, :],
                                      ALU.add).then_inc(added.sem, 1)
                dve.wait_ge(added.sem, HALVES)

            @block.gpsimd
            def _(pool):
                for half in range(HALVES):
                    ys = y[:, half * 4:half * 4 + 4, :]
                    pool.wait_ge(normed2.sem, 4 * half + 4)
                    pool.tensor_tensor(ys, ys, gamma[:].unsqueeze(1).broadcast_to([P, 4, DM]),
                                       ALU.mult).then_inc(scaled.sem, 1)
                    pool.wait_ge(scaled.sem, half + 1)
                    pool.tensor_tensor(ys, ys, beta[:].unsqueeze(1).broadcast_to([P, 4, DM]),
                                       ALU.add).then_inc(shifted.sem, 1)

            @block.scalar
            def _(act):
                roots_on_scalar(act, n, moments_ready, std_ready)
                for q in range(4):
                    act.wait_ge(turned.sem, q + 1)
                    act.copy(columns_of(yT, q, pad=1), bank[:, q, :]).then_inc(yT_ready.sem, 1)
                act.wait_ge(below_ready.sem, 1)
                act.activation(below[:], below[:], ACT.Exp).then_inc(exp_taken.sem, 1)
                roots_on_scalar(act, n2, moments2_ready, std2_ready)

            @block.tensor
            def _(pe):
                transpose_on_tensor(pe, k, y, bank, normed, 0, turned)
                for source, slot, wait in ((low2, 4, None), (qT, 5, q_ready)):
                    pe.wait_ge(q_ready.sem, DK)
                    for i in range(2):
                        for c in range(DK):
                            last = pe.transpose(bank[:, slot, (i * DK + c) * P:(i * DK + c + 1) * P],
                                                source[:, c, i * P:(i + 1) * P], k.ident[:])
                    last.then_inc(tokens_turned.sem, 1)
                pe.wait_ge(tokens_ready.sem, 2)
                for c in range(DK):
                    for i in range(2):
                        last = pe.matmul(bank[:, 6, c * P:(c + 1) * P], k_tokens[:, i, c * P:(c + 1) * P],
                                         v_tokens[:, i, c * P:(c + 1) * P], start=(i == 0), stop=(i == 1))
                last.then_inc(kv_done.sem, 1)
                for c in range(DK):
                    for i in range(2):
                        last = pe.matmul(bank[:, 7, c:c + 1], k_tokens[:, i, c * P:(c + 1) * P], k.ones[:, 0:1],
                                         start=(i == 0), stop=(i == 1))
                last.then_inc(kv_done.sem, 1)
                pe.wait_ge(kv_ready.sem, DK)
                for w, slot in ((kv, 4), (z_heads, 5)):
                    for c in range(DK):
                        last = pe.matmul(bank[:, slot, c * LOW2:(c + 1) * LOW2], w[:, c, :], qT[:, c, :],
                                         start=True, stop=True)
                    last.then_inc(num_den.sem, 1)
                pe.wait_ge(tapped.sem, WAVELET_TAPS)
                for j in range(TILES):
                    for c in range(DK):
                        last = pe.transpose(bank[:, j // 2, ((j % 2) * DK + c) * P:((j % 2) * DK + c + 1) * P],
                                            back1[:, c, j * P:(j + 1) * P], k.ident[:])
                    if j % 2:
                        last.then_inc(back_turned.sem, 1)

            block_ctx.close()
            signal.clear()


WAVELET_TAPS = 2 * (2 * DK * FILTER) + 2 * (2 * DK * 5)



A_HEADS, A_W = 16, 64
INNER = A_HEADS * A_W
KEYS_ALL = SEQ + CTX
KT = TILES + 1
PAIRS = A_HEADS // 2
GROUP = 4
TP = 2 * TILES
GP = TP // GROUP
PIECES = 8
CHUNKS = 2 * GROUP + 1
STACKED = 8 * 16
F16 = mybir.dt.float16

BANK7 = {2: ["piece"], 3: ["piece"] * 2, 4: ["values"], 5: ["out", "piece"], 6: ["out", "piece"],
         7: ["piece"] * 3, 8: ["values"], 9: ["out"], 10: ["out"], 12: ["values"], 13: ["out"], 14: ["out"],
         16: ["values", "out", "out"]}


def attention_stage(k):
    nc, d = k.nc, k.dram
    with ExitStack() as ctx:
        def sb(name, shape, dt=F32):
            return ctx.enter_context(nc.sbuf_tensor(name, shape, dt))

        media = sb("media", [CTX, BATCH, DM])
        mediaT = sb("mediaT", [P, DK, BATCH, CTX])
        m_stats = sb("m_stats", [CTX, BATCH, 6])
        m_moments = sb("m_moments", [CTX, BATCH, 2])
        m_std = sb("m_std", [CTX, BATCH])
        m_rstd = sb("m_rstd", [CTX, BATCH])
        m_eps = sb("m_eps", [CTX, 1])
        ln = sb("ln", [P, 4, DK])
        n = NormBuffers(sb, "attention")
        n2 = NormBuffers(sb, "attention2")
        z = sb("attention_z", [P, TILES, DM])
        zT = sb("attention_zT", [P, DK, KEYS_ALL])
        w_q = sb("attention_w_q", [P, DK, P])
        w_k = sb("attention_w_k", [P, DK, P])
        w_v = sb("attention_w_v", [P, DK, P])
        w_o = sb("attention_w_o", [P, 2, DM])
        q_new = sb("q_new", [P, 2, SEQ], BF16)
        k_new = sb("k_new", [P, 2, KEYS_ALL], BF16)
        v_new = sb("v_new", [P, KT, 2, P], BF16)
        q_stack = sb("q_stack", [P, 2, SEQ], BF16)
        k_high = sb("k_high", [P, 2, KEYS_ALL], BF16)
        k_low = sb("k_low", [P, 2, KEYS_ALL], BF16)
        v_cols = sb("v_cols", [P, 2, KT, P], BF16)
        neg_max = sb("neg_max", [P, TP])
        den = sb("attention_den", [P, TP])
        inv_den = sb("inv_den", [P, TP])
        numer = sb("numer", [P, GROUP, KEYS_ALL])
        nT_high = sb("nT_high", [P, 2, KT, GROUP * P], F16)
        nT_low = sb("nT_low", [P, 2, KT, GROUP * P], F16)
        values = sb("values", [P, 2, GROUP * P])
        bank = ctx.enter_context(nc.psum_tensor("attention_psum", [P, 8, BANK], F32))
        logits_flat = bank[:, 0:5, :].rearrange("p a b -> p (a b)")
        ODD = 3 * BANK - CTX

        def logits(t):
            return logits_flat[:, ODD:ODD + KEYS_ALL] if t % 2 else logits_flat[:, 0:KEYS_ALL]

        def logits_z(t, half):
            return bank[:, (3 if t % 2 else 0) + half, :]

        def logits_ctx(t):
            return bank[:, 2, BANK - CTX:] if t % 2 else bank[:, 2, 0:CTX]

        def z_at(t):
            return CTX if t % 2 else 0

        def ctx_at(t):
            return 0 if t % 2 else SEQ

        with Prologue(nc) as pre:
            loaded = pre.semaphore("attention_loaded")
            m_done = pre.semaphore("media_done")
            m_var = pre.semaphore("media_var")
            m_root = pre.semaphore("media_root")
            m_turned = pre.semaphore("media_turned")
            block = pre.block()

            @block.sync
            def _(sp):
                sp.dma_start(media[:], d["ctx_1024"].rearrange("b l d -> l b d")).then_inc(loaded, 16)
                for i, name in enumerate(("m_g", "m_b", "l_g", "l_b")):
                    sp.dma_start(ln[:, i, :], d["L1_xattn_ln_" + name].rearrange("(c p) -> p c", p=P),
                                 allow_slow_non_contiguous=True).then_inc(loaded, 16)
                sp.wait_ge(loaded, 80)

            @block.vector
            def _(dve):
                dve.memset(m_eps[:], LN_EPS)
                dve.wait_ge(loaded, 80)
                for b in range(BATCH):
                    last = dve.bn_stats(m_stats[:, b, :], media[:, b, :])
                last.then_inc(m_done, 1)
                dve.wait_ge(m_done, 1)
                for b in range(BATCH):
                    last = dve.bn_aggr(m_moments[:, b, :], m_stats[:, b, :])
                last.then_inc(m_var, 1)
                dve.wait_ge(m_root, 1)
                dve.reciprocal(m_rstd[:], m_std[:]).then_inc(m_done, 1)
                dve.wait_ge(m_done, 2)
                for b in range(BATCH):
                    last = dve.tensor_scalar(media[:, b, :], media[:, b, :], m_moments[:, b, 0:1], m_rstd[:, b:b + 1],
                                             ALU.subtract, ALU.mult)
                last.then_inc(m_done, 1)
                dve.wait_ge(m_turned, 1)
                for c in range(DK):
                    last = dve.tensor_scalar(mediaT[:, c], bank[:, c, :].rearrange("p (b l) -> p b l", l=P)[:, :, 0:CTX],
                                             ln[:, 0, c:c + 1], ln[:, 1, c:c + 1], ALU.mult, ALU.add)
                last.then_inc(m_done, 1)
                dve.wait_ge(m_done, 4)

            @block.scalar
            def _(act):
                act.wait_ge(m_var, 1)
                act.activation(m_std[:], m_moments[:, :, 1], ACT.Sqrt, bias=m_eps[:, 0:1]).then_inc(m_root, 1)

            @block.tensor
            def _(pe):
                pe.wait_ge(m_done, 3)
                for b in range(BATCH):
                    for c in range(DK):
                        last = pe.transpose(bank[:, c, b * P:b * P + CTX], media[:, b, c * P:(c + 1) * P],
                                            k.ident[0:CTX, 0:CTX])
                last.then_inc(m_turned, 1)

        with ExitStack() as run, nc.Fori(0, BATCH) as b:
            signal = BatchSignals(run, nc, "attention_")
            chain = Chain(signal("chain"))
            moments_ready = signal("moments_ready")
            std_ready = signal("std_ready")
            normed = signal("normed")
            moments2_ready = signal("moments2_ready")
            std2_ready = signal("std2_ready")
            normed2 = signal("normed2")
            turned = signal("turned")
            zT_ready = signal("zT_ready")
            w_loaded = signal("w_loaded")
            wo_loaded = signal("wo_loaded")
            piece_done = signal("piece_done")
            piece_high = signal("piece_high")
            piece_low = signal("piece_low")
            stacked = [signal("stacked_a"), signal("stacked_b")]
            scored = signal("scored")
            maxed = signal("maxed")
            numer_ready = signal("numer_ready")
            n_turned = signal("n_turned")
            n_high = signal("n_high")
            n_low = signal("n_low")
            values_done = signal("values_done")
            values_ready = signal("values_ready")
            den_ready = signal("den_ready")
            out_done = signal("out_done")
            added = signal("added")
            copied = signal("copied")
            block_ctx = ExitStack()
            block = block_ctx.enter_context(nc.Block())

            def numer_part(t, kt):
                if kt == TILES:
                    return numer[:, t % GROUP, ctx_at(t):ctx_at(t) + CTX]
                return numer[:, t % GROUP, z_at(t) + kt * P:z_at(t) + (kt + 1) * P]

            def piece_shape(i):
                if i < 2:
                    return "q", i * BANK, BANK
                if i < 5:
                    return "k", (i - 2) * BANK, min(BANK, KEYS_ALL - (i - 2) * BANK)
                return "v", (i - 5) * 4, min(4, KT - (i - 5) * 4)

            def new_v(i, part):
                _, first, count = piece_shape(i)
                rows = CTX if first == TILES else P
                return v_new[0:rows, first:first + count, :, part * A_W:(part + 1) * A_W]

            def piece_psum(i):
                kind, first, count = piece_shape(i)
                if kind != "v":
                    return bank[:, 7, 0:count]
                rows = CTX if first == TILES else P
                return bank[0:rows, 7, 0:count * P].rearrange("p (t a w) -> p t a w", a=2, w=A_W)

            def over_pairs(engine, body):
                with engine.Fori(0, PAIRS - 1) as pair:
                    body(pair, True)
                body(PAIRS - 1, False)

            def schedule(last_pair):
                counts = {"piece": 0, "values": 0, "out": 0}
                out = []
                for t, uses in BANK7.items():
                    for use in uses:
                        if use != "piece" or not last_pair:
                            out.append((t, use, counts[use]))
                        counts[use] += 1
                return out

            @block.tensor
            def _(pe):
                transpose_on_tensor(pe, k, z, bank, normed2, 0, turned)

                def piece(i, done):
                    kind, first, count = piece_shape(i)
                    if kind == "v":
                        for s in range(count):
                            kt = first + s
                            rows = CTX if kt == TILES else P
                            for c in range(DK):
                                last = pe.matmul(bank[0:rows, 7, s * P:(s + 1) * P], zT[:, c, kt * P:kt * P + rows],
                                                 w_v[:, c, :], start=(c == 0), stop=(c == DK - 1))
                    else:
                        w = w_q if kind == "q" else w_k
                        for c in range(DK):
                            last = pe.matmul(bank[:, 7, 0:count], w[:, c, :], zT[:, c, first:first + count],
                                             start=(c == 0), stop=(c == DK - 1))
                    last.then_inc(piece_done.sem, 1)

                pe.wait_ge(zT_ready.sem, 4)
                pe.wait_ge(copied.sem, 1)
                pe.wait_ge(w_loaded.sem, 48)
                for i in range(PIECES):
                    if i:
                        pe.wait_ge(piece_low.sem, i)
                    piece(i, 0)

                def body(pair, project):
                    def free_bank7(use, i):
                        order = schedule(not project)
                        at = [(u, n) for _, u, n in order].index((use, i))
                        if at == 0:
                            pe.wait_ge(piece_low.sem, pair * PIECES + PIECES)
                            pe.wait_ge(added.sem, pair * (TP // 2) + 1)
                            return
                        _, before, m = order[at - 1]
                        if before == "piece":
                            pe.wait_ge(piece_low.sem, pair * PIECES + PIECES + m + 1)
                        elif before == "out":
                            pe.wait_ge(added.sem, pair * (TP // 2) + m + 2)
                        else:
                            pe.wait_ge(values_ready.sem, pair * GP + m + 1)

                    def score_z(t):
                        a, i = divmod(t, TILES)
                        if i == 0:
                            pe.wait_ge(stacked[a].sem, pair * STACKED + STACKED)
                        pe.wait_ge(numer_ready.sem, pair * TP + t + 1)
                        for half in range(HALVES):
                            for part, kx in enumerate((k_high, k_low)):
                                pe.matmul(logits_z(t, half), q_stack[:, a, i * P:(i + 1) * P],
                                          kx[:, a, half * BANK:(half + 1) * BANK], start=(part == 0), stop=(part == 1))

                    def score_ctx(t):
                        a, i = divmod(t, TILES)
                        pe.wait_ge(numer_ready.sem, pair * TP + t + 2)
                        for part, kx in enumerate((k_high, k_low)):
                            last = pe.matmul(logits_ctx(t), q_stack[:, a, i * P:(i + 1) * P], kx[:, a, SEQ:],
                                             start=(part == 0), stop=(part == 1))
                        last.then_inc(scored.sem, 1)

                    def turn(t):
                        g, r = divmod(t, GROUP)
                        for u in range(2 + (r == GROUP - 1)):
                            chunk = g * CHUNKS + 2 * r + u
                            pe.wait_ge(n_low.sem, pair * GP * CHUNKS + chunk + 1)
                            for s in range(GROUP):
                                if u < 2:
                                    last = pe.transpose(bank[:, 5 + chunk % 2, s * P:(s + 1) * P],
                                                        numer_part(t, 4 * u + s), k.ident[:])
                                else:
                                    last = pe.transpose(bank[0:CTX, 5 + chunk % 2, s * P:(s + 1) * P],
                                                        numer_part(g * GROUP + s, TILES), k.ident[:])
                            last.then_inc(n_turned.sem, 1)

                    def values_of(g):
                        a = g // (GP // 2)
                        pe.wait_ge(n_low.sem, pair * GP * CHUNKS + (g + 1) * CHUNKS + 2)
                        for kt in range(KT):
                            rows = CTX if kt == TILES else P
                            for part, nx in enumerate((nT_high, nT_low)):
                                last = pe.matmul(bank[:, 7, :], v_cols[0:rows, a, kt, :], nx[0:rows, g % 2, kt, :],
                                                 start=(kt == 0 and part == 0), stop=(kt == KT - 1 and part == 1))
                        last.then_inc(values_done.sem, 1)

                    def out_of(i):
                        g, r = divmod(i, 2)
                        a = g // (GP // 2)
                        if i == 0:
                            pe.wait_ge(wo_loaded.sem, pair * 64 + 64)
                        pe.wait_ge(values_ready.sem, pair * GP + g + 1)
                        for s in range(2):
                            last = pe.matmul(bank[:, 7, s * DM:(s + 1) * DM],
                                             values[:, g % 2, (2 * r + s) * P:(2 * r + s + 1) * P], w_o[:, a, :],
                                             start=True, stop=True)
                        last.then_inc(out_done.sem, 1)

                    score_z(0)
                    score_ctx(0)
                    score_z(1)
                    order = schedule(not project)
                    for t in range(TP + 1):
                        if t < TP:
                            if t + 1 < TP:
                                score_ctx(t + 1)
                            else:
                                pe.wait_ge(numer_ready.sem, pair * TP + t + 3)
                            turn(t)
                            if t + 2 < TP:
                                score_z(t + 2)
                        for at, use, i in order:
                            if at == t:
                                free_bank7(use, i)
                                if use == "piece":
                                    if i == 0:
                                        pe.wait_ge(w_loaded.sem, pair * 48 + 96)
                                    piece(i, None)
                                elif use == "values":
                                    values_of(i)
                                else:
                                    out_of(i)

                over_pairs(pe, body)

            def split_high(act, i, scale_q):
                kind, first, count = piece_shape(i)
                if kind == "q":
                    act.activation(q_new[:, 0, first:first + count], piece_psum(i), ACT.Copy,
                                   scale=scale_q).then_inc(piece_high.sem, 1)
                elif kind == "k":
                    act.copy(k_new[:, 0, first:first + count], piece_psum(i)).then_inc(piece_high.sem, 1)
                else:
                    act.copy(new_v(i, 0), piece_psum(i)).then_inc(piece_high.sem, 1)

            def split_low(dve, i, scale_q):
                kind, first, count = piece_shape(i)
                if kind == "q":
                    last = dve.scalar_tensor_tensor(out=q_new[:, 1, first:first + count], in0=piece_psum(i), scalar=scale_q,
                                                    in1=q_new[:, 0, first:first + count], op0=ALU.mult, op1=ALU.subtract)
                elif kind == "k":
                    last = dve.tensor_tensor(k_new[:, 1, first:first + count], piece_psum(i),
                                             k_new[:, 0, first:first + count], ALU.subtract)
                else:
                    last = dve.tensor_tensor(new_v(i, 1), piece_psum(i), new_v(i, 0), ALU.subtract)
                last.then_inc(piece_low.sem, 1)

            SCALE = float(A_W) ** -0.5

            @block.scalar
            def _(act):
                roots_on_scalar(act, n, moments_ready, std_ready)
                roots_on_scalar(act, n2, moments2_ready, std2_ready)
                for q in range(4):
                    c = q % DK
                    act.wait_ge(turned.sem, q + 1)
                    act.activation(columns_of(zT, q), bank[:, q, :], ACT.Identity, scale=ln[:, 2, c:c + 1],
                                   bias=ln[:, 3, c:c + 1]).then_inc(zT_ready.sem, 1)
                for i in range(PIECES):
                    act.wait_ge(piece_done.sem, i + 1)
                    split_high(act, i, SCALE)

                def body(pair, project):
                    order = schedule(not project)
                    for t in range(TP + 1):
                        if t < TP:
                            g, r = divmod(t, GROUP)
                            act.wait_ge(maxed.sem, pair * TP + t + 1)
                            act.activation(numer[:, r, :], logits(t), ACT.Exp, bias=neg_max[:, t:t + 1],
                                           accum_out=den[:, t:t + 1]).then_inc(numer_ready.sem, 1)
                            for u in range(2 + (r == GROUP - 1)):
                                chunk = g * CHUNKS + 2 * r + u
                                act.wait_ge(n_turned.sem, pair * GP * CHUNKS + chunk + 1)
                                if r == 0 and u == 0:
                                    act.wait_ge(values_done.sem, pair * GP + g + 1)
                                src = bank[:, 5 + chunk % 2, :].rearrange("p (s q) -> p s q", q=P)
                                if u < 2:
                                    dst = nT_high[:, g % 2, 4 * u:4 * u + 4, r * P:(r + 1) * P]
                                else:
                                    dst, src = nT_high[0:CTX, g % 2, TILES, :], bank[0:CTX, 5 + chunk % 2, :]
                                act.copy(dst, src).then_inc(n_high.sem, 1)
                        for at, use, i in order:
                            if at != t:
                                continue
                            if use == "piece":
                                act.wait_ge(piece_done.sem, pair * PIECES + PIECES + i + 1)
                                if i == 0:
                                    for s in stacked:
                                        act.wait_ge(s.sem, pair * STACKED + STACKED)
                                split_high(act, i, SCALE)
                            elif use == "values":
                                act.wait_ge(values_done.sem, pair * GP + i + 3)
                                act.copy(values[:, i % 2, :], bank[:, 7, :]).then_inc(values_ready.sem, 1)

                over_pairs(act, body)

            @block.vector
            def _(dve):
                dve.sem_inc(numer_ready.sem, 2)
                dve.sem_inc(n_low.sem, 2)
                dve.sem_inc(values_done.sem, 2)
                dve.sem_inc(added.sem, 1)
                dve.tensor_copy(zT[:, :, SEQ:].rearrange("p c (o l) -> p c o l", o=1),
                                mediaT[:, :, bass.ds(b, 1), :]).then_inc(copied.sem, 1)
                norm_on_vector(dve, n, lambda j: k.X[:, b * TILES + j, :], z, chain, std_ready, moments_ready, normed)
                dve.wait_ge(normed.sem, TILES)
                norm_on_vector(dve, n2, lambda j: z[:, j, :], z, chain, std2_ready, moments2_ready, normed2)
                for i in range(PIECES):
                    dve.wait_ge(piece_high.sem, i + 1)
                    split_low(dve, i, SCALE)

                def body(pair, project):
                    order = schedule(not project)

                    def low(t):
                        g, r = divmod(t, GROUP)
                        for u in range(2 + (r == GROUP - 1)):
                            chunk = g * CHUNKS + 2 * r + u
                            dve.wait_ge(n_high.sem, pair * GP * CHUNKS + chunk + 1)
                            src = bank[:, 5 + chunk % 2, :].rearrange("p (s q) -> p s q", q=P)
                            if u < 2:
                                at = (slice(None), g % 2, slice(4 * u, 4 * u + 4), slice(r * P, (r + 1) * P))
                            else:
                                at, src = (slice(0, CTX), g % 2, TILES, slice(None)), bank[0:CTX, 5 + chunk % 2, :]
                            dve.tensor_tensor(nT_low[at], src, nT_high[at], ALU.subtract).then_inc(n_low.sem, 1)

                    for t in range(TP + 2):
                        if t < TP:
                            dve.wait_ge(scored.sem, pair * TP + t + 1)
                            dve.tensor_reduce(neg_max[:, t:t + 1], logits(t), AXIS.X, ALU.max,
                                              negate=True).then_inc(maxed.sem, 1)
                        if 1 <= t <= TP:
                            low(t - 1)
                        for at, use, i in order:
                            if at != t - 1:
                                continue
                            if use == "piece":
                                dve.wait_ge(piece_high.sem, pair * PIECES + PIECES + i + 1)
                                split_low(dve, i, SCALE)
                            elif use == "out":
                                g, r = divmod(i, 2)
                                cols = slice(g * GROUP, (g + 1) * GROUP)
                                if r == 0:
                                    dve.reciprocal(inv_den[:, cols], den[:, cols]).then_inc(den_ready.sem, 1)
                                dve.wait_ge(out_done.sem, pair * (TP // 2) + i + 1)
                                dve.wait_ge(den_ready.sem, pair * GP + g + 1)
                                for s in range(2):
                                    tile = g * GROUP + 2 * r + s
                                    x = k.X[:, b * TILES + tile % TILES, :]
                                    last = dve.scalar_tensor_tensor(out=x, in0=bank[:, 7, s * DM:(s + 1) * DM],
                                                                    scalar=inv_den[:, tile:tile + 1], in1=x,
                                                                    op0=ALU.mult, op1=ALU.add)
                                last.then_inc(added.sem, 1)

                over_pairs(dve, body)
                dve.wait_ge(added.sem, PAIRS * TP // 2 + 1)

            @block.sync
            def _(sp):
                heads_of = {"q": d["L1_xattn_Wq"], "k": d["L1_xattn_Wkv"][:, 0:INNER], "v": d["L1_xattn_Wkv"][:, INNER:]}
                w_rows = {x: w.rearrange("(c p) n -> p c n", p=P) for x, w in heads_of.items()}

                def load_weights(pair):
                    for dst, x in ((w_q, "q"), (w_k, "k"), (w_v, "v")):
                        sp.dma_start(dst[:], w_rows[x][:, :, bass.ds(pair * P, P)]).then_inc(w_loaded.sem, 16)

                def stack(a, pair_done, scored_at, values_at):
                    rows = slice(a * A_W, (a + 1) * A_W)
                    if scored_at is not None:
                        sp.wait_ge(scored.sem, scored_at)
                    upper, lower = slice(0, A_W), slice(A_W, P)
                    for dst, src in ((q_stack[upper, a, :], q_new[rows, 0, :]), (q_stack[lower, a, :], q_new[rows, 1, :]),
                                     (k_high[upper, a, :], k_new[rows, 0, :]), (k_high[lower, a, :], k_new[rows, 0, :]),
                                     (k_low[upper, a, :], k_new[rows, 1, :]), (k_low[lower, a, :], k_new[rows, 1, :])):
                        sp.dma_start(dst, src).then_inc(stacked[a].sem, 16)
                    if values_at is not None:
                        sp.wait_ge(values_done.sem, values_at)
                    sp.dma_start(v_cols[:, a, 0:TILES], v_new[:, 0:TILES, a, :]).then_inc(stacked[a].sem, 16)
                    sp.dma_start(v_cols[0:CTX, a, TILES], v_new[0:CTX, TILES, a, :]).then_inc(stacked[a].sem, 16)

                load_weights(0)
                sp.wait_ge(piece_low.sem, PIECES)
                for a in range(2):
                    stack(a, 0, None, None)

                def body(pair, project):
                    if project:
                        sp.wait_ge(piece_done.sem, pair * PIECES + PIECES)
                        load_weights(pair + 1)
                    sp.wait_ge(added.sem, pair * (TP // 2) + 1)
                    for a in range(2):
                        for half in range(2):
                            sp.dma_start(w_o[half * A_W:(half + 1) * A_W, a, :],
                                         d["L1_xattn_Wout"][bass.ds(pair * P + a * A_W, A_W), :]).then_inc(wo_loaded.sem, 16)
                    if project:
                        sp.wait_ge(piece_low.sem, pair * PIECES + 2 * PIECES)
                        stack(0, None, pair * TP + TILES, pair * GP + GP // 2 + 2)
                        stack(1, None, pair * TP + TP, pair * GP + GP + 2)

                over_pairs(sp, body)

            block_ctx.close()
            signal.clear()



FP8_MAX = 448.0
FP8_LEAST_NORMAL = 2.0 ** -6
EXPONENT_BITS = 0x7F800000
ROUNDER = 1.5 * 2.0 ** 20


def round_to_fp8(dve, v, c, out, chain):
    chain.link(dve, dve.tensor_scalar(c.bitcast(I32), v.bitcast(I32), EXPONENT_BITS, None, ALU.bitwise_and))
    chain.link(dve, dve.tensor_scalar(c, c, FP8_LEAST_NORMAL, ROUNDER, ALU.max, ALU.mult))
    chain.link(dve, dve.scalar_tensor_tensor(out=v, in0=v, scalar=-FP8_MAX, in1=c, op0=ALU.max, op1=ALU.add))
    return dve.tensor_tensor(out, v, c, ALU.subtract)


def quantized_stage(k):
    nc, d = k.nc, k.dram
    with ExitStack() as ctx:
        def sb(name, shape, dt=F32):
            return ctx.enter_context(nc.sbuf_tensor(name, shape, dt))

        n = NormBuffers(sb, "quant")
        y = sb("quant_y", [P, BATCH * TILES, DM])
        w = sb("quant_w", [P, DK * DM])
        w_round = sb("w_round", [P, DK * DM])
        w_fp8 = sb("w_fp8", [P, DK, DM], BF16)
        bias = sb("quant_bias", [P, DM])
        tops = sb("tops", [P, BATCH])
        top = sb("top", [P, 2])
        top_row = sb("top_row", [2, 1])
        top_diag = sb("top_diag", [2, 2])
        scale = sb("quant_scale", [P, 2])
        inverse = sb("inverse", [P, 2])
        inverse_both = sb("inverse_both", [P, 1])
        v = sb("quant_v", [P, 2, 4 * DM])
        c = sb("quant_c", [P, 2, 4 * DM])
        x_fp8 = sb("x_fp8", [P, TILES, DM])
        xT_fp8 = sb("xT_fp8", [P, DK, SEQ], BF16)
        out = sb("quant_out", [P, 2, 2, DM], BF16)
        bank = ctx.enter_context(nc.psum_tensor("quant_psum", [P, 8, BANK], F32))

        with ExitStack() as run, nc.Fori(0, BATCH) as b:
            signal = BatchSignals(run, nc, "quant_norm_")
            chain = Chain(signal("chain"))
            moments_ready = signal("moments_ready")
            std_ready = signal("std_ready")
            normed = signal("normed")
            block_ctx = ExitStack()
            block = block_ctx.enter_context(nc.Block())

            @block.vector
            def _(dve):
                batch = y[:, bass.ds(b * TILES, TILES), :]
                norm_on_vector(dve, n, lambda j: k.X[:, b * TILES + j, :], batch, chain, std_ready,
                               moments_ready, normed)
                dve.wait_ge(normed.sem, TILES)
                chain.link(dve, dve.tensor_reduce(tops[:, bass.ds(b, 1)], batch, AXIS.XY, ALU.max,
                                                  apply_absolute_value=True))

            @block.scalar
            def _(act):
                roots_on_scalar(act, n, moments_ready, std_ready)

            block_ctx.close()
            signal.clear()

        with Prologue(nc) as pre:
            loaded = pre.semaphore("quant_loaded")
            top_ready = pre.semaphore("top_ready")
            top_turned = pre.semaphore("top_turned")
            diag_ready = pre.semaphore("diag_ready")
            top_spread = pre.semaphore("top_spread")
            chain = Chain(pre.counter("quant_scale_chain"))
            block = pre.block()

            @block.sync
            def _(sp):
                sp.dma_start(w[:].rearrange("p (c n) -> p c n", c=DK),
                             d["L1_ffn_weight"].rearrange("(c p) n -> p c n", p=P)).then_inc(loaded, 16)
                row = d["L1_ffn_bias"].rearrange("(o n) -> o n", o=1)
                sp.dma_start(bias[:], row.broadcast_to([P, DM])).then_inc(loaded, 16)
                sp.wait_ge(loaded, 32)

            @block.vector
            def _(dve):
                dve.tensor_reduce(top[:, 0:1], tops[:], AXIS.X, ALU.max)
                dve.wait_ge(loaded, 32)
                dve.tensor_reduce(top[:, 1:2], w[:], AXIS.X, ALU.max,
                                  apply_absolute_value=True).then_inc(top_ready, 1)
                dve.wait_ge(top_turned, 1)
                chain.link(dve, dve.tensor_reduce(top_row[:], bank[0:2, 0, 0:P], AXIS.X, ALU.max))
                dve.tensor_scalar(top_diag[:], k.ident[0:2, 0:2], top_row[:], None, ALU.mult).then_inc(diag_ready, 1)
                dve.wait_ge(top_spread, 1)
                chain.link(dve, dve.tensor_scalar(scale[:], bank[:, 1, 0:2], 1e-12, None, ALU.max))
                chain.link(dve, dve.reciprocal(scale[:], scale[:]))
                chain.link(dve, dve.tensor_scalar(scale[:], scale[:], FP8_MAX, FP8_MAX, ALU.mult, ALU.min))
                chain.link(dve, dve.reciprocal(inverse[:], scale[:]))
                dve.tensor_tensor(inverse_both[:], inverse[:, 0:1], inverse[:, 1:2], ALU.mult)
                chain.link(dve, dve.tensor_scalar(w[:], w[:], scale[:, 1:2], FP8_MAX, ALU.mult, ALU.min))
                chain.link(dve, round_to_fp8(dve, w[:], w_round[:], w_fp8[:].rearrange("p c n -> p (c n)"), chain))

            @block.tensor
            def _(pe):
                pe.wait_ge(top_ready, 1)
                pe.transpose(bank[0:2, 0, 0:P], top[:], k.ident[:]).then_inc(top_turned, 1)
                pe.wait_ge(diag_ready, 1)
                pe.matmul(bank[:, 1, 0:2], k.ones[0:2, :], top_diag[:], start=True, stop=True).then_inc(top_spread, 1)

        with ExitStack() as run, nc.Fori(0, BATCH) as b:
            signal = BatchSignals(run, nc, "quant_")
            chain = Chain(signal("chain"))
            scaled = signal("scaled")
            v_ready = signal("v_ready")
            rounded = signal("rounded")
            turned = signal("turned")
            xT_ready = signal("xT_ready")
            multiplied = signal("multiplied")
            out_ready = signal("out_ready")
            added = signal("added")
            block_ctx = ExitStack()
            block = block_ctx.enter_context(nc.Block())

            @block.gpsimd
            def _(pool):
                for half in range(HALVES):
                    pool.wait_ge(scaled.sem, half + 1)
                    pool.tensor_scalar(v[:, half, :], v[:, half, :], FP8_MAX, None, ALU.min).then_inc(v_ready.sem, 1)

            @block.vector
            def _(dve):
                for half in range(HALVES):
                    dve.wait_ge(v_ready.sem, half + 1)
                    tiles = x_fp8[:, half * 4:half * 4 + 4, :].rearrange("p j n -> p (j n)")
                    round_to_fp8(dve, v[:, half, :], c[:, half, :], tiles, chain).then_inc(rounded.sem, 4)
                for pair in range(TILES // 2):
                    dve.wait_ge(multiplied.sem, pair + 1)
                    for i in range(2):
                        dve.scalar_tensor_tensor(out=out[:, pair % 2, i, :], in0=bank[:, 4 + pair, i * DM:(i + 1) * DM],
                                                 scalar=inverse_both[:], in1=bias[:], op0=ALU.mult,
                                                 op1=ALU.add).then_inc(out_ready.sem, 1)
                    dve.wait_ge(out_ready.sem, 2 * pair + 2)
                    js = bass.ds(b * TILES + pair * 2, 2)
                    chain.link(dve, dve.tensor_tensor(k.X[:, js, :], k.X[:, js, :], out[:, pair % 2], ALU.add))

            @block.scalar
            def _(act):
                for half in range(HALVES):
                    ys = y[:, bass.ds(b * TILES + half * 4, 4), :].rearrange("p j n -> p (j n)")
                    act.mul(v[:, half, :], ys, scale[:, 0:1]).then_inc(scaled.sem, 1)
                for q in range(4):
                    act.wait_ge(turned.sem, q + 1)
                    act.copy(columns_of(xT_fp8, q), bank[:, q, :]).then_inc(xT_ready.sem, 1)

            @block.tensor
            def _(pe):
                transpose_on_tensor(pe, k, x_fp8, bank, rounded, 0, turned)
                for j in range(TILES):
                    pe.wait_ge(xT_ready.sem, DK * (1 + j // 4))
                    for i in range(DK):
                        last = pe.matmul(bank[:, 4 + j // 2, (j % 2) * DM:(j % 2 + 1) * DM],
                                         xT_fp8[:, i, j * P:(j + 1) * P], w_fp8[:, i, :],
                                         start=(i == 0), stop=(i == DK - 1))
                    if j % 2:
                        last.then_inc(multiplied.sem, 1)

            block_ctx.close()
            signal.clear()


def decoder(nc, dram):
    with ExitStack() as ctx:
        k = Kernel(nc, ctx, dram)
        load_residual(k)
        stages = [mamba_stage, memory_stage, expert_stage, wavelet_stage, attention_stage, quantized_stage]
        for stage in stages[:LAST_STAGE]:
            stage(k)
        store_residual(k)



TRANSPOSED = ("L0_attn_W_in", "L0_attn_W_x", "L0_attn_W_dt", "L0_attn_W_out", "L0_ffn_Wq", "L0_ffn_down_embed",
              "L1_ffn_weight")


def kernel(**inputs):
    import numpy as np
    import concourse.bacc as bacc
    from concourse.bass_utils import run_bass_kernel_spmd

    nc = bacc.Bacc("TRN2", target_bir_lowering=False, num_devices=1)
    arrays, dram = {}, {}
    for name, value in inputs.items():
        a = np.asarray(value)
        if name in TRANSPOSED:
            a = a.T
        if name == "L0_ffn_keys":
            a = a.transpose(3, 2, 0, 1)
        a = np.ascontiguousarray(a)
        arrays[f"in_{name}"] = a
        dram[name] = nc.dram_tensor(f"in_{name}", a.shape, mybir.dt.from_np(a.dtype), kind="ExternalInput").ap()
    dram["out"] = nc.dram_tensor("out_x", (BATCH, SEQ, DM), F32, kind="ExternalOutput").ap()
    decoder(nc, dram)
    result = run_bass_kernel_spmd(nc, [arrays], core_ids=[0])
    return result.results[0]["out_x"]
```

```python
from contextlib import ExitStack

import concourse.bass as bass
from concourse import mybir

ALU = mybir.AluOpType
ACT = mybir.ActivationFunctionType
AXIS = mybir.AxisListType
F32 = mybir.dt.float32
BF16 = mybir.dt.bfloat16
I32 = mybir.dt.int32
P = 128
BANK = 512
LN_EPS = 1e-5

BATCH, SEQ, DM = 4, 1024, 256
TILES = SEQ // P
DK = DM // P
HALVES = SEQ // BANK

LAST_STAGE = 6


class Signal:

    def __init__(self, ctx, nc, name):
        self.sem = ctx.enter_context(nc.semaphore(name))


class Chain:

    def __init__(self, steps):
        self.steps, self.count = steps, 0

    def link(self, engine, instruction):
        self.count += 1
        instruction.then_inc(self.steps.sem, 1)
        engine.wait_ge(self.steps.sem, self.count)


class BatchSignals:

    def __init__(self, ctx, nc, prefix):
        self.ctx, self.nc, self.prefix, self.all = ctx, nc, prefix, []

    def __call__(self, name):
        self.all.append(Signal(self.ctx, self.nc, self.prefix + name))
        return self.all[-1]

    def clear(self):
        for signal in self.all:
            self.nc.sync.sem_clear(signal.sem)
        self.nc.all_engine_barrier()


class Prologue(ExitStack):

    def __init__(self, nc):
        super().__init__()
        self.nc, self.semaphores = nc, []

    def semaphore(self, name):
        self.semaphores.append(self.enter_context(self.nc.semaphore(name)))
        return self.semaphores[-1]

    def counter(self, name):
        counter = Signal(self, self.nc, name)
        self.semaphores.append(counter.sem)
        return counter

    def block(self):
        self.callback(self.clear)
        return self.enter_context(self.nc.Block())

    def clear(self):
        for semaphore in self.semaphores:
            self.nc.sync.sem_clear(semaphore)
        self.nc.all_engine_barrier()


class Kernel:

    def __init__(self, nc, ctx, dram):
        self.nc, self.ctx, self.dram = nc, ctx, dram
        self.X = ctx.enter_context(nc.sbuf_tensor("X", [P, BATCH * TILES, DM], F32))
        self.ident = ctx.enter_context(nc.sbuf_tensor("ident", [P, P], F32))
        self.ones = ctx.enter_context(nc.sbuf_tensor("ones", [P, P], F32))


def load_residual(k):
    nc = k.nc
    with Prologue(nc) as pre:
        x_loaded = pre.semaphore("x_loaded")
        ident_filled = pre.semaphore("ident_filled")
        block = pre.block()

        @block.sync
        def _(sp):
            view = k.dram["x"].rearrange("b (j p) d -> b p j d", p=P)
            for b in range(BATCH):
                sp.dma_start(k.X[:, b * TILES:(b + 1) * TILES, :], view[b]).then_inc(x_loaded, 16)
            sp.wait_ge(x_loaded, 16 * BATCH)

        @block.gpsimd
        def _(pool):
            pool.memset(k.ones[:], 1.0).then_inc(ident_filled, 1)
            pool.wait_ge(ident_filled, 1)
            pool.affine_select(out=k.ident[:], in_=k.ones[:], compare_op=ALU.is_equal, fill=0.0,
                               base=0, pattern=[[-1, P]], channel_multiplier=1).then_inc(ident_filled, 1)
            pool.wait_ge(ident_filled, 2)


def store_residual(k):
    nc = k.nc
    with ExitStack() as ctx:
        stored = ctx.enter_context(nc.semaphore("stored"))
        block = ctx.enter_context(nc.Block())

        @block.sync
        def _(sp):
            view = k.dram["out"].rearrange("b (j p) d -> b p j d", p=P)
            for b in range(BATCH):
                sp.dma_start(view[b], k.X[:, b * TILES:(b + 1) * TILES, :]).then_inc(stored, 16)
            sp.wait_ge(stored, 16 * BATCH)



class NormBuffers:
    def __init__(self, sb, name):
        self.stats = sb(f"{name}_stats", [P, TILES, 6], F32)
        self.moments = sb(f"{name}_moments", [P, TILES, 2], F32)
        self.std = sb(f"{name}_std", [P, TILES], F32)
        self.rstd = sb(f"{name}_rstd", [P, TILES], F32)
        self.eps = sb(f"{name}_eps", [P, 1], F32)


def norm_on_vector(dve, n, source, out, chain, std_ready, moments_ready, normed):
    chain.link(dve, dve.memset(n.eps[:], LN_EPS))
    for j in range(TILES):
        last = dve.bn_stats(n.stats[:, j, :], source(j))
    chain.link(dve, last)
    for j in range(TILES):
        last = dve.bn_aggr(n.moments[:, j, :], n.stats[:, j, :])
    last.then_inc(moments_ready.sem, 1)
    dve.wait_ge(std_ready.sem, 1)
    chain.link(dve, dve.reciprocal(n.rstd[:], n.std[:]))
    for j in range(TILES):
        dve.tensor_scalar(out[:, j, :], source(j), n.moments[:, j, 0:1], n.rstd[:, j:j + 1],
                          ALU.subtract, ALU.mult).then_inc(normed.sem, 1)


def roots_on_scalar(act, n, moments_ready, std_ready):
    act.wait_ge(moments_ready.sem, 1)
    act.activation(n.std[:], n.moments[:, :, 1], ACT.Sqrt, bias=n.eps[:, 0:1]).then_inc(std_ready.sem, 1)


def transpose_on_tensor(pe, k, tiles, banks, tiles_ready, ready_at, turned):
    for half in range(HALVES):
        pe.wait_ge(tiles_ready.sem, ready_at + 4 * (half + 1))
        for c in range(DK):
            for i in range(4):
                last = pe.transpose(banks[:, half * DK + c, i * P:(i + 1) * P],
                                    tiles[:, half * 4 + i, c * P:(c + 1) * P], k.ident[:])
            last.then_inc(turned.sem, 1)


def columns_of(turned_tile, q, pad=0):
    half, c = divmod(q, DK)
    return turned_tile[:, c, pad + half * BANK:pad + (half + 1) * BANK]



D_INNER, D_STATE, D_CONV, DT_RANK = 512, 16, 4, 64
DI = D_INNER // P


def mamba_stage(k):
    nc, d = k.nc, k.dram
    with ExitStack() as ctx:
        def sb(name, shape, dt=F32):
            return ctx.enter_context(nc.sbuf_tensor(name, shape, dt))

        w_in = sb("w_in", [P, DK, 2 * D_INNER])
        w_x = sb("w_x", [P, DI, DT_RANK + 2 * D_STATE])
        w_dt = sb("w_dt", [DT_RANK, D_INNER])
        w_out = sb("w_out", [P, DI, DM])
        conv_w = sb("conv_w", [P, DI, D_CONV])
        conv_b = sb("conv_b", [P, DI])
        b_dt = sb("b_dt", [P, DI])
        skip = sb("skip", [P, DI])
        a_neg = sb("a_neg", [P, D_STATE, DI])
        skip_diag = sb("skip_diag", [P, DI, P])
        n = NormBuffers(sb, "mamba")
        xs = sb("xs", [P, DI, SEQ])
        gate = sb("gate", [P, DI, SEQ])
        delta = sb("delta", [P, DI, SEQ])
        du = sb("du", [P, DI, SEQ])
        decay = sb("decay", [P, DI, SEQ])
        drive = sb("drive", [P, DI, SEQ])
        h = sb("h", [P, DI, SEQ])
        b_row = sb("b_row", [P, 2, SEQ])
        c_row = sb("c_row", [P, 2, SEQ])
        z = h[:, 0:2, :].rearrange("p a (b d) -> p (a b) d", d=DM)
        zT = h[:, 2:4, :]
        xc = decay
        dt_low = drive[0:DT_RANK, 0, :]
        bc = drive[DT_RANK:DT_RANK + 2 * D_STATE, 1, :]
        convolved_x = du
        soft = h
        bank = ctx.enter_context(nc.psum_tensor("mamba_psum", [P, 8, BANK], F32))
        bc_dram = nc.dram_tensor("bc_scratch", [2 * D_STATE, SEQ], F32, kind="Internal").ap()

        with Prologue(nc) as pre:
            loaded = pre.semaphore("mamba_loaded")
            a_ready = pre.semaphore("mamba_a_ready")
            diag_ready = pre.semaphore("mamba_diag_ready")
            block = pre.block()

            @block.sync
            def _(sp):
                loads = [
                    (w_in[:], d["L0_attn_W_in"].rearrange("(c p) n -> p c n", p=P)),
                    (w_x[:], d["L0_attn_W_x"].rearrange("(c p) n -> p c n", p=P)),
                    (w_dt[:], d["L0_attn_W_dt"]),
                    (w_out[:], d["L0_attn_W_out"].rearrange("(c p) n -> p c n", p=P)),
                    (conv_w[:], d["L0_attn_conv_w"].rearrange("(c p) o n -> p c (o n)", p=P)),
                    (conv_b[:], d["L0_attn_conv_b"].rearrange("(c p) -> p c", p=P)),
                    (b_dt[:], d["L0_attn_b_dt"].rearrange("(c p) -> p c", p=P)),
                    (skip[:], d["L0_attn_D"].rearrange("(c p) -> p c", p=P)),
                    (a_neg[:], d["L0_attn_A_raw"].rearrange("n (c p) -> p n c", p=P)),
                ]
                for dst, src in loads:
                    sp.dma_start(dst, src, allow_slow_non_contiguous=True).then_inc(loaded, 16)
                sp.wait_ge(loaded, 16 * len(loads))

            @block.scalar
            def _(act):
                act.wait_ge(loaded, 16 * 9)
                act.activation(a_neg[:], a_neg[:], ACT.Exp).then_inc(a_ready, 1)

            @block.vector
            def _(dve):
                dve.wait_ge(a_ready, 1)
                dve.tensor_scalar(a_neg[:], a_neg[:], -1.0, None, ALU.mult)
                for c in range(DI):
                    last = dve.tensor_scalar(skip_diag[:, c, :], k.ident[:], skip[:, c:c + 1], None, ALU.mult)
                last.then_inc(diag_ready, 1)
                dve.wait_ge(diag_ready, 1)

        with ExitStack() as run, nc.Fori(0, BATCH) as b:
            signal = BatchSignals(run, nc, "mamba_")
            chain = Chain(signal("chain"))
            moments_ready = signal("moments_ready")
            std_ready = signal("std_ready")
            normed = signal("normed")
            turned = signal("turned")
            zT_ready = signal("zT_ready")
            projected = signal("projected")
            taken = signal("taken")
            convolved = signal("convolved")
            xs_ready = signal("xs_ready")
            low_ranked = signal("low_ranked")
            low_ready = signal("low_ready")
            bc_stored = signal("bc_stored")
            raised = signal("raised")
            delta_biased = signal("delta_biased")
            clamped = signal("clamped")
            exp_taken = signal("exp_taken")
            log_taken = signal("log_taken")
            delta_ready = signal("delta_ready")
            du_ready = signal("du_ready")
            b_loaded = [signal(f"b_loaded{r}") for r in range(2)]
            c_loaded = [signal(f"c_loaded{r}") for r in range(2)]
            steps = D_STATE * DI
            decay_ready = signal("decay_ready")
            drive_ready = signal("drive_ready")
            scanned = signal("scanned")
            weighted = signal("weighted")
            summed = signal("summed")
            gated = signal("gated")
            out_summed = signal("out_summed")
            added = signal("added")
            block_ctx = ExitStack()
            block = block_ctx.enter_context(nc.Block())

            @block.vector
            def _(dve):
                dve.sem_inc(scanned.sem, DI)
                dve.sem_inc(weighted.sem, DI + 1)
                norm_on_vector(dve, n, lambda j: k.X[:, b * TILES + j, :], z, chain, std_ready,
                               moments_ready, normed)
                for c in range(DI):
                    dve.wait_ge(taken.sem, 2 * c + 2)
                    y = convolved_x[:, c, :]
                    for t in (3, 2, 1, 0):
                        back = D_CONV - 1 - t
                        w = conv_w[:, c, t:t + 1]
                        if back == 0:
                            last = dve.tensor_scalar(y, xc[:, c, :], w, None, ALU.mult)
                        else:
                            last = dve.scalar_tensor_tensor(out=y[:, back:], in0=xc[:, c, 0:SEQ - back], scalar=w,
                                                            in1=y[:, back:], op0=ALU.mult, op1=ALU.add)
                        if t:
                            chain.link(dve, last)
                    last.then_inc(convolved.sem, 1)
                for half in range(HALVES):
                    dve.wait_ge(low_ranked.sem, half + 1)
                    cols = slice(half * BANK, (half + 1) * BANK)
                    dve.tensor_copy(dt_low[:, cols], bank[0:DT_RANK, 4 + half, :]).then_inc(low_ready.sem, 1)
                    dve.tensor_copy(bc[:, cols], bank[DT_RANK:DT_RANK + 2 * D_STATE, 4 + half, :]).then_inc(low_ready.sem, 1)
                dve.wait_ge(taken.sem, 16)
                for r in range(8):
                    c, half = divmod(r, HALVES)
                    dve.wait_ge(raised.sem, r + 1)
                    cols = slice(half * BANK, (half + 1) * BANK)
                    dve.tensor_scalar(soft[:, c, cols], bank[:, r % 4, :], b_dt[:, c:c + 1], 80.0,
                                      ALU.add, ALU.min).then_inc(clamped.sem, 1)
                    dve.tensor_scalar(delta[:, c, cols], bank[:, r % 4, :], b_dt[:, c:c + 1], None,
                                      ALU.add).then_inc(delta_biased.sem, 1)
                for c in range(DI):
                    dve.wait_ge(log_taken.sem, c + 1)
                    dve.tensor_tensor(delta[:, c, :], delta[:, c, :], soft[:, c, :],
                                      ALU.max).then_inc(delta_ready.sem, 1)
                    dve.wait_ge(delta_ready.sem, c + 1)
                    dve.tensor_tensor(du[:, c, :], delta[:, c, :], xs[:, c, :], ALU.mult).then_inc(du_ready.sem, 1)

                def scan(s, c):
                    dve.wait_ge(decay_ready.sem, s * DI + c + 1)
                    dve.wait_ge(drive_ready.sem, s * DI + c + 1)
                    dve.tensor_tensor_scan(h[:, c, :], decay[:, c, :], drive[:, c, :], 0.0,
                                           ALU.mult, ALU.add).then_inc(scanned.sem, 1)

                def weigh(s, c, r):
                    dve.wait_ge(scanned.sem, DI + s * DI + c + 1)
                    dve.tensor_tensor(h[:, c, :], h[:, c, :], c_row[:, r, :], ALU.mult).then_inc(weighted.sem, 1)

                with dve.Fori(0, D_STATE // 2) as pair:
                    for r in range(2):
                        s = pair * 2 + r
                        dve.wait_ge(c_loaded[r].sem, pair * 16 + 16)
                        for c in range(DI + 1):
                            if c < DI:
                                dve.wait_ge(summed.sem, s * DI + c + 1)
                                scan(s, c)
                            if c >= 1:
                                weigh(s, c - 1, r)
                for c in range(DI):
                    dve.wait_ge(summed.sem, steps + c + 1)
                    dve.tensor_tensor(xs[:, c, :], bank[:, 2 * c:2 * c + 2, :].rearrange("p a b -> p (a b)"),
                                      gate[:, c, :], ALU.mult).then_inc(gated.sem, 1)
                for j in range(TILES):
                    dve.wait_ge(out_summed.sem, j + 1)
                    dve.tensor_tensor(k.X[:, b * TILES + j, :], k.X[:, b * TILES + j, :], bank[:, j, 0:DM],
                                      ALU.add).then_inc(added.sem, 1)
                dve.wait_ge(added.sem, TILES)

            @block.scalar
            def _(act):
                roots_on_scalar(act, n, moments_ready, std_ready)
                for q in range(4):
                    act.wait_ge(turned.sem, q + 1)
                    act.copy(columns_of(zT, q), bank[:, q, :]).then_inc(zT_ready.sem, 1)
                for q in range(8):
                    c, half = divmod(q, HALVES)
                    act.wait_ge(projected.sem, q + 1)
                    act.copy(xc[:, c, half * BANK:(half + 1) * BANK], bank[:, 4 + q % 4, :]).then_inc(taken.sem, 1)
                for c in range(DI):
                    act.wait_ge(convolved.sem, c + 1)
                    act.activation(xs[:, c, :], convolved_x[:, c, :], ACT.Silu, bias=conv_b[:, c:c + 1]).then_inc(xs_ready.sem, 1)
                    for half in range(HALVES):
                        q = c * HALVES + half
                        act.wait_ge(projected.sem, 8 + q + 1)
                        act.activation(gate[:, c, half * BANK:(half + 1) * BANK], bank[:, 4 + q % 4, :],
                                       ACT.Silu).then_inc(taken.sem, 1)
                for c in range(DI):
                    act.wait_ge(clamped.sem, 2 * c + 2)
                    act.activation(soft[:, c, :], soft[:, c, :], ACT.Exp).then_inc(exp_taken.sem, 1)
                for c in range(DI):
                    act.wait_ge(exp_taken.sem, c + 1)
                    act.activation(soft[:, c, :], soft[:, c, :], ACT.Ln, bias=1.0).then_inc(log_taken.sem, 1)
                for c in range(DI):
                    act.wait_ge(delta_ready.sem, c + 1)
                with act.Fori(0, D_STATE) as s:
                    for c in range(DI):
                        act.wait_ge(scanned.sem, s * DI + c + 1)
                        act.activation(decay[:, c, :], delta[:, c, :], ACT.Exp,
                                       scale=a_neg[:, s, c:c + 1]).then_inc(decay_ready.sem, 1)

            @block.gpsimd
            def _(pool):
                for c in range(DI):
                    pool.wait_ge(du_ready.sem, c + 1)
                with pool.Fori(0, D_STATE // 2) as pair:
                    for r in range(2):
                        s = pair * 2 + r
                        pool.wait_ge(b_loaded[r].sem, pair * 16 + 16)
                        for c in range(DI):
                            pool.wait_ge(scanned.sem, s * DI + c + 1)
                            pool.tensor_tensor(drive[:, c, :], du[:, c, :], b_row[:, r, :],
                                               ALU.mult).then_inc(drive_ready.sem, 1)

            @block.tensor
            def _(pe):
                transpose_on_tensor(pe, k, z, bank, normed, 0, turned)

                def project(q):
                    m, half = divmod(q, HALVES)
                    if q >= 4:
                        pe.wait_ge(taken.sem, q - 3)
                    for c in range(DK):
                        last = pe.matmul(bank[:, 4 + q % 4, :], w_in[:, c, m * P:(m + 1) * P],
                                         zT[:, c, half * BANK:(half + 1) * BANK], start=(c == 0), stop=(c == DK - 1))
                    last.then_inc(projected.sem, 1)

                for q in range(8):
                    pe.wait_ge(zT_ready.sem, 2 * (q % 2) + 2)
                    project(q)
                for q in range(8, 16):
                    project(q)
                for half in range(HALVES):
                    pe.wait_ge(xs_ready.sem, DI)
                    pe.wait_ge(taken.sem, 16)
                    for c in range(DI):
                        last = pe.matmul(bank[0:DT_RANK + 2 * D_STATE, 4 + half, :], w_x[:, c, :],
                                         xs[:, c, half * BANK:(half + 1) * BANK], start=(c == 0), stop=(c == DI - 1))
                    last.then_inc(low_ranked.sem, 1)
                for r in range(8):
                    c, half = divmod(r, HALVES)
                    pe.wait_ge(low_ready.sem, 2 * half + 1)
                    if r >= 4:
                        pe.wait_ge(delta_biased.sem, r - 3)
                    pe.matmul(bank[:, r % 4, :], w_dt[:, c * P:(c + 1) * P], dt_low[:, half * BANK:(half + 1) * BANK],
                              start=True, stop=True).then_inc(raised.sem, 1)
                pe.wait_ge(delta_biased.sem, 8)
                pe.wait_ge(low_ready.sem, 4)
                for c in range(DI):
                    for half in range(HALVES):
                        last = pe.matmul(bank[:, 2 * c + half, :], skip_diag[:, c, :],
                                         xs[:, c, half * BANK:(half + 1) * BANK], start=True, stop=False,
                                         skip_group_check=True)
                    last.then_inc(summed.sem, 1)
                with pe.Fori(0, D_STATE) as s:
                    for c in range(DI):
                        pe.wait_ge(weighted.sem, DI + s * DI + c + 2)
                        for half in range(HALVES):
                            last = pe.matmul(bank[:, 2 * c + half, :], k.ident[:],
                                             h[:, c, half * BANK:(half + 1) * BANK], start=False, stop=False,
                                             skip_group_check=True)
                        last.then_inc(summed.sem, 1)
                pe.wait_ge(gated.sem, DI)
                for j in range(TILES):
                    for c in range(DI):
                        last = pe.matmul(bank[:, j, 0:DM], xs[:, c, j * P:(j + 1) * P], w_out[:, c, :],
                                         start=(c == 0), stop=(c == DI - 1))
                    last.then_inc(out_summed.sem, 1)

            @block.sync
            def _(sp):
                sp.wait_ge(low_ready.sem, 4)
                sp.dma_start(bc_dram, bc).then_inc(bc_stored.sem, 16)
                sp.wait_ge(bc_stored.sem, 16)
                with sp.Fori(0, D_STATE // 2) as pair:
                    for r in range(2):
                        row = pair * 2 + r
                        sp.wait_ge(weighted.sem, row * DI + 1)
                        sp.dma_start(b_row[:, r, :], bc_dram[bass.ds(row, 1), :].broadcast_to([P, SEQ])).then_inc(b_loaded[r].sem, 16)
                        sp.dma_start(c_row[:, r, :], bc_dram[bass.ds(row + D_STATE, 1), :].broadcast_to([P, SEQ])).then_inc(c_loaded[r].sem, 16)
            block_ctx.close()
            signal.clear()



CTX = 77
HOPS = 2
MASKED = -3.4028234663852886e38


def memory_stage(k):
    nc, d = k.nc, k.dram
    with ExitStack() as ctx:
        def sb(name, shape, dt=F32):
            return ctx.enter_context(nc.sbuf_tensor(name, shape, dt))

        context = sb("context", [CTX, BATCH, DM])
        contextT = sb("contextT", [P, DK, BATCH, CTX])
        w_hop = sb("w_hop", [P, HOPS, DK, DM])
        w_context = sb("w_context", [P, HOPS, DK, BATCH, CTX])
        mask_in = sb("mask_in", [P, BATCH, CTX], I32)
        keep = sb("keep", [P, BATCH, CTX])
        fill = sb("fill", [P, BATCH, CTX])
        n = NormBuffers(sb, "memory")
        u = sb("u", [P, TILES, DM])
        uT = sb("uT", [P, DK, SEQ])
        logits = sb("logits", [P, TILES, CTX])
        most = sb("most", [P, TILES])
        total = sb("total", [P, TILES])
        scale = sb("scale", [P, TILES])
        weightT = sb("weightT", [CTX, TILES, P])
        bank = ctx.enter_context(nc.psum_tensor("memory_psum", [P, 8, BANK], F32))

        with Prologue(nc) as pre:
            loaded = pre.semaphore("memory_loaded")
            turned = pre.semaphore("memory_turned")
            contextT_ready = pre.semaphore("memory_contextT_ready")
            folded = pre.semaphore("memory_folded")
            kept = pre.semaphore("memory_kept")
            block = pre.block()

            @block.sync
            def _(sp):
                sp.dma_start(context[:], d["ctx_1024"].rearrange("b l d -> l b d")).then_inc(loaded, 16)
                for i, name in enumerate(("L0_xattn_W0", "L0_xattn_W1")):
                    sp.dma_start(w_hop[:, i], d[name].rearrange("(c p) n -> p c n", p=P)).then_inc(loaded, 16)
                mask = d["mask_BxS2_if1"].rearrange("(o b) l -> o (b l)", o=1)
                sp.dma_start(mask_in[:].rearrange("p b l -> p (b l)"),
                             mask.broadcast_to([P, BATCH * CTX])).then_inc(loaded, 16)
                sp.wait_ge(loaded, 64)

            @block.tensor
            def _(pe):
                pe.wait_ge(loaded, 64)
                for b in range(BATCH):
                    for c in range(DK):
                        last = pe.transpose(bank[:, c, b * P:b * P + CTX], context[:, b, c * P:(c + 1) * P],
                                            k.ident[0:CTX, 0:CTX])
                last.then_inc(turned, 1)
                pe.wait_ge(contextT_ready, 1)
                for i in range(HOPS):
                    for m in range(DK):
                        for c in range(DK):
                            last = pe.matmul(bank[:, 2 + i * DK + m, 0:BATCH * CTX],
                                             w_hop[:, i, c, m * P:(m + 1) * P],
                                             contextT[:, c].rearrange("p b l -> p (b l)"),
                                             start=(c == 0), stop=(c == DK - 1))
                last.then_inc(folded, 1)

            @block.vector
            def _(dve):
                dve.wait_ge(loaded, 64)
                dve.tensor_scalar(keep[:], mask_in[:], 0, None, ALU.not_equal).then_inc(kept, 1)
                dve.wait_ge(kept, 1)
                dve.tensor_scalar(fill[:], keep[:], 1.0, -MASKED, ALU.subtract, ALU.mult)
                dve.wait_ge(turned, 1)
                for c in range(DK):
                    last = dve.tensor_copy(contextT[:, c],
                                           bank[:, c, :].rearrange("p (b l) -> p b l", l=P)[:, :, 0:CTX])
                last.then_inc(contextT_ready, 1)
                dve.wait_ge(folded, 1)
                for i in range(HOPS):
                    for m in range(DK):
                        last = dve.tensor_copy(w_context[:, i, m].rearrange("p b l -> p (b l)"),
                                               bank[:, 2 + i * DK + m, 0:BATCH * CTX])
                last.then_inc(kept, 1)
                dve.wait_ge(kept, 2)

        with ExitStack() as run, nc.Fori(0, BATCH) as b:
            signal = BatchSignals(run, nc, "memory_")
            chain = Chain(signal("chain"))
            moments_ready = signal("moments_ready")
            std_ready = signal("std_ready")
            u_ready = signal("u_ready")
            turned = signal("turned")
            uT_ready = signal("uT_ready")
            scored = signal("scored")
            shifted = signal("shifted")
            exp_taken = signal("exp_taken")
            weight_turned = signal("weight_turned")
            weightT_ready = signal("weightT_ready")
            read = signal("read")
            added = signal("added")
            block_ctx = ExitStack()
            block = block_ctx.enter_context(nc.Block())

            @block.vector
            def _(dve):
                norm_on_vector(dve, n, lambda j: k.X[:, b * TILES + j, :], u, chain, std_ready,
                               moments_ready, u_ready)
                for i in range(HOPS):
                    for half in range(HALVES):
                        js = slice(half * 4, half * 4 + 4)
                        psum = bank[:, 4 + half, :].rearrange("p (j l) -> p j l", l=P)[:, :, 0:CTX]
                        dve.wait_ge(scored.sem, i * HALVES + half + 1)
                        chain.link(dve, dve.tensor_tensor(logits[:, js], psum,
                                                          keep[:, bass.ds(b, 1), :].broadcast_to([P, 4, CTX]), ALU.mult))
                        chain.link(dve, dve.tensor_tensor(logits[:, js], logits[:, js],
                                                          fill[:, bass.ds(b, 1), :].broadcast_to([P, 4, CTX]), ALU.add))
                        chain.link(dve, dve.tensor_reduce(most[:, js], logits[:, js], AXIS.X, ALU.max))
                        dve.tensor_tensor(logits[:, js], logits[:, js],
                                          most[:, js].unsqueeze(2).broadcast_to([P, 4, CTX]),
                                          ALU.subtract).then_inc(shifted.sem, 1)
                    for half in range(HALVES):
                        js = slice(half * 4, half * 4 + 4)
                        dve.wait_ge(exp_taken.sem, i * HALVES + half + 1)
                        chain.link(dve, dve.tensor_reduce(total[:, js], logits[:, js], AXIS.X, ALU.add))
                        chain.link(dve, dve.reciprocal(scale[:, js], total[:, js]))
                    for j in range(TILES):
                        dve.wait_ge(read.sem, i * TILES // 2 + j // 2 + 1)
                        dve.scalar_tensor_tensor(out=u[:, j, :], in0=bank[:, j // 2, (j % 2) * DM:(j % 2 + 1) * DM],
                                                 scalar=scale[:, j:j + 1], in1=u[:, j, :], op0=ALU.mult,
                                                 op1=ALU.add).then_inc(u_ready.sem, 1)
                for j in range(TILES):
                    dve.wait_ge(u_ready.sem, HOPS * TILES + j + 1)
                    dve.tensor_tensor(k.X[:, b * TILES + j, :], k.X[:, b * TILES + j, :], u[:, j, :],
                                      ALU.add).then_inc(added.sem, 1)
                dve.wait_ge(added.sem, TILES)

            @block.scalar
            def _(act):
                roots_on_scalar(act, n, moments_ready, std_ready)
                for i in range(HOPS):
                    for q in range(4):
                        act.wait_ge(turned.sem, i * 4 + q + 1)
                        act.copy(columns_of(uT, q), bank[:, q, :]).then_inc(uT_ready.sem, 1)
                    for half in range(HALVES):
                        js = slice(half * 4, half * 4 + 4)
                        act.wait_ge(shifted.sem, i * HALVES + half + 1)
                        act.activation(logits[:, js], logits[:, js], ACT.Exp).then_inc(exp_taken.sem, 1)
                    for half in range(HALVES):
                        act.wait_ge(weight_turned.sem, i * HALVES + half + 1)
                        act.copy(weightT[:, half * 4:half * 4 + 4, :],
                                 bank[0:CTX, 6 + half, :].rearrange("p (j l) -> p j l", l=P)).then_inc(weightT_ready.sem, 1)

            @block.tensor
            def _(pe):
                for i in range(HOPS):
                    transpose_on_tensor(pe, k, u, bank, u_ready, i * TILES, turned)
                    for half in range(HALVES):
                        pe.wait_ge(uT_ready.sem, i * 4 + 2 * half + 2)
                        for j in range(half * 4, half * 4 + 4):
                            for c in range(DK):
                                last = pe.matmul(bank[:, 4 + half, (j % 4) * P:(j % 4) * P + CTX],
                                                 uT[:, c, j * P:(j + 1) * P],
                                                 w_context[:, i, c, bass.ds(b, 1), :].rearrange("p o l -> p (o l)"),
                                                 start=(c == 0), stop=(c == DK - 1))
                        last.then_inc(scored.sem, 1)
                    for half in range(HALVES):
                        pe.wait_ge(exp_taken.sem, i * HALVES + half + 1)
                        for j in range(half * 4, half * 4 + 4):
                            last = pe.transpose(bank[0:CTX, 6 + half, (j % 4) * P:(j % 4 + 1) * P],
                                                logits[:, j, :], k.ident[:])
                        last.then_inc(weight_turned.sem, 1)
                    for half in range(HALVES):
                        pe.wait_ge(weightT_ready.sem, i * HALVES + half + 1)
                        for j in range(half * 4, half * 4 + 4):
                            last = pe.matmul(bank[:, j // 2, (j % 2) * DM:(j % 2 + 1) * DM], weightT[:, j, :],
                                             context[:, bass.ds(b, 1), :].rearrange("p o l -> p (o l)"),
                                             start=True, stop=True)
                            if j % 2:
                                last.then_inc(read.sem, 1)

            block_ctx.close()
            signal.clear()



FF = 1024
HEADS, KEYS, TOP = 4, 64, 8
EXPERTS = 1024
ROWS = EXPERTS // KEYS
KW = 64
SIDES = 2
FC = FF // P
EC = EXPERTS // P


def expert_plan():
    def weights(j, heads):
        return ([("choose", j)] if 0 in heads else []) + [("head", j, h) for h in heads]

    plan = []
    for q in range(FC):
        plan += weights(q // HEADS, [q % HEADS]) + [("piece", q)]
    for j in range(TILES):
        plan += [("turn", j)]
        if j < TILES // 2:
            plan += weights(j + 2, [0]) + [("piece", FC + 2 * j)] + weights(j + 2, range(1, HEADS))
            plan += [("out", j), ("piece", FC + 2 * j + 1)]
        else:
            plan += [("out", j)] + (weights(j + 2, range(HEADS)) if j + 2 < TILES else [])
    return plan


def expert_stage(k):
    nc, d = k.nc, k.dram
    with ExitStack() as ctx:
        def sb(name, shape, dt=F32):
            return ctx.enter_context(nc.sbuf_tensor(name, shape, dt))

        w_sim = sb("w_sim", [P, DK, SIDES * HEADS * KEYS])
        downT = sb("downT", [P, DK, EXPERTS])
        up = sb("up", [P, EC, DM])
        w_g = sb("w_g", [P, DK, FF])
        w_u = sb("w_u", [P, DK, FF])
        w_d = sb("w_d", [P, FC, DM])
        b_g = sb("b_g", [P, FC])
        b_u = sb("b_u", [P, FC])
        b_d = sb("b_d", [1, DM])
        n = NormBuffers(sb, "expert")
        y = sb("y", [P, TILES, DM])
        yT = sb("yT", [P, DK, SEQ])
        sims = sb("sims", [P, TILES, SIDES * HEADS * KEYS])
        hitT = sb("hitT", [P, EC, SEQ])
        innerT = sb("innerT", [P, FC, SEQ])
        gate = sb("ffn_gate", [P, BANK])
        best = sb("best", [P, SIDES, HEADS, TOP])
        pairs = sb("pairs", [P, HEADS, TOP, TOP])
        score = sb("score", [P, HEADS, TOP])
        escore = sb("escore", [P, HEADS, TOP])
        neg_most = sb("neg_most", [P, 2, HEADS])
        total = sb("expert_total", [P, HEADS])
        inv_total = sb("inv_total", [P, HEADS])
        given = sb("given", [P, 2])
        table = sb("table", [P, 2, ROWS, KEYS])
        picked = sb("picked", [P, 2, ROWS, KEYS])
        weight = sb("weight", [P, 2, EXPERTS])
        mixedT = y[:].rearrange("p (r e) t -> p r (e t)", r=2)
        bank = ctx.enter_context(nc.psum_tensor("expert_psum", [P, 8, BANK], F32))

        with Prologue(nc) as pre:
            loaded = pre.semaphore("expert_loaded")
            folded = pre.semaphore("expert_folded")
            kept = pre.semaphore("expert_kept")
            w_q = hitT[0:KW, 0:2, :].rearrange("p a (s d) -> p (a s) d", d=DM)
            keys = hitT[0:KW, 2, 0:SIDES * HEADS * KEYS].rearrange("p (s h e) -> p s h e", s=SIDES, h=HEADS)
            block = pre.block()
            loads = [
                (w_q[:], d["L0_ffn_Wq"].rearrange("(s n) d -> n s d", n=KW)),
                (keys[:], d["L0_ffn_keys"]),
                (downT[:], d["L0_ffn_down_embed"].rearrange("(c p) n -> p c n", p=P)),
                (up[:], d["L0_ffn_up_embed"].rearrange("(c p) n -> p c n", p=P)),
                (w_g[:], d["L0_ffn_Wg"].rearrange("(c p) n -> p c n", p=P)),
                (w_u[:], d["L0_ffn_Wu"].rearrange("(c p) n -> p c n", p=P)),
                (w_d[:], d["L0_ffn_Wd"].rearrange("(c p) n -> p c n", p=P)),
                (b_g[:], d["L0_ffn_bg"].rearrange("(c p) -> p c", p=P)),
                (b_u[:], d["L0_ffn_bu"].rearrange("(c p) -> p c", p=P)),
                (b_d[:], d["L0_ffn_bd"].rearrange("(o n) -> o n", o=1)),
            ]

            @block.sync
            def _(sp):
                for dst, src in loads:
                    sp.dma_start(dst, src, allow_slow_non_contiguous=True).then_inc(loaded, 16)
                sp.wait_ge(loaded, 16 * len(loads))

            @block.tensor
            def _(pe):
                pe.wait_ge(loaded, 16 * len(loads))
                for m in range(DK):
                    for s in range(SIDES * HEADS):
                        last = pe.matmul(bank[:, m, s * KEYS:(s + 1) * KEYS], w_q[:, s, m * P:(m + 1) * P],
                                         keys[:, s // HEADS, s % HEADS, :], start=True, stop=True)
                last.then_inc(folded, 1)

            @block.vector
            def _(dve):
                dve.wait_ge(folded, 1)
                for m in range(DK):
                    dve.tensor_copy(w_sim[:, m, :], bank[:, m, :]).then_inc(kept, 1)
                dve.wait_ge(kept, DK)

        with ExitStack() as run, nc.Fori(0, BATCH) as b:
            signal = BatchSignals(run, nc, "expert_")
            chain = Chain(signal("chain"))
            moments_ready = signal("moments_ready")
            std_ready = signal("std_ready")
            normed = signal("normed")
            turned = signal("turned")
            yT_ready = signal("yT_ready")
            compared = signal("compared")
            sims_ready = signal("sims_ready")
            hit = signal("hit")
            hitT_ready = signal("hitT_ready")
            gate_done = signal("gate_done")
            up_done = signal("up_done")
            gate_ready = signal("gate_ready")
            innerT_ready = signal("innerT_ready")
            most_ready = signal("most_ready")
            score_shifted = signal("score_shifted")
            escore_ready = signal("escore_ready")
            table_ready = signal("table_ready")
            exp_ready = signal("exp_ready")
            picked_ready = signal("picked_ready")
            head_added = signal("head_added")
            weight_ready = signal("weight_ready")
            weight_turned = signal("weight_turned")
            mixed = signal("mixed")
            out_summed = signal("out_summed")
            added = signal("added")
            block_ctx = ExitStack()
            block = block_ctx.enter_context(nc.Block())

            @block.vector
            def _(dve):
                norm_on_vector(dve, n, lambda j: k.X[:, b * TILES + j, :], y, chain, std_ready,
                               moments_ready, normed)

                def gate_up(q):
                    half, m = divmod(q, FC)
                    dve.wait_ge(up_done.sem, q + 1)
                    dve.wait_ge(gate_ready.sem, q + 1)
                    dve.scalar_tensor_tensor(out=innerT[:, m, half * BANK:(half + 1) * BANK], in0=bank[:, 7, :],
                                             scalar=b_u[:, m:m + 1], in1=gate[:], op0=ALU.add,
                                             op1=ALU.mult).then_inc(innerT_ready.sem, 1)

                def choose(j):
                    dve.wait_ge(sims_ready.sem, j + 1)
                    sim = sims[:, j, :].rearrange("p (s h e) -> p s h e", s=SIDES, h=HEADS)
                    for s in range(SIDES):
                        for h in range(HEADS):
                            last = dve.max(best[:, s, h, :], sim[:, s, h, :])
                    chain.link(dve, last)
                    chain.link(dve, dve.tensor_tensor(
                        pairs[:], best[:, 0].unsqueeze(3).broadcast_to([P, HEADS, TOP, TOP]),
                        best[:, 1].unsqueeze(2).broadcast_to([P, HEADS, TOP, TOP]), ALU.add))
                    if j >= 1:
                        dve.wait_ge(escore_ready.sem, j)
                    for h in range(HEADS):
                        last = dve.max(score[:, h, :], pairs[:, h].rearrange("p a b -> p (a b)"))
                    chain.link(dve, last)
                    if j >= 2:
                        dve.wait_ge(exp_ready.sem, HEADS * (j - 1))
                    dve.tensor_scalar(neg_most[:, j % 2, :], score[:, :, 0], -1.0, None,
                                      ALU.mult).then_inc(most_ready.sem, 1)
                    dve.tensor_tensor(escore[:], score[:], score[:, :, 0:1].broadcast_to([P, HEADS, TOP]),
                                      ALU.subtract).then_inc(score_shifted.sem, 1)

                def weigh(j, h):
                    t = j * HEADS + h
                    if h == 0:
                        dve.wait_ge(escore_ready.sem, j + 1)
                        chain.link(dve, dve.tensor_reduce(total[:], escore[:], AXIS.X, ALU.add))
                        chain.link(dve, dve.reciprocal(inv_total[:], total[:]))
                        if j >= 2:
                            dve.wait_ge(weight_turned.sem, j - 1)
                    w = weight[:, j % 2, :]
                    e = picked[:, t % 2].rearrange("p r e -> p (r e)")
                    dve.wait_ge(exp_ready.sem, t + 1)
                    dve.scalar_tensor_tensor(out=e, in0=table[:, t % 2].rearrange("p r e -> p (r e)"),
                                             scalar=score[:, h, TOP - 1:TOP], in1=e, op0=ALU.is_ge,
                                             op1=ALU.mult).then_inc(picked_ready.sem, 1)
                    dve.wait_ge(picked_ready.sem, t + 1)
                    if h == 0:
                        last = dve.tensor_scalar(w, e, inv_total[:, 0:1], None, ALU.mult)
                    elif h < HEADS - 1:
                        last = dve.scalar_tensor_tensor(out=w, in0=e, scalar=inv_total[:, h:h + 1], in1=w,
                                                        op0=ALU.mult, op1=ALU.add)
                    else:
                        last = dve.scalar_tensor_tensor(out=w, in0=e, scalar=inv_total[:, h:h + 1], in1=w,
                                                        op0=ALU.mult, op1=ALU.add, accum_out=given[:, 0:1])
                    last.then_inc(head_added.sem, 1)
                    dve.wait_ge(head_added.sem, t + 1)
                    if h == HEADS - 1:
                        chain.link(dve, dve.tensor_scalar(given[:, 1:2], given[:, 0:1], -1.0, float(HEADS),
                                                          ALU.mult, ALU.add))
                        dve.tensor_tensor(w[:, EXPERTS - 1:], w[:, EXPERTS - 1:], given[:, 1:2],
                                          ALU.add).then_inc(weight_ready.sem, 1)

                def mix(j):
                    dve.wait_ge(weight_turned.sem, j + 1)
                    dve.wait_ge(hitT_ready.sem, FC * (1 + j // 4))
                    if j >= 2:
                        dve.wait_ge(out_summed.sem, j - 1)
                    dve.tensor_tensor(mixedT[:, j % 2].rearrange("p (e t) -> p e t", t=P),
                                      bank[:, 2:4, :].rearrange("p a (e t) -> p (a e) t", t=P),
                                      hitT[:, :, j * P:(j + 1) * P], ALU.mult).then_inc(mixed.sem, 1)

                def add_out(j):
                    dve.wait_ge(out_summed.sem, j + 1)
                    dve.tensor_tensor(k.X[:, b * TILES + j, :], k.X[:, b * TILES + j, :], bank[:, j % 2, 0:DM],
                                      ALU.add).then_inc(added.sem, 1)

                for what, *at in expert_plan():
                    if what == "choose":
                        choose(*at)
                    elif what == "head":
                        weigh(*at)
                    elif what == "piece":
                        gate_up(*at)
                    elif what == "turn":
                        mix(*at)
                        if at[0] >= 1:
                            add_out(at[0] - 1)
                add_out(TILES - 1)
                dve.wait_ge(added.sem, TILES)

            @block.gpsimd
            def _(pool):
                for j in range(TILES):
                    pool.wait_ge(sims_ready.sem, j + 1)
                    sim = sims[:, j, :].rearrange("p (s h e) -> p s h e", s=SIDES, h=HEADS)
                    for h in range(HEADS):
                        t = j * HEADS + h
                        if t >= 2:
                            pool.wait_ge(picked_ready.sem, t - 1)
                        pool.tensor_tensor(table[:, t % 2], sim[:, 0, h, 0:ROWS].unsqueeze(2).broadcast_to([P, ROWS, KEYS]),
                                           sim[:, 1, h:h + 1, :].broadcast_to([P, ROWS, KEYS]),
                                           ALU.add).then_inc(table_ready.sem, 1)

            @block.scalar
            def _(act):
                roots_on_scalar(act, n, moments_ready, std_ready)
                for q in range(4):
                    act.wait_ge(turned.sem, q + 1)
                    act.copy(columns_of(yT, q), bank[:, q, :]).then_inc(yT_ready.sem, 1)
                for j in range(TILES):
                    act.wait_ge(compared.sem, j + 1)
                    act.copy(sims[:, j, :], bank[:, 4 + j % 4, :]).then_inc(sims_ready.sem, 1)
                for what, *at in expert_plan():
                    if what == "piece":
                        q = at[0]
                        half, m = divmod(q, FC)
                        act.wait_ge(hit.sem, q + 1)
                        act.activation(hitT[:, m, half * BANK:(half + 1) * BANK], bank[:, 4 + q % 2, :],
                                       ACT.Silu).then_inc(hitT_ready.sem, 1)
                        act.wait_ge(gate_done.sem, q + 1)
                        if q >= 1:
                            act.wait_ge(innerT_ready.sem, q)
                        act.activation(gate[:], bank[:, 6, :], ACT.Silu, bias=b_g[:, m:m + 1]).then_inc(gate_ready.sem, 1)
                    elif what == "choose":
                        j = at[0]
                        act.wait_ge(score_shifted.sem, j + 1)
                        act.activation(escore[:], escore[:], ACT.Exp).then_inc(escore_ready.sem, 1)
                    elif what == "head":
                        j, h = at
                        t = j * HEADS + h
                        act.wait_ge(most_ready.sem, j + 1)
                        act.wait_ge(table_ready.sem, t + 1)
                        if t >= 2:
                            act.wait_ge(head_added.sem, t - 1)
                        act.activation(picked[:, t % 2], table[:, t % 2], ACT.Exp,
                                       bias=neg_most[:, j % 2, h:h + 1]).then_inc(exp_ready.sem, 1)

            @block.tensor
            def _(pe):
                transpose_on_tensor(pe, k, y, bank, normed, 0, turned)
                for j in range(TILES):
                    pe.wait_ge(yT_ready.sem, 2 if j < 4 else 4)
                    if j >= 4:
                        pe.wait_ge(sims_ready.sem, j - 3)
                    for c in range(DK):
                        last = pe.matmul(bank[:, 4 + j % 4, :], yT[:, c, j * P:(j + 1) * P], w_sim[:, c, :],
                                         start=(c == 0), stop=(c == DK - 1))
                    last.then_inc(compared.sem, 1)
                pe.wait_ge(sims_ready.sem, TILES)

                def piece(q):
                    half, m = divmod(q, FC)
                    cols = slice(half * BANK, (half + 1) * BANK)
                    for w, slot, done, taken, lag in ((downT, 4 + q % 2, hit, hitT_ready, 2),
                                                      (w_g, 6, gate_done, gate_ready, 1),
                                                      (w_u, 7, up_done, innerT_ready, 1)):
                        if q >= lag:
                            pe.wait_ge(taken.sem, q - lag + 1)
                        for c in range(DK):
                            last = pe.matmul(bank[:, slot, :], w[:, c, m * P:(m + 1) * P], yT[:, c, cols],
                                             start=(c == 0), stop=(c == DK - 1))
                        last.then_inc(done.sem, 1)

                def turn(j):
                    pe.wait_ge(weight_ready.sem, j + 1)
                    if j >= 1:
                        pe.wait_ge(mixed.sem, j)
                    for e in range(EC):
                        last = pe.transpose(bank[:, 2 + e // 4, (e % 4) * P:(e % 4 + 1) * P],
                                            weight[:, j % 2, e * P:(e + 1) * P], k.ident[:])
                    last.then_inc(weight_turned.sem, 1)

                def out_of(j):
                    out = bank[:, j % 2, 0:DM]
                    if j >= 2:
                        pe.wait_ge(added.sem, j - 1)
                    pe.matmul(out, k.ones[0:1, :], b_d[:], start=True, stop=False)
                    pe.wait_ge(innerT_ready.sem, FC * (1 + j // 4))
                    for c in range(FC):
                        pe.matmul(out, innerT[:, c, j * P:(j + 1) * P], w_d[:, c, :], start=False, stop=False)
                    pe.wait_ge(mixed.sem, j + 1)
                    for c in range(EC):
                        last = pe.matmul(out, mixedT[:, j % 2, c * P:(c + 1) * P], up[:, c, :], start=False,
                                         stop=(c == EC - 1))
                    last.then_inc(out_summed.sem, 1)

                for what, *at in expert_plan():
                    if what == "piece":
                        piece(*at)
                    elif what == "turn":
                        turn(*at)
                    elif what == "out":
                        out_of(*at)

            block_ctx.close()
            signal.clear()



FILTER = 4
LOW1, LOW2 = SEQ // 2, SEQ // 4
HEAD_W = 16
ATTN_EPS = 1e-6


def wavelet_stage(k):
    nc, d = k.nc, k.dram
    with ExitStack() as ctx:
        def sb(name, shape, dt=F32):
            return ctx.enter_context(nc.sbuf_tensor(name, shape, dt))

        filters = sb("filters", [P, 4, DK, FILTER])
        even = sb("even", [P, 2, DK, 3])
        odd = sb("odd", [P, 2, DK, 2])
        gamma = sb("gamma", [P, DM])
        beta = sb("beta", [P, DM])
        heads = sb("heads", [P, P])
        n = NormBuffers(sb, "wavelet")
        n2 = NormBuffers(sb, "wavelet2")
        y = sb("wavelet_y", [P, TILES, DM])
        yT = sb("wavelet_yT", [P, DK, SEQ + 3])
        low1 = sb("low1", [P, DK, LOW1 + 3])
        high1 = sb("high1", [P, DK, LOW1 + 2])
        low2 = sb("low2", [P, DK, LOW2])
        high2 = sb("high2", [P, DK, LOW2 + 2])
        below = sb("below", [P, DK, LOW2])
        qT = sb("qT", [P, DK, LOW2])
        v_tokens = sb("v_tokens", [P, 2, DM])
        k_tokens = sb("k_tokens", [P, 2, DM])
        kv = sb("kv", [P, DK, P])
        z_column = sb("z_column", [P, DK])
        z_heads = sb("z_heads", [P, DK, P])
        den = sb("den", [P, DK, LOW2])
        attended = sb("attended", [P, DK, LOW2 + 2])
        back2 = sb("back2", [P, DK, LOW1 + 2])
        back1 = sb("back1", [P, DK, SEQ])
        bank = ctx.enter_context(nc.psum_tensor("wavelet_psum", [P, 8, BANK], F32))

        with Prologue(nc) as pre:
            loaded = pre.semaphore("wavelet_loaded")
            masked = pre.semaphore("wavelet_masked")
            combined = pre.semaphore("wavelet_combined")
            block = pre.block()

            @block.sync
            def _(sp):
                for i, name in enumerate(("h_filter", "g_filter", "h_synth", "g_synth")):
                    for c in range(DK):
                        sp.dma_start(filters[:, i, c, :], d["L1_attn_" + name][:, c * P:(c + 1) * P].rearrange("f p -> p f"),
                                     allow_slow_non_contiguous=True).then_inc(loaded, 16)
                for dst, name in ((gamma, "norm_gamma"), (beta, "norm_beta")):
                    row = d["L1_attn_" + name].rearrange("(o n) -> o n", o=1)
                    sp.dma_start(dst[:], row.broadcast_to([P, DM])).then_inc(loaded, 16)
                sp.wait_ge(loaded, 160)

            @block.gpsimd
            def _(pool):
                blocks = heads[:].rearrange("p (a r) -> p a r", r=HEAD_W)
                pool.affine_select(out=blocks, in_=k.ones[:].rearrange("p (a r) -> p a r", r=HEAD_W),
                                   compare_op=ALU.is_ge, fill=0.0, base=0, pattern=[[-HEAD_W, P // HEAD_W], [0, HEAD_W]],
                                   channel_multiplier=1).then_inc(masked, 1)
                pool.wait_ge(masked, 1)
                pool.affine_select(out=blocks, in_=blocks, compare_op=ALU.is_ge, fill=0.0, base=HEAD_W - 1,
                                   pattern=[[HEAD_W, P // HEAD_W], [0, HEAD_W]],
                                   channel_multiplier=-1).then_inc(masked, 1)
                pool.wait_ge(masked, 2)

            @block.vector
            def _(dve):
                dve.wait_ge(loaded, 160)
                f = filters[:, 2:4]
                dve.tensor_copy(even[:, :, :, 0:1], f[:, :, :, 0:1])
                dve.tensor_tensor(even[:, :, :, 1:2], f[:, :, :, 1:2], f[:, :, :, 2:3], ALU.add)
                dve.tensor_copy(even[:, :, :, 2:3], f[:, :, :, 3:4])
                dve.tensor_tensor(odd[:, :, :, 0:1], f[:, :, :, 0:1], f[:, :, :, 1:2], ALU.add)
                dve.tensor_tensor(odd[:, :, :, 1:2], f[:, :, :, 2:3], f[:, :, :, 3:4], ALU.add)
                for t, w in ((yT, SEQ), (low1, LOW1), (high1, LOW1), (high2, LOW2), (attended, LOW2), (back2, LOW1)):
                    for c in range(DK):
                        dve.memset(t[:, c, 0:1], 0.0)
                        last = dve.memset(t[:, c, w + 1:], 0.0)
                last.then_inc(combined, 1)
                dve.wait_ge(combined, 1)

        with ExitStack() as run, nc.Fori(0, BATCH) as b:
            signal = BatchSignals(run, nc, "wavelet_")
            chain = Chain(signal("chain"))
            moments_ready = signal("moments_ready")
            std_ready = signal("std_ready")
            normed = signal("normed")
            turned = signal("turned")
            yT_ready = signal("yT_ready")
            tapped = signal("tapped")
            below_ready = signal("below_ready")
            exp_taken = signal("exp_taken")
            q_ready = signal("q_ready")
            tokens_turned = signal("tokens_turned")
            tokens_ready = signal("tokens_ready")
            kv_done = signal("kv_done")
            kv_ready = signal("kv_ready")
            num_den = signal("num_den")
            back_turned = signal("back_turned")
            moments2_ready = signal("moments2_ready")
            std2_ready = signal("std2_ready")
            normed2 = signal("normed2")
            scaled = signal("scaled")
            shifted = signal("shifted")
            added = signal("added")
            block_ctx = ExitStack()
            block = block_ctx.enter_context(nc.Block())

            @block.vector
            def _(dve):
                norm_on_vector(dve, n, lambda j: k.X[:, b * TILES + j, :], y, chain, std_ready,
                               moments_ready, normed)
                count = [0]

                def filter_all(outputs):
                    last_of = {}
                    for i in range(max(len(taps) for _, _, taps in outputs)):
                        for o, (out, start, taps) in enumerate(outputs):
                            if i >= len(taps):
                                continue
                            tap, source = taps[i]
                            if i:
                                dve.wait_ge(tapped.sem, last_of[o])
                            acc = out if i else start
                            if acc is None:
                                ins = dve.tensor_scalar(out, source, tap, None, ALU.mult)
                            else:
                                ins = dve.scalar_tensor_tensor(out=out, in0=source, scalar=tap, in1=acc,
                                                               op0=ALU.mult, op1=ALU.add)
                            ins.then_inc(tapped.sem, 1)
                            count[0] += 1
                            last_of[o] = count[0]
                    dve.wait_ge(tapped.sem, count[0])

                def analysis(source, low, high, length):
                    filter_all([(out, None, [(filters[:, i, c, t:t + 1], source[:, c, t:t + 2 * length - 1:2])
                                             for t in range(FILTER)])
                                for c in range(DK) for i, out in ((0, low[c]), (1, high[c]))])

                def synthesis(sources, out, start, length):
                    outputs = []
                    for c in range(DK):
                        for parity, taps in ((0, even), (1, odd)):
                            n_taps = 3 - parity
                            outputs.append((out[c][:, parity:2 * length:2],
                                            start[c][:, parity:2 * length:2] if start else None,
                                            [(taps[:, i, c, t:t + 1], sources[i][:, c, t + parity:t + parity + length])
                                             for i in range(2) for t in range(n_taps)]))
                    filter_all(outputs)

                dve.wait_ge(yT_ready.sem, 4)
                analysis(yT, [low1[:, c, 1:1 + LOW1] for c in range(DK)], [high1[:, c, 1:1 + LOW1] for c in range(DK)], LOW1)
                analysis(low1, [low2[:, c, :] for c in range(DK)], [high2[:, c, 1:1 + LOW2] for c in range(DK)], LOW2)
                dve.tensor_scalar(below[:], low2[:], 0.0, None, ALU.min).then_inc(below_ready.sem, 1)
                dve.wait_ge(exp_taken.sem, 1)
                for c in range(DK):
                    dve.scalar_tensor_tensor(out=qT[:, c, :], in0=low2[:, c, :], scalar=0.0, in1=below[:, c, :],
                                             op0=ALU.max, op1=ALU.add).then_inc(q_ready.sem, 1)
                dve.wait_ge(tokens_turned.sem, 2)
                dve.tensor_copy(v_tokens[:].rearrange("p i n -> p (i n)"), bank[:, 4, :]).then_inc(tokens_ready.sem, 1)
                dve.tensor_copy(k_tokens[:].rearrange("p i n -> p (i n)"), bank[:, 5, :]).then_inc(tokens_ready.sem, 1)
                dve.wait_ge(kv_done.sem, 2)
                chain.link(dve, dve.tensor_copy(z_column[:], bank[:, 7, 0:DK]))
                for c in range(DK):
                    dve.tensor_tensor(kv[:, c, :], bank[:, 6, c * P:(c + 1) * P], heads[:], ALU.mult)
                    dve.tensor_scalar(z_heads[:, c, :], heads[:], z_column[:, c:c + 1], None,
                                      ALU.mult).then_inc(kv_ready.sem, 1)
                dve.wait_ge(num_den.sem, 2)
                chain.link(dve, dve.tensor_scalar(den[:].rearrange("p c t -> p (c t)"), bank[:, 5, :], ATTN_EPS, None,
                                                  ALU.add))
                chain.link(dve, dve.reciprocal(den[:], den[:]))
                chain.link(dve, dve.tensor_tensor(attended[:, :, 1:1 + LOW2],
                                                  bank[:, 4, :].rearrange("p (c t) -> p c t", c=DK), den[:], ALU.mult))
                synthesis([attended, high2], [back2[:, c, 1:1 + LOW1] for c in range(DK)], None, LOW2)
                synthesis([back2, high1], [back1[:, c, :] for c in range(DK)],
                          [yT[:, c, 1:1 + SEQ] for c in range(DK)], LOW1)
                dve.wait_ge(back_turned.sem, 4)
                norm_on_vector(dve, n2, lambda j: bank[:, j // 2, (j % 2) * DM:(j % 2 + 1) * DM], y, chain, std2_ready,
                               moments2_ready, normed2)
                for half in range(HALVES):
                    js = bass.ds(b * TILES + half * 4, 4)
                    dve.wait_ge(shifted.sem, half + 1)
                    dve.tensor_tensor(k.X[:, js, :], k.X[:, js, :], y[:, half * 4:half * 4 + 4, :],
                                      ALU.add).then_inc(added.sem, 1)
                dve.wait_ge(added.sem, HALVES)

            @block.gpsimd
            def _(pool):
                for half in range(HALVES):
                    ys = y[:, half * 4:half * 4 + 4, :]
                    pool.wait_ge(normed2.sem, 4 * half + 4)
                    pool.tensor_tensor(ys, ys, gamma[:].unsqueeze(1).broadcast_to([P, 4, DM]),
                                       ALU.mult).then_inc(scaled.sem, 1)
                    pool.wait_ge(scaled.sem, half + 1)
                    pool.tensor_tensor(ys, ys, beta[:].unsqueeze(1).broadcast_to([P, 4, DM]),
                                       ALU.add).then_inc(shifted.sem, 1)

            @block.scalar
            def _(act):
                roots_on_scalar(act, n, moments_ready, std_ready)
                for q in range(4):
                    act.wait_ge(turned.sem, q + 1)
                    act.copy(columns_of(yT, q, pad=1), bank[:, q, :]).then_inc(yT_ready.sem, 1)
                act.wait_ge(below_ready.sem, 1)
                act.activation(below[:], below[:], ACT.Exp).then_inc(exp_taken.sem, 1)
                roots_on_scalar(act, n2, moments2_ready, std2_ready)

            @block.tensor
            def _(pe):
                transpose_on_tensor(pe, k, y, bank, normed, 0, turned)
                for source, slot, wait in ((low2, 4, None), (qT, 5, q_ready)):
                    pe.wait_ge(q_ready.sem, DK)
                    for i in range(2):
                        for c in range(DK):
                            last = pe.transpose(bank[:, slot, (i * DK + c) * P:(i * DK + c + 1) * P],
                                                source[:, c, i * P:(i + 1) * P], k.ident[:])
                    last.then_inc(tokens_turned.sem, 1)
                pe.wait_ge(tokens_ready.sem, 2)
                for c in range(DK):
                    for i in range(2):
                        last = pe.matmul(bank[:, 6, c * P:(c + 1) * P], k_tokens[:, i, c * P:(c + 1) * P],
                                         v_tokens[:, i, c * P:(c + 1) * P], start=(i == 0), stop=(i == 1))
                last.then_inc(kv_done.sem, 1)
                for c in range(DK):
                    for i in range(2):
                        last = pe.matmul(bank[:, 7, c:c + 1], k_tokens[:, i, c * P:(c + 1) * P], k.ones[:, 0:1],
                                         start=(i == 0), stop=(i == 1))
                last.then_inc(kv_done.sem, 1)
                pe.wait_ge(kv_ready.sem, DK)
                for w, slot in ((kv, 4), (z_heads, 5)):
                    for c in range(DK):
                        last = pe.matmul(bank[:, slot, c * LOW2:(c + 1) * LOW2], w[:, c, :], qT[:, c, :],
                                         start=True, stop=True)
                    last.then_inc(num_den.sem, 1)
                pe.wait_ge(tapped.sem, WAVELET_TAPS)
                for j in range(TILES):
                    for c in range(DK):
                        last = pe.transpose(bank[:, j // 2, ((j % 2) * DK + c) * P:((j % 2) * DK + c + 1) * P],
                                            back1[:, c, j * P:(j + 1) * P], k.ident[:])
                    if j % 2:
                        last.then_inc(back_turned.sem, 1)

            block_ctx.close()
            signal.clear()


WAVELET_TAPS = 2 * (2 * DK * FILTER) + 2 * (2 * DK * 5)



A_HEADS, A_W = 16, 64
INNER = A_HEADS * A_W
KEYS_ALL = SEQ + CTX
KT = TILES + 1
PAIRS = A_HEADS // 2
GROUP = 4
TP = 2 * TILES
GP = TP // GROUP
PIECES = 8
V_PIECES_AT = 5
CHUNKS = 2 * GROUP + 1
CTX_CHUNK = 2
QK_STACKED, V_STACKED = 6 * 16, 2 * 16
RING = 2 * GROUP
V_SPLIT = 3
F16 = mybir.dt.float16

BANK7 = [(0, "end", "values", -1), (1, "end", "values_rest", -1),
         (2, "middle", "out", -2), (2, "end", "out", -1), (3, "middle", "piece", 0),
         (4, "middle", "piece", 1), (4, "end", "values", 0), (5, "end", "values_rest", 0),
         (6, "middle", "out", 0), (6, "end", "out", 1), (7, "middle", "piece", 2),
         (8, "middle", "piece", 3), (8, "end", "values", 1), (9, "end", "values_rest", 1),
         (10, "middle", "out", 2), (10, "end", "out", 3), (11, "middle", "piece", 4), (11, "end", "piece", 5),
         (12, "middle", "piece", 6), (12, "end", "values", 2), (13, "end", "values_rest", 2),
         (14, "middle", "out", 4), (14, "end", "out", 5), (15, "middle", "piece", 7)]
BANK7_LAST = [(TP, "end", "values", GP - 1), (TP, "end", "values_rest", GP - 1),
              (TP, "end", "out", TP // 2 - 2), (TP, "end", "out", TP // 2 - 1)]


def chunk_of(t, u):
    g, r = divmod(t, GROUP)
    if t == TP:
        return GP * CHUNKS
    return g * CHUNKS + 2 * r + u + (r > 0)


def counts_for(first_pair, t, u):
    return 2 if first_pair and (t, u) == (0, 1) else 1


def bank7_uses(first_pair, last_pair):
    uses = [u for u in BANK7 if not (first_pair and u[3] < 0) and not (last_pair and u[2] == "piece")]
    return uses + (BANK7_LAST if last_pair else [])


def attention_stage(k):
    nc, d = k.nc, k.dram
    with ExitStack() as ctx:
        def sb(name, shape, dt=F32):
            return ctx.enter_context(nc.sbuf_tensor(name, shape, dt))

        media = sb("media", [CTX, BATCH, DM])
        mediaT = sb("mediaT", [P, DK, BATCH, CTX])
        m_stats = sb("m_stats", [CTX, BATCH, 6])
        m_moments = sb("m_moments", [CTX, BATCH, 2])
        m_std = sb("m_std", [CTX, BATCH])
        m_rstd = sb("m_rstd", [CTX, BATCH])
        m_eps = sb("m_eps", [CTX, 1])
        ln = sb("ln", [P, 4, DK])
        n = NormBuffers(sb, "attention")
        n2 = NormBuffers(sb, "attention2")
        z = sb("attention_z", [P, TILES, DM])
        zT = sb("attention_zT", [P, DK, KEYS_ALL])
        w_q = sb("attention_w_q", [P, DK, P])
        w_k = sb("attention_w_k", [P, DK, P])
        w_v = sb("attention_w_v", [P, DK, P])
        w_o = sb("attention_w_o", [P, 2, DM])
        q_new = sb("q_new", [P, 2, SEQ], BF16)
        k_new = sb("k_new", [P, 2, KEYS_ALL], BF16)
        v_new = sb("v_new", [P, KT, 2, P], BF16)
        q_stack = sb("q_stack", [P, 2, SEQ], BF16)
        k_high = sb("k_high", [P, 2, KEYS_ALL], BF16)
        k_low = sb("k_low", [P, 2, KEYS_ALL], BF16)
        v_cols = sb("v_cols", [P, 2, KT, P], BF16)
        neg_max = sb("neg_max", [P, TP])
        den = sb("attention_den", [P, TP])
        inv_den = sb("inv_den", [P, TP])
        numer = sb("numer", [P, RING, KEYS_ALL])
        nT_high = sb("nT_high", [P, 2, KT, GROUP * P], F16)
        nT_low = sb("nT_low", [P, 2, KT, GROUP * P], F16)
        values = sb("values", [P, 2, GROUP * P])
        bank = ctx.enter_context(nc.psum_tensor("attention_psum", [P, 8, BANK], F32))
        logits_flat = bank[:, 0:5, :].rearrange("p a b -> p (a b)")
        ODD = 3 * BANK - CTX

        def logits(t):
            return logits_flat[:, ODD:ODD + KEYS_ALL] if t % 2 else logits_flat[:, 0:KEYS_ALL]

        def logits_z(t, half):
            return bank[:, (3 if t % 2 else 0) + half, :]

        def logits_ctx(t):
            return bank[:, 2, BANK - CTX:] if t % 2 else bank[:, 2, 0:CTX]

        def z_at(t):
            return CTX if t % 2 else 0

        def ctx_at(t):
            return 0 if t % 2 else SEQ

        with Prologue(nc) as pre:
            loaded = pre.semaphore("attention_loaded")
            m_done = pre.semaphore("media_done")
            m_var = pre.semaphore("media_var")
            m_root = pre.semaphore("media_root")
            m_turned = pre.semaphore("media_turned")
            block = pre.block()

            @block.sync
            def _(sp):
                sp.dma_start(media[:], d["ctx_1024"].rearrange("b l d -> l b d")).then_inc(loaded, 16)
                for i, name in enumerate(("m_g", "m_b", "l_g", "l_b")):
                    sp.dma_start(ln[:, i, :], d["L1_xattn_ln_" + name].rearrange("(c p) -> p c", p=P),
                                 allow_slow_non_contiguous=True).then_inc(loaded, 16)
                sp.wait_ge(loaded, 80)

            @block.vector
            def _(dve):
                dve.memset(m_eps[:], LN_EPS)
                dve.wait_ge(loaded, 80)
                for b in range(BATCH):
                    last = dve.bn_stats(m_stats[:, b, :], media[:, b, :])
                last.then_inc(m_done, 1)
                dve.wait_ge(m_done, 1)
                for b in range(BATCH):
                    last = dve.bn_aggr(m_moments[:, b, :], m_stats[:, b, :])
                last.then_inc(m_var, 1)
                dve.wait_ge(m_root, 1)
                dve.reciprocal(m_rstd[:], m_std[:]).then_inc(m_done, 1)
                dve.wait_ge(m_done, 2)
                for b in range(BATCH):
                    last = dve.tensor_scalar(media[:, b, :], media[:, b, :], m_moments[:, b, 0:1], m_rstd[:, b:b + 1],
                                             ALU.subtract, ALU.mult)
                last.then_inc(m_done, 1)
                dve.wait_ge(m_turned, 1)
                for c in range(DK):
                    last = dve.tensor_scalar(mediaT[:, c], bank[:, c, :].rearrange("p (b l) -> p b l", l=P)[:, :, 0:CTX],
                                             ln[:, 0, c:c + 1], ln[:, 1, c:c + 1], ALU.mult, ALU.add)
                last.then_inc(m_done, 1)
                dve.wait_ge(m_done, 4)

            @block.scalar
            def _(act):
                act.wait_ge(m_var, 1)
                act.activation(m_std[:], m_moments[:, :, 1], ACT.Sqrt, bias=m_eps[:, 0:1]).then_inc(m_root, 1)

            @block.tensor
            def _(pe):
                pe.wait_ge(m_done, 3)
                for b in range(BATCH):
                    for c in range(DK):
                        last = pe.transpose(bank[:, c, b * P:b * P + CTX], media[:, b, c * P:(c + 1) * P],
                                            k.ident[0:CTX, 0:CTX])
                last.then_inc(m_turned, 1)

        with ExitStack() as run, nc.Fori(0, BATCH) as b:
            signal = BatchSignals(run, nc, "attention_")
            chain = Chain(signal("chain"))
            moments_ready = signal("moments_ready")
            std_ready = signal("std_ready")
            normed = signal("normed")
            moments2_ready = signal("moments2_ready")
            std2_ready = signal("std2_ready")
            normed2 = signal("normed2")
            turned = signal("turned")
            zT_ready = signal("zT_ready")
            w_loaded = signal("w_loaded")
            wo_loaded = [signal("wo_loaded_a"), signal("wo_loaded_b")]
            piece_done = signal("piece_done")
            piece_high = signal("piece_high")
            piece_low = signal("piece_low")
            qk_stacked = [signal("qk_stacked_a"), signal("qk_stacked_b")]
            v_stacked = [signal("v_stacked_a"), signal("v_stacked_b")]
            scored = signal("scored")
            maxed = signal("maxed")
            numer_ready = signal("numer_ready")
            n_turned = signal("n_turned")
            n_high = signal("n_high")
            n_low = signal("n_low")
            values_done = signal("values_done")
            values_ready = signal("values_ready")
            den_ready = signal("den_ready")
            out_done = signal("out_done")
            added = signal("added")
            copied = signal("copied")
            block_ctx = ExitStack()
            block = block_ctx.enter_context(nc.Block())

            def numer_part(t, kt):
                if kt == TILES:
                    return numer[:, t % RING, ctx_at(t):ctx_at(t) + CTX]
                return numer[:, t % RING, z_at(t) + kt * P:z_at(t) + (kt + 1) * P]

            def piece_shape(i):
                if i < 2:
                    return "q", i * BANK, BANK
                if i < 5:
                    return "k", (i - 2) * BANK, min(BANK, KEYS_ALL - (i - 2) * BANK)
                return "v", (i - 5) * 4, min(4, KT - (i - 5) * 4)

            def new_v(i, part):
                _, first, count = piece_shape(i)
                rows = CTX if first == TILES else P
                return v_new[0:rows, first:first + count, :, part * A_W:(part + 1) * A_W]

            def piece_psum(i):
                kind, first, count = piece_shape(i)
                if kind != "v":
                    return bank[:, 7, 0:count]
                rows = CTX if first == TILES else P
                return bank[0:rows, 7, 0:count * P].rearrange("p (t a w) -> p t a w", a=2, w=A_W)

            def over_pairs(engine, body):
                body(0, True, False)
                with engine.Fori(1, PAIRS - 1) as pair:
                    body(pair, False, False)
                body(PAIRS - 1, False, True)

            @block.tensor
            def _(pe):
                transpose_on_tensor(pe, k, z, bank, normed2, 0, turned)

                def piece(i):
                    kind, first, count = piece_shape(i)
                    if kind == "v":
                        for s in range(count):
                            kt = first + s
                            rows = CTX if kt == TILES else P
                            for c in range(DK):
                                last = pe.matmul(bank[0:rows, 7, s * P:(s + 1) * P], zT[:, c, kt * P:kt * P + rows],
                                                 w_v[:, c, :], start=(c == 0), stop=(c == DK - 1))
                    else:
                        w = w_q if kind == "q" else w_k
                        for c in range(DK):
                            last = pe.matmul(bank[:, 7, 0:count], w[:, c, :], zT[:, c, first:first + count],
                                             start=(c == 0), stop=(c == DK - 1))
                    last.then_inc(piece_done.sem, 1)

                pe.wait_ge(zT_ready.sem, 4)
                pe.wait_ge(copied.sem, 1)
                pe.wait_ge(w_loaded.sem, 48)
                for i in range(PIECES):
                    if i:
                        pe.wait_ge(piece_low.sem, i)
                    piece(i)

                def score_z(pair, t):
                    a, i = divmod(t % TP, TILES)
                    if i == 0:
                        pe.wait_ge(qk_stacked[a].sem, pair * QK_STACKED + (1 + t // TP) * QK_STACKED)
                    pe.wait_ge(numer_ready.sem, pair * TP + t + 1)
                    for half in range(HALVES):
                        for part, kx in enumerate((k_high, k_low)):
                            pe.matmul(logits_z(t, half), q_stack[:, a, i * P:(i + 1) * P],
                                      kx[:, a, half * BANK:(half + 1) * BANK], start=(part == 0), stop=(part == 1))

                def score_ctx(pair, t):
                    a, i = divmod(t % TP, TILES)
                    pe.wait_ge(numer_ready.sem, pair * TP + t + 2)
                    for part, kx in enumerate((k_high, k_low)):
                        last = pe.matmul(logits_ctx(t), q_stack[:, a, i * P:(i + 1) * P], kx[:, a, SEQ:],
                                         start=(part == 0), stop=(part == 1))
                    last.then_inc(scored.sem, 1)

                score_z(0, 0)
                score_ctx(0, 0)
                score_z(0, 1)

                def body(pair, first, last_pair):
                    uses = bank7_uses(first, last_pair)

                    def free_bank7(at):
                        if at == 0:
                            pe.wait_ge(piece_low.sem, pair * PIECES + PIECES)
                            return
                        _, _, before, m = uses[at - 1]
                        if before == "piece":
                            pe.wait_ge(piece_low.sem, pair * PIECES + PIECES + m + 1)
                        elif before == "out":
                            pe.wait_ge(added.sem, pair * (TP // 2) + m + 2)
                        elif before == "values_rest":
                            pe.wait_ge(values_ready.sem, pair * GP + m + 1)

                    def turn(t, u):
                        chunk = chunk_of(t, u)
                        if u == 0:
                            pe.wait_ge(numer_ready.sem, pair * TP + t + 3)
                        pe.wait_ge(n_low.sem, pair * GP * CHUNKS + chunk + 1)
                        out = bank[:, 5 + chunk % 2, :]
                        for s in range(GROUP):
                            if u == CTX_CHUNK:
                                last = pe.transpose(out[0:CTX, s * P:(s + 1) * P], numer_part(t - GROUP + s, TILES), k.ident[:])
                            else:
                                last = pe.transpose(out[:, s * P:(s + 1) * P], numer_part(t, 4 * u + s), k.ident[:])
                        last.then_inc(n_turned.sem, counts_for(first, t, u))

                    def values_of(g, key_tiles):
                        a = g % GP // (GP // 2)
                        if key_tiles[0] == 0:
                            if g in (0, GP // 2):
                                pe.wait_ge(v_stacked[a].sem, pair * V_STACKED + V_STACKED)
                            pe.wait_ge(n_low.sem, pair * GP * CHUNKS + chunk_of(g * GROUP + GROUP - 1, 1) + 3)
                        else:
                            pe.wait_ge(n_low.sem, pair * GP * CHUNKS + chunk_of((g + 1) * GROUP, CTX_CHUNK) + 3)
                        for kt in key_tiles:
                            rows = CTX if kt == TILES else P
                            for part, nx in enumerate((nT_high, nT_low)):
                                last = pe.matmul(bank[:, 7, :], v_cols[0:rows, a, kt, :], nx[0:rows, g % 2, kt, :],
                                                 start=(kt == 0 and part == 0), stop=(kt == KT - 1 and part == 1))
                        if key_tiles[-1] == TILES:
                            last.then_inc(values_done.sem, 1)

                    def out_of(i):
                        g, r = divmod(i, 2)
                        a = g % GP // (GP // 2)
                        if i in (0, GP):
                            pe.wait_ge(wo_loaded[a].sem, pair * 32 + 32)
                        pe.wait_ge(values_ready.sem, pair * GP + g + 1)
                        for s in range(2):
                            last = pe.matmul(bank[:, 7, s * DM:(s + 1) * DM],
                                             values[:, g % 2, (2 * r + s) * P:(2 * r + s + 1) * P], w_o[:, a, :],
                                             start=True, stop=True)
                        last.then_inc(out_done.sem, 1)

                    def use_bank7(t, slot):
                        for at, (when, where, use, i) in enumerate(uses):
                            if (when, where) != (t, slot):
                                continue
                            free_bank7(at)
                            if use == "piece":
                                if i == 0:
                                    pe.wait_ge(w_loaded.sem, pair * 48 + 96)
                                piece(i)
                            elif use == "values":
                                values_of(i, range(0, V_SPLIT))
                            elif use == "values_rest":
                                values_of(i, range(V_SPLIT, KT))
                            else:
                                out_of(i)

                    ahead = TP if last_pair else TP + 2
                    for t in range(TP):
                        if t + 1 < ahead:
                            score_ctx(pair, t + 1)
                        turn(t, 0)
                        turn(t, 1)
                        use_bank7(t, "middle")
                        if t + 2 < ahead:
                            score_z(pair, t + 2)
                        if t % GROUP == 0 and not (first and t == 0):
                            turn(t, CTX_CHUNK)
                        use_bank7(t, "end")
                    if last_pair:
                        turn(TP, CTX_CHUNK)
                        use_bank7(TP, "end")

                over_pairs(pe, body)

            def split_high(act, i, scale_q):
                kind, first, count = piece_shape(i)
                if kind == "q":
                    act.activation(q_new[:, 0, first:first + count], piece_psum(i), ACT.Copy,
                                   scale=scale_q).then_inc(piece_high.sem, 1)
                elif kind == "k":
                    act.copy(k_new[:, 0, first:first + count], piece_psum(i)).then_inc(piece_high.sem, 1)
                else:
                    act.copy(new_v(i, 0), piece_psum(i)).then_inc(piece_high.sem, 1)

            def split_low(dve, i, scale_q):
                kind, first, count = piece_shape(i)
                if kind == "q":
                    last = dve.scalar_tensor_tensor(out=q_new[:, 1, first:first + count], in0=piece_psum(i), scalar=scale_q,
                                                    in1=q_new[:, 0, first:first + count], op0=ALU.mult, op1=ALU.subtract)
                elif kind == "k":
                    last = dve.tensor_tensor(k_new[:, 1, first:first + count], piece_psum(i),
                                             k_new[:, 0, first:first + count], ALU.subtract)
                else:
                    last = dve.tensor_tensor(new_v(i, 1), piece_psum(i), new_v(i, 0), ALU.subtract)
                last.then_inc(piece_low.sem, 1)

            SCALE = float(A_W) ** -0.5

            @block.scalar
            def _(act):
                roots_on_scalar(act, n, moments_ready, std_ready)
                roots_on_scalar(act, n2, moments2_ready, std2_ready)
                for q in range(4):
                    c = q % DK
                    act.wait_ge(turned.sem, q + 1)
                    act.activation(columns_of(zT, q), bank[:, q, :], ACT.Identity, scale=ln[:, 2, c:c + 1],
                                   bias=ln[:, 3, c:c + 1]).then_inc(zT_ready.sem, 1)
                for i in range(PIECES):
                    act.wait_ge(piece_done.sem, i + 1)
                    split_high(act, i, SCALE)

                def exps(pair, t):
                    act.wait_ge(maxed.sem, pair * TP + t + 1)
                    act.activation(numer[:, t % RING, :], logits(t), ACT.Exp, bias=neg_max[:, t % TP:t % TP + 1],
                                   accum_out=den[:, t % TP:t % TP + 1]).then_inc(numer_ready.sem, 1)

                exps(0, 0)

                def body(pair, first, last_pair):
                    uses = bank7_uses(first, last_pair)

                    def high(t, u):
                        g, r = divmod(t, GROUP)
                        chunk = chunk_of(t, u)
                        act.wait_ge(n_turned.sem, pair * GP * CHUNKS + chunk + 1)
                        if r == 0 and u == 0:
                            act.wait_ge(values_done.sem, pair * GP + g + 1)
                        src = bank[:, 5 + chunk % 2, :].rearrange("p (s q) -> p s q", q=P)
                        if u < 2:
                            dst = nT_high[:, g % 2, 4 * u:4 * u + 4, r * P:(r + 1) * P]
                        else:
                            dst, src = nT_high[0:CTX, (g - 1) % 2, TILES, :], bank[0:CTX, 5 + chunk % 2, :]
                        act.copy(dst, src).then_inc(n_high.sem, counts_for(first, t, u))

                    def use_bank7(t, slot):
                        for when, where, use, i in uses:
                            if (when, where) != (t, slot):
                                continue
                            if use == "piece":
                                act.wait_ge(piece_done.sem, pair * PIECES + PIECES + i + 1)
                                if i == 0:
                                    for done in qk_stacked:
                                        act.wait_ge(done.sem, pair * QK_STACKED + QK_STACKED)
                                if i == V_PIECES_AT:
                                    for done in v_stacked:
                                        act.wait_ge(done.sem, pair * V_STACKED + V_STACKED)
                                split_high(act, i, SCALE)
                            elif use == "values_rest":
                                act.wait_ge(values_done.sem, pair * GP + i + 3)
                                act.copy(values[:, i % 2, :], bank[:, 7, :]).then_inc(values_ready.sem, 1)

                    for t in range(TP):
                        high(t, 0)
                        high(t, 1)
                        if t + 1 < TP or not last_pair:
                            exps(pair, t + 1)
                        use_bank7(t, "middle")
                        if t % GROUP == 0 and not (first and t == 0):
                            high(t, CTX_CHUNK)
                        use_bank7(t, "end")
                    if last_pair:
                        high(TP, CTX_CHUNK)
                        use_bank7(TP, "end")

                over_pairs(act, body)

            @block.vector
            def _(dve):
                dve.sem_inc(numer_ready.sem, 2)
                dve.sem_inc(n_low.sem, 2)
                dve.sem_inc(values_done.sem, 2)
                dve.sem_inc(added.sem, 1)
                dve.tensor_copy(zT[:, :, SEQ:].rearrange("p c (o l) -> p c o l", o=1),
                                mediaT[:, :, bass.ds(b, 1), :]).then_inc(copied.sem, 1)
                norm_on_vector(dve, n, lambda j: k.X[:, b * TILES + j, :], z, chain, std_ready, moments_ready, normed)
                dve.wait_ge(normed.sem, TILES)
                norm_on_vector(dve, n2, lambda j: z[:, j, :], z, chain, std2_ready, moments2_ready, normed2)
                for i in range(PIECES):
                    dve.wait_ge(piece_high.sem, i + 1)
                    split_low(dve, i, SCALE)

                def maximum(pair, t):
                    dve.wait_ge(scored.sem, pair * TP + t + 1)
                    dve.tensor_reduce(neg_max[:, t % TP:t % TP + 1], logits(t), AXIS.X, ALU.max,
                                      negate=True).then_inc(maxed.sem, 1)

                maximum(0, 0)

                def body(pair, first, last_pair):
                    uses = bank7_uses(first, last_pair)

                    def low(t, u):
                        g, r = divmod(t, GROUP)
                        chunk = chunk_of(t, u)
                        dve.wait_ge(n_high.sem, pair * GP * CHUNKS + chunk + 1)
                        src = bank[:, 5 + chunk % 2, :].rearrange("p (s q) -> p s q", q=P)
                        if u < 2:
                            at = (slice(None), g % 2, slice(4 * u, 4 * u + 4), slice(r * P, (r + 1) * P))
                        else:
                            at, src = (slice(0, CTX), (g - 1) % 2, TILES, slice(None)), bank[0:CTX, 5 + chunk % 2, :]
                        dve.tensor_tensor(nT_low[at], src, nT_high[at],
                                          ALU.subtract).then_inc(n_low.sem, counts_for(first, t, u))

                    def add_out(i):
                        g, r = divmod(i, 2)
                        first_tile = g % GP * GROUP
                        cols = slice(first_tile, first_tile + GROUP)
                        if r == 0:
                            dve.reciprocal(inv_den[:, cols], den[:, cols]).then_inc(den_ready.sem, 1)
                        dve.wait_ge(out_done.sem, pair * (TP // 2) + i + 1)
                        dve.wait_ge(den_ready.sem, pair * GP + g + 1)
                        for s in range(2):
                            tile = first_tile + 2 * r + s
                            x = k.X[:, b * TILES + tile % TILES, :]
                            last = dve.scalar_tensor_tensor(out=x, in0=bank[:, 7, s * DM:(s + 1) * DM],
                                                            scalar=inv_den[:, tile:tile + 1], in1=x,
                                                            op0=ALU.mult, op1=ALU.add)
                        last.then_inc(added.sem, 1)

                    def use_bank7(t, slot, kind):
                        for when, where, use, i in uses:
                            if (when, where, use) != (t, slot, kind):
                                continue
                            if use == "piece":
                                dve.wait_ge(piece_high.sem, pair * PIECES + PIECES + i + 1)
                                split_low(dve, i, SCALE)
                            elif use == "out":
                                add_out(i)

                    for t in range(TP):
                        if t + 1 < TP or not last_pair:
                            maximum(pair, t + 1)
                        low(t, 0)
                        use_bank7(t, "middle", "out")
                        low(t, 1)
                        use_bank7(t, "middle", "piece")
                        if t % GROUP == 0 and not (first and t == 0):
                            low(t, CTX_CHUNK)
                        use_bank7(t, "end", "piece")
                        use_bank7(t, "end", "out")
                    if last_pair:
                        low(TP, CTX_CHUNK)
                        use_bank7(TP, "end", "out")

                over_pairs(dve, body)
                dve.wait_ge(added.sem, PAIRS * TP // 2 + 1)

            @block.sync
            def _(sp):
                heads_of = {"q": d["L1_xattn_Wq"], "k": d["L1_xattn_Wkv"][:, 0:INNER], "v": d["L1_xattn_Wkv"][:, INNER:]}
                w_rows = {x: w.rearrange("(c p) n -> p c n", p=P) for x, w in heads_of.items()}

                def load_weights(pair):
                    for dst, x in ((w_q, "q"), (w_k, "k"), (w_v, "v")):
                        sp.dma_start(dst[:], w_rows[x][:, :, bass.ds(pair * P, P)]).then_inc(w_loaded.sem, 16)

                def load_out_weights(pair, a):
                    for half in range(2):
                        sp.dma_start(w_o[half * A_W:(half + 1) * A_W, a, :],
                                     d["L1_xattn_Wout"][bass.ds(pair * P + a * A_W, A_W), :]).then_inc(wo_loaded[a].sem, 16)

                def stack_qk(a):
                    rows = slice(a * A_W, (a + 1) * A_W)
                    upper, lower = slice(0, A_W), slice(A_W, P)
                    for dst, src in ((q_stack[upper, a, :], q_new[rows, 0, :]), (q_stack[lower, a, :], q_new[rows, 1, :]),
                                     (k_high[upper, a, :], k_new[rows, 0, :]), (k_high[lower, a, :], k_new[rows, 0, :]),
                                     (k_low[upper, a, :], k_new[rows, 1, :]), (k_low[lower, a, :], k_new[rows, 1, :])):
                        sp.dma_start(dst, src).then_inc(qk_stacked[a].sem, 16)

                def stack_v(a):
                    sp.dma_start(v_cols[:, a, 0:TILES], v_new[:, 0:TILES, a, :]).then_inc(v_stacked[a].sem, 16)
                    sp.dma_start(v_cols[0:CTX, a, TILES], v_new[0:CTX, TILES, a, :]).then_inc(v_stacked[a].sem, 16)

                load_weights(0)
                load_out_weights(0, 0)
                sp.wait_ge(piece_low.sem, V_PIECES_AT)
                for a in range(2):
                    stack_qk(a)

                def body(pair, first, last_pair):
                    if not last_pair:
                        sp.wait_ge(piece_done.sem, pair * PIECES + PIECES)
                        load_weights(pair + 1)
                    sp.wait_ge(piece_low.sem, pair * PIECES + PIECES)
                    stack_v(0)
                    if not first:
                        sp.wait_ge(values_done.sem, pair * GP + 2)
                    stack_v(1)
                    if not first:
                        sp.wait_ge(added.sem, pair * (TP // 2) + 1)
                    load_out_weights(pair, 1)
                    if not last_pair:
                        sp.wait_ge(piece_low.sem, pair * PIECES + PIECES + V_PIECES_AT)
                        stack_qk(0)
                        sp.wait_ge(added.sem, pair * (TP // 2) + 1 + TP // 4)
                        load_out_weights(pair + 1, 0)
                        sp.wait_ge(scored.sem, pair * TP + TP)
                        stack_qk(1)

                over_pairs(sp, body)

            block_ctx.close()
            signal.clear()



FP8_MAX = 448.0
FP8_LEAST_NORMAL = 2.0 ** -6
EXPONENT_BITS = 0x7F800000
ROUNDER = 1.5 * 2.0 ** 20


def round_to_fp8(dve, v, c, out, chain):
    chain.link(dve, dve.tensor_scalar(c.bitcast(I32), v.bitcast(I32), EXPONENT_BITS, None, ALU.bitwise_and))
    chain.link(dve, dve.tensor_scalar(c, c, FP8_LEAST_NORMAL, ROUNDER, ALU.max, ALU.mult))
    chain.link(dve, dve.scalar_tensor_tensor(out=v, in0=v, scalar=-FP8_MAX, in1=c, op0=ALU.max, op1=ALU.add))
    return dve.tensor_tensor(out, v, c, ALU.subtract)


def quantized_stage(k):
    nc, d = k.nc, k.dram
    with ExitStack() as ctx:
        def sb(name, shape, dt=F32):
            return ctx.enter_context(nc.sbuf_tensor(name, shape, dt))

        n = NormBuffers(sb, "quant")
        y = sb("quant_y", [P, BATCH * TILES, DM])
        w = sb("quant_w", [P, DK * DM])
        w_round = sb("w_round", [P, DK * DM])
        w_fp8 = sb("w_fp8", [P, DK, DM], BF16)
        bias = sb("quant_bias", [P, DM])
        tops = sb("tops", [P, BATCH])
        top = sb("top", [P, 2])
        top_row = sb("top_row", [2, 1])
        top_diag = sb("top_diag", [2, 2])
        scale = sb("quant_scale", [P, 2])
        inverse = sb("inverse", [P, 2])
        inverse_both = sb("inverse_both", [P, 1])
        v = sb("quant_v", [P, 2, 4 * DM])
        c = sb("quant_c", [P, 2, 4 * DM])
        x_fp8 = sb("x_fp8", [P, TILES, DM])
        xT_fp8 = sb("xT_fp8", [P, DK, SEQ], BF16)
        out = sb("quant_out", [P, 2, 2, DM], BF16)
        bank = ctx.enter_context(nc.psum_tensor("quant_psum", [P, 8, BANK], F32))

        with ExitStack() as run, nc.Fori(0, BATCH) as b:
            signal = BatchSignals(run, nc, "quant_norm_")
            chain = Chain(signal("chain"))
            moments_ready = signal("moments_ready")
            std_ready = signal("std_ready")
            normed = signal("normed")
            block_ctx = ExitStack()
            block = block_ctx.enter_context(nc.Block())

            @block.vector
            def _(dve):
                batch = y[:, bass.ds(b * TILES, TILES), :]
                norm_on_vector(dve, n, lambda j: k.X[:, b * TILES + j, :], batch, chain, std_ready,
                               moments_ready, normed)
                dve.wait_ge(normed.sem, TILES)
                chain.link(dve, dve.tensor_reduce(tops[:, bass.ds(b, 1)], batch, AXIS.XY, ALU.max,
                                                  apply_absolute_value=True))

            @block.scalar
            def _(act):
                roots_on_scalar(act, n, moments_ready, std_ready)

            block_ctx.close()
            signal.clear()

        with Prologue(nc) as pre:
            loaded = pre.semaphore("quant_loaded")
            top_ready = pre.semaphore("top_ready")
            top_turned = pre.semaphore("top_turned")
            diag_ready = pre.semaphore("diag_ready")
            top_spread = pre.semaphore("top_spread")
            chain = Chain(pre.counter("quant_scale_chain"))
            block = pre.block()

            @block.sync
            def _(sp):
                sp.dma_start(w[:].rearrange("p (c n) -> p c n", c=DK),
                             d["L1_ffn_weight"].rearrange("(c p) n -> p c n", p=P)).then_inc(loaded, 16)
                row = d["L1_ffn_bias"].rearrange("(o n) -> o n", o=1)
                sp.dma_start(bias[:], row.broadcast_to([P, DM])).then_inc(loaded, 16)
                sp.wait_ge(loaded, 32)

            @block.vector
            def _(dve):
                dve.tensor_reduce(top[:, 0:1], tops[:], AXIS.X, ALU.max)
                dve.wait_ge(loaded, 32)
                dve.tensor_reduce(top[:, 1:2], w[:], AXIS.X, ALU.max,
                                  apply_absolute_value=True).then_inc(top_ready, 1)
                dve.wait_ge(top_turned, 1)
                chain.link(dve, dve.tensor_reduce(top_row[:], bank[0:2, 0, 0:P], AXIS.X, ALU.max))
                dve.tensor_scalar(top_diag[:], k.ident[0:2, 0:2], top_row[:], None, ALU.mult).then_inc(diag_ready, 1)
                dve.wait_ge(top_spread, 1)
                chain.link(dve, dve.tensor_scalar(scale[:], bank[:, 1, 0:2], 1e-12, None, ALU.max))
                chain.link(dve, dve.reciprocal(scale[:], scale[:]))
                chain.link(dve, dve.tensor_scalar(scale[:], scale[:], FP8_MAX, FP8_MAX, ALU.mult, ALU.min))
                chain.link(dve, dve.reciprocal(inverse[:], scale[:]))
                dve.tensor_tensor(inverse_both[:], inverse[:, 0:1], inverse[:, 1:2], ALU.mult)
                chain.link(dve, dve.tensor_scalar(w[:], w[:], scale[:, 1:2], FP8_MAX, ALU.mult, ALU.min))
                chain.link(dve, round_to_fp8(dve, w[:], w_round[:], w_fp8[:].rearrange("p c n -> p (c n)"), chain))

            @block.tensor
            def _(pe):
                pe.wait_ge(top_ready, 1)
                pe.transpose(bank[0:2, 0, 0:P], top[:], k.ident[:]).then_inc(top_turned, 1)
                pe.wait_ge(diag_ready, 1)
                pe.matmul(bank[:, 1, 0:2], k.ones[0:2, :], top_diag[:], start=True, stop=True).then_inc(top_spread, 1)

        with ExitStack() as run, nc.Fori(0, BATCH) as b:
            signal = BatchSignals(run, nc, "quant_")
            chain = Chain(signal("chain"))
            scaled = signal("scaled")
            v_ready = signal("v_ready")
            rounded = signal("rounded")
            turned = signal("turned")
            xT_ready = signal("xT_ready")
            multiplied = signal("multiplied")
            out_ready = signal("out_ready")
            added = signal("added")
            block_ctx = ExitStack()
            block = block_ctx.enter_context(nc.Block())

            @block.gpsimd
            def _(pool):
                for half in range(HALVES):
                    pool.wait_ge(scaled.sem, half + 1)
                    pool.tensor_scalar(v[:, half, :], v[:, half, :], FP8_MAX, None, ALU.min).then_inc(v_ready.sem, 1)

            @block.vector
            def _(dve):
                for half in range(HALVES):
                    dve.wait_ge(v_ready.sem, half + 1)
                    tiles = x_fp8[:, half * 4:half * 4 + 4, :].rearrange("p j n -> p (j n)")
                    round_to_fp8(dve, v[:, half, :], c[:, half, :], tiles, chain).then_inc(rounded.sem, 4)
                for pair in range(TILES // 2):
                    dve.wait_ge(multiplied.sem, pair + 1)
                    for i in range(2):
                        dve.scalar_tensor_tensor(out=out[:, pair % 2, i, :], in0=bank[:, 4 + pair, i * DM:(i + 1) * DM],
                                                 scalar=inverse_both[:], in1=bias[:], op0=ALU.mult,
                                                 op1=ALU.add).then_inc(out_ready.sem, 1)
                    dve.wait_ge(out_ready.sem, 2 * pair + 2)
                    js = bass.ds(b * TILES + pair * 2, 2)
                    chain.link(dve, dve.tensor_tensor(k.X[:, js, :], k.X[:, js, :], out[:, pair % 2], ALU.add))

            @block.scalar
            def _(act):
                for half in range(HALVES):
                    ys = y[:, bass.ds(b * TILES + half * 4, 4), :].rearrange("p j n -> p (j n)")
                    act.mul(v[:, half, :], ys, scale[:, 0:1]).then_inc(scaled.sem, 1)
                for q in range(4):
                    act.wait_ge(turned.sem, q + 1)
                    act.copy(columns_of(xT_fp8, q), bank[:, q, :]).then_inc(xT_ready.sem, 1)

            @block.tensor
            def _(pe):
                transpose_on_tensor(pe, k, x_fp8, bank, rounded, 0, turned)
                for j in range(TILES):
                    pe.wait_ge(xT_ready.sem, DK * (1 + j // 4))
                    for i in range(DK):
                        last = pe.matmul(bank[:, 4 + j // 2, (j % 2) * DM:(j % 2 + 1) * DM],
                                         xT_fp8[:, i, j * P:(j + 1) * P], w_fp8[:, i, :],
                                         start=(i == 0), stop=(i == DK - 1))
                    if j % 2:
                        last.then_inc(multiplied.sem, 1)

            block_ctx.close()
            signal.clear()


def decoder(nc, dram):
    with ExitStack() as ctx:
        k = Kernel(nc, ctx, dram)
        load_residual(k)
        stages = [mamba_stage, memory_stage, expert_stage, wavelet_stage, attention_stage, quantized_stage]
        for stage in stages[:LAST_STAGE]:
            stage(k)
        store_residual(k)



TRANSPOSED = ("L0_attn_W_in", "L0_attn_W_x", "L0_attn_W_dt", "L0_attn_W_out", "L0_ffn_Wq", "L0_ffn_down_embed",
              "L1_ffn_weight")


def kernel(**inputs):
    import numpy as np
    import concourse.bacc as bacc
    from concourse.bass_utils import run_bass_kernel_spmd

    nc = bacc.Bacc("TRN2", target_bir_lowering=False, num_devices=1)
    arrays, dram = {}, {}
    for name, value in inputs.items():
        a = np.asarray(value)
        if name in TRANSPOSED:
            a = a.T
        if name == "L0_ffn_keys":
            a = a.transpose(3, 2, 0, 1)
        a = np.ascontiguousarray(a)
        arrays[f"in_{name}"] = a
        dram[name] = nc.dram_tensor(f"in_{name}", a.shape, mybir.dt.from_np(a.dtype), kind="ExternalInput").ap()
    dram["out"] = nc.dram_tensor("out_x", (BATCH, SEQ, DM), F32, kind="ExternalOutput").ap()
    decoder(nc, dram)
    result = run_bass_kernel_spmd(nc, [arrays], core_ids=[0])
    return result.results[0]["out_x"]
```

```python
from contextlib import ExitStack

import concourse.bass as bass
from concourse import mybir

ALU = mybir.AluOpType
ACT = mybir.ActivationFunctionType
AXIS = mybir.AxisListType
F32 = mybir.dt.float32
BF16 = mybir.dt.bfloat16
I32 = mybir.dt.int32
P = 128
BANK = 512
LN_EPS = 1e-5

BATCH, SEQ, DM = 4, 1024, 256
TILES = SEQ // P
DK = DM // P
HALVES = SEQ // BANK


class Signal:

    def __init__(self, ctx, nc, name):
        self.sem = ctx.enter_context(nc.semaphore(name))


class Chain:

    def __init__(self, steps):
        self.steps, self.count = steps, 0

    def link(self, engine, instruction):
        self.count += 1
        instruction.then_inc(self.steps.sem, 1)
        engine.wait_ge(self.steps.sem, self.count)


class BatchSignals:

    def __init__(self, ctx, nc, prefix):
        self.ctx, self.nc, self.prefix, self.all = ctx, nc, prefix, []

    def __call__(self, name):
        self.all.append(Signal(self.ctx, self.nc, self.prefix + name))
        return self.all[-1]

    def clear(self):
        for signal in self.all:
            self.nc.sync.sem_clear(signal.sem)
        self.nc.all_engine_barrier()


class Prologue(ExitStack):

    def __init__(self, nc):
        super().__init__()
        self.nc, self.semaphores = nc, []

    def semaphore(self, name):
        self.semaphores.append(self.enter_context(self.nc.semaphore(name)))
        return self.semaphores[-1]

    def counter(self, name):
        counter = Signal(self, self.nc, name)
        self.semaphores.append(counter.sem)
        return counter

    def block(self):
        self.callback(self.clear)
        return self.enter_context(self.nc.Block())

    def clear(self):
        for semaphore in self.semaphores:
            self.nc.sync.sem_clear(semaphore)
        self.nc.all_engine_barrier()


class Kernel:

    def __init__(self, nc, ctx, dram):
        self.nc, self.ctx, self.dram = nc, ctx, dram
        self.X = ctx.enter_context(nc.sbuf_tensor("X", [P, BATCH * TILES, DM], F32))
        self.ident = ctx.enter_context(nc.sbuf_tensor("ident", [P, P], F32))
        self.ones = ctx.enter_context(nc.sbuf_tensor("ones", [P, P], F32))


def load_residual(k):
    nc = k.nc
    with Prologue(nc) as pre:
        x_loaded = pre.semaphore("x_loaded")
        ident_filled = pre.semaphore("ident_filled")
        block = pre.block()

        @block.sync
        def _(sp):
            view = k.dram["x"].rearrange("b (j p) d -> b p j d", p=P)
            for b in range(BATCH):
                sp.dma_start(k.X[:, b * TILES:(b + 1) * TILES, :], view[b]).then_inc(x_loaded, 16)
            sp.wait_ge(x_loaded, 16 * BATCH)

        @block.gpsimd
        def _(pool):
            pool.memset(k.ones[:], 1.0).then_inc(ident_filled, 1)
            pool.wait_ge(ident_filled, 1)
            pool.affine_select(out=k.ident[:], in_=k.ones[:], compare_op=ALU.is_equal, fill=0.0,
                               base=0, pattern=[[-1, P]], channel_multiplier=1).then_inc(ident_filled, 1)
            pool.wait_ge(ident_filled, 2)


def store_residual(k):
    nc = k.nc
    with ExitStack() as ctx:
        stored = ctx.enter_context(nc.semaphore("stored"))
        block = ctx.enter_context(nc.Block())

        @block.sync
        def _(sp):
            view = k.dram["out"].rearrange("b (j p) d -> b p j d", p=P)
            for b in range(BATCH):
                sp.dma_start(view[b], k.X[:, b * TILES:(b + 1) * TILES, :]).then_inc(stored, 16)
            sp.wait_ge(stored, 16 * BATCH)



class NormBuffers:
    def __init__(self, sb, name):
        self.stats = sb(f"{name}_stats", [P, TILES, 6], F32)
        self.moments = sb(f"{name}_moments", [P, TILES, 2], F32)
        self.std = sb(f"{name}_std", [P, TILES], F32)
        self.rstd = sb(f"{name}_rstd", [P, TILES], F32)
        self.eps = sb(f"{name}_eps", [P, 1], F32)


def norm_on_vector(dve, n, source, out, chain, std_ready, moments_ready, normed):
    chain.link(dve, dve.memset(n.eps[:], LN_EPS))
    for j in range(TILES):
        last = dve.bn_stats(n.stats[:, j, :], source(j))
    chain.link(dve, last)
    for j in range(TILES):
        last = dve.bn_aggr(n.moments[:, j, :], n.stats[:, j, :])
    last.then_inc(moments_ready.sem, 1)
    dve.wait_ge(std_ready.sem, 1)
    chain.link(dve, dve.reciprocal(n.rstd[:], n.std[:]))
    for j in range(TILES):
        dve.tensor_scalar(out[:, j, :], source(j), n.moments[:, j, 0:1], n.rstd[:, j:j + 1],
                          ALU.subtract, ALU.mult).then_inc(normed.sem, 1)


def roots_on_scalar(act, n, moments_ready, std_ready):
    act.wait_ge(moments_ready.sem, 1)
    act.activation(n.std[:], n.moments[:, :, 1], ACT.Sqrt, bias=n.eps[:, 0:1]).then_inc(std_ready.sem, 1)


def transpose_on_tensor(pe, k, tiles, banks, tiles_ready, ready_at, turned):
    for half in range(HALVES):
        pe.wait_ge(tiles_ready.sem, ready_at + 4 * (half + 1))
        for c in range(DK):
            for i in range(4):
                last = pe.transpose(banks[:, half * DK + c, i * P:(i + 1) * P],
                                    tiles[:, half * 4 + i, c * P:(c + 1) * P], k.ident[:])
            last.then_inc(turned.sem, 1)


def columns_of(turned_tile, q, pad=0):
    half, c = divmod(q, DK)
    return turned_tile[:, c, pad + half * BANK:pad + (half + 1) * BANK]



D_INNER, D_STATE, D_CONV, DT_RANK = 512, 16, 4, 64
DI = D_INNER // P


def mamba_stage(k):
    nc, d = k.nc, k.dram
    with ExitStack() as ctx:
        def sb(name, shape, dt=F32):
            return ctx.enter_context(nc.sbuf_tensor(name, shape, dt))

        w_in = sb("w_in", [P, DK, 2 * D_INNER])
        w_x = sb("w_x", [P, DI, DT_RANK + 2 * D_STATE])
        w_dt = sb("w_dt", [DT_RANK, D_INNER])
        w_out = sb("w_out", [P, DI, DM])
        conv_w = sb("conv_w", [P, DI, D_CONV])
        conv_b = sb("conv_b", [P, DI])
        b_dt = sb("b_dt", [P, DI])
        skip = sb("skip", [P, DI])
        a_neg = sb("a_neg", [P, D_STATE, DI])
        skip_diag = sb("skip_diag", [P, DI, P])
        n = NormBuffers(sb, "mamba")
        xs = sb("xs", [P, DI, SEQ])
        gate = sb("gate", [P, DI, SEQ])
        delta = sb("delta", [P, DI, SEQ])
        du = sb("du", [P, DI, SEQ])
        decay = sb("decay", [P, DI, SEQ])
        drive = sb("drive", [P, DI, SEQ])
        h = sb("h", [P, DI, SEQ])
        b_row = sb("b_row", [P, 2, SEQ])
        c_row = sb("c_row", [P, 2, SEQ])
        z = h[:, 0:2, :].rearrange("p a (b d) -> p (a b) d", d=DM)
        zT = h[:, 2:4, :]
        xc = decay
        dt_low = drive[0:DT_RANK, 0, :]
        bc = drive[DT_RANK:DT_RANK + 2 * D_STATE, 1, :]
        convolved_x = du
        soft = decay
        bank = ctx.enter_context(nc.psum_tensor("mamba_psum", [P, 8, BANK], F32))
        bc_dram = nc.dram_tensor("bc_scratch", [2 * D_STATE, SEQ], F32, kind="Internal").ap()

        with Prologue(nc) as pre:
            loaded = pre.semaphore("mamba_loaded")
            a_ready = pre.semaphore("mamba_a_ready")
            diag_ready = pre.semaphore("mamba_diag_ready")
            block = pre.block()

            @block.sync
            def _(sp):
                loads = [
                    (w_in[:], d["L0_attn_W_in"].rearrange("(c p) n -> p c n", p=P)),
                    (w_x[:], d["L0_attn_W_x"].rearrange("(c p) n -> p c n", p=P)),
                    (w_dt[:], d["L0_attn_W_dt"]),
                    (w_out[:], d["L0_attn_W_out"].rearrange("(c p) n -> p c n", p=P)),
                    (conv_w[:], d["L0_attn_conv_w"].rearrange("(c p) o n -> p c (o n)", p=P)),
                    (conv_b[:], d["L0_attn_conv_b"].rearrange("(c p) -> p c", p=P)),
                    (b_dt[:], d["L0_attn_b_dt"].rearrange("(c p) -> p c", p=P)),
                    (skip[:], d["L0_attn_D"].rearrange("(c p) -> p c", p=P)),
                    (a_neg[:], d["L0_attn_A_raw"].rearrange("n (c p) -> p n c", p=P)),
                ]
                for dst, src in loads:
                    sp.dma_start(dst, src, allow_slow_non_contiguous=True).then_inc(loaded, 16)
                sp.wait_ge(loaded, 16 * len(loads))

            @block.scalar
            def _(act):
                act.wait_ge(loaded, 16 * 9)
                act.activation(a_neg[:], a_neg[:], ACT.Exp).then_inc(a_ready, 1)

            @block.vector
            def _(dve):
                dve.wait_ge(a_ready, 1)
                dve.tensor_scalar(a_neg[:], a_neg[:], -1.0, None, ALU.mult)
                for c in range(DI):
                    last = dve.tensor_scalar(skip_diag[:, c, :], k.ident[:], skip[:, c:c + 1], None, ALU.mult)
                last.then_inc(diag_ready, 1)
                dve.wait_ge(diag_ready, 1)

        with ExitStack() as run, nc.Fori(0, BATCH) as b:
            signal = BatchSignals(run, nc, "mamba_")
            chain = Chain(signal("chain"))
            moments_ready = signal("moments_ready")
            std_ready = signal("std_ready")
            normed = signal("normed")
            turned = signal("turned")
            zT_ready = signal("zT_ready")
            projected = signal("projected")
            taken = signal("taken")
            convolved = signal("convolved")
            xs_ready = signal("xs_ready")
            gate_projected = signal("gate_projected")
            gate_taken = signal("gate_taken")
            gate_ready = signal("gate_ready")
            low_ranked = signal("low_ranked")
            low_ready = signal("low_ready")
            bc_stored = signal("bc_stored")
            raised = signal("raised")
            delta_biased = signal("delta_biased")
            clamped = signal("clamped")
            exp_taken = signal("exp_taken")
            log_taken = signal("log_taken")
            delta_ready = signal("delta_ready")
            du_ready = signal("du_ready")
            b_loaded = [signal(f"b_loaded{r}") for r in range(2)]
            c_loaded = [signal(f"c_loaded{r}") for r in range(2)]
            steps = D_STATE * DI
            decay_ready = signal("decay_ready")
            drive_ready = signal("drive_ready")
            scanned = signal("scanned")
            weighted = signal("weighted")
            summed = signal("summed")
            gated = signal("gated")
            out_summed = signal("out_summed")
            added = signal("added")
            block_ctx = ExitStack()
            block = block_ctx.enter_context(nc.Block())

            @block.vector
            def _(dve):
                dve.sem_inc(scanned.sem, DI)
                dve.sem_inc(weighted.sem, DI + 1)
                norm_on_vector(dve, n, lambda j: k.X[:, b * TILES + j, :], z, chain, std_ready,
                               moments_ready, normed)
                for c in range(DI):
                    dve.wait_ge(taken.sem, 2 * c + 2)
                    y = convolved_x[:, c, :]
                    for t in (3, 2, 1, 0):
                        back = D_CONV - 1 - t
                        w = conv_w[:, c, t:t + 1]
                        if back == 0:
                            last = dve.tensor_scalar(y, xc[:, c, :], w, None, ALU.mult)
                        else:
                            last = dve.scalar_tensor_tensor(out=y[:, back:], in0=xc[:, c, 0:SEQ - back], scalar=w,
                                                            in1=y[:, back:], op0=ALU.mult, op1=ALU.add)
                        if t:
                            chain.link(dve, last)
                    last.then_inc(convolved.sem, 1)
                for half in range(HALVES):
                    dve.wait_ge(low_ranked.sem, half + 1)
                    cols = slice(half * BANK, (half + 1) * BANK)
                    dve.tensor_copy(dt_low[:, cols], bank[0:DT_RANK, half, :]).then_inc(low_ready.sem, 1)
                    dve.tensor_copy(bc[:, cols], bank[DT_RANK:DT_RANK + 2 * D_STATE, half, :]).then_inc(low_ready.sem, 1)
                for r in range(8):
                    c, half = divmod(r, HALVES)
                    dve.wait_ge(raised.sem, r + 1)
                    cols = slice(half * BANK, (half + 1) * BANK)
                    dve.tensor_scalar(soft[:, c, cols], bank[:, 2 + r % 4, :], b_dt[:, c:c + 1], 80.0,
                                      ALU.add, ALU.min).then_inc(clamped.sem, 1)
                    dve.tensor_scalar(delta[:, c, cols], bank[:, 2 + r % 4, :], b_dt[:, c:c + 1], None,
                                      ALU.add).then_inc(delta_biased.sem, 1)
                for c in range(DI):
                    dve.wait_ge(log_taken.sem, c + 1)
                    dve.tensor_tensor(delta[:, c, :], delta[:, c, :], soft[:, c, :],
                                      ALU.max).then_inc(delta_ready.sem, 1)
                    dve.wait_ge(delta_ready.sem, c + 1)
                    dve.tensor_tensor(du[:, c, :], delta[:, c, :], xs[:, c, :], ALU.mult).then_inc(du_ready.sem, 1)

                def scan(s, c):
                    dve.wait_ge(decay_ready.sem, s * DI + c + 1)
                    dve.wait_ge(drive_ready.sem, s * DI + c + 1)
                    dve.tensor_tensor_scan(h[:, c, :], decay[:, c, :], drive[:, c, :], 0.0,
                                           ALU.mult, ALU.add).then_inc(scanned.sem, 1)

                def weigh(s, c, r):
                    dve.wait_ge(scanned.sem, DI + s * DI + c + 1)
                    dve.tensor_tensor(h[:, c, :], h[:, c, :], c_row[:, r, :], ALU.mult).then_inc(weighted.sem, 1)

                dve.wait_ge(gate_projected.sem, 8)
                with dve.Fori(0, D_STATE // 2) as pair:
                    for r in range(2):
                        s = pair * 2 + r
                        dve.wait_ge(c_loaded[r].sem, pair * 16 + 16)
                        for c in range(DI + 1):
                            if c < DI:
                                dve.wait_ge(summed.sem, s * DI + c + 1)
                                scan(s, c)
                            if c >= 1:
                                weigh(s, c - 1, r)
                for c in range(DI):
                    dve.wait_ge(summed.sem, steps + c + 1)
                    if c >= DI // 2:
                        dve.wait_ge(gate_ready.sem, c - DI // 2 + 1)
                    dve.tensor_tensor(xs[:, c, :], bank[:, 2 * c:2 * c + 2, :].rearrange("p a b -> p (a b)"),
                                      gate[:, c, :], ALU.mult).then_inc(gated.sem, 1)
                for j in range(TILES):
                    dve.wait_ge(out_summed.sem, j + 1)
                    dve.tensor_tensor(k.X[:, b * TILES + j, :], k.X[:, b * TILES + j, :], bank[:, j, 0:DM],
                                      ALU.add).then_inc(added.sem, 1)
                dve.wait_ge(added.sem, TILES)

            @block.scalar
            def _(act):
                roots_on_scalar(act, n, moments_ready, std_ready)
                for q in range(4):
                    act.wait_ge(turned.sem, q + 1)
                    act.copy(columns_of(zT, q), bank[:, q, :]).then_inc(zT_ready.sem, 1)
                for q in range(8):
                    c, half = divmod(q, HALVES)
                    act.wait_ge(projected.sem, q + 1)
                    act.copy(xc[:, c, half * BANK:(half + 1) * BANK], bank[:, 4 + q % 4, :]).then_inc(taken.sem, 1)
                def take_gate(q, function):
                    c, half = divmod(q, HALVES)
                    act.wait_ge(gate_projected.sem, q + 1)
                    act.activation(gate[:, c, half * BANK:(half + 1) * BANK], bank[:, 6 + q % 2, :],
                                   function).then_inc(gate_taken.sem, 1)

                for c in range(DI):
                    act.wait_ge(convolved.sem, c + 1)
                    act.activation(xs[:, c, :], convolved_x[:, c, :], ACT.Silu, bias=conv_b[:, c:c + 1]).then_inc(xs_ready.sem, 1)
                    take_gate(c, ACT.Silu)
                for c in range(DI):
                    take_gate(DI + c, ACT.Copy)
                    act.wait_ge(clamped.sem, 2 * c + 2)
                    act.activation(soft[:, c, :], soft[:, c, :], ACT.Exp).then_inc(exp_taken.sem, 1)
                for c in range(DI):
                    act.wait_ge(exp_taken.sem, c + 1)
                    act.activation(soft[:, c, :], soft[:, c, :], ACT.Ln, bias=1.0).then_inc(log_taken.sem, 1)
                for c in range(DI):
                    act.wait_ge(delta_ready.sem, c + 1)
                with act.Fori(0, D_STATE) as s:
                    for c in range(DI):
                        act.wait_ge(scanned.sem, s * DI + c + 1)
                        act.activation(decay[:, c, :], delta[:, c, :], ACT.Exp,
                                       scale=a_neg[:, s, c:c + 1]).then_inc(decay_ready.sem, 1)
                act.wait_ge(gate_taken.sem, 8)
                for c in range(DI // 2, DI):
                    act.activation(gate[:, c, :], gate[:, c, :], ACT.Silu).then_inc(gate_ready.sem, 1)

            @block.gpsimd
            def _(pool):
                for c in range(DI):
                    pool.wait_ge(du_ready.sem, c + 1)
                with pool.Fori(0, D_STATE // 2) as pair:
                    for r in range(2):
                        s = pair * 2 + r
                        pool.wait_ge(b_loaded[r].sem, pair * 16 + 16)
                        for c in range(DI):
                            pool.wait_ge(scanned.sem, s * DI + c + 1)
                            pool.tensor_tensor(drive[:, c, :], du[:, c, :], b_row[:, r, :],
                                               ALU.mult).then_inc(drive_ready.sem, 1)

            @block.tensor
            def _(pe):
                transpose_on_tensor(pe, k, z, bank, normed, 0, turned)

                def project(q, at, done):
                    m, half = divmod(q, HALVES)
                    for c in range(DK):
                        last = pe.matmul(bank[:, at, :], w_in[:, c, m * P:(m + 1) * P],
                                         zT[:, c, half * BANK:(half + 1) * BANK], start=(c == 0), stop=(c == DK - 1))
                    last.then_inc(done.sem, 1)

                def low_rank(c):
                    pe.wait_ge(xs_ready.sem, c + 1)
                    for half in range(HALVES):
                        last = pe.matmul(bank[0:DT_RANK + 2 * D_STATE, half, :], w_x[:, c, :],
                                         xs[:, c, half * BANK:(half + 1) * BANK], start=(c == 0), stop=(c == DI - 1))
                        if c == DI - 1:
                            last.then_inc(low_ranked.sem, 1)

                def raise_delta(r):
                    c, half = divmod(r, HALVES)
                    pe.wait_ge(low_ready.sem, 2 * half + 1)
                    if r >= 4:
                        pe.wait_ge(delta_biased.sem, r - 3)
                    pe.matmul(bank[:, 2 + r % 4, :], w_dt[:, c * P:(c + 1) * P], dt_low[:, half * BANK:(half + 1) * BANK],
                              start=True, stop=True).then_inc(raised.sem, 1)

                def project_gate(q):
                    if q >= 2:
                        pe.wait_ge(gate_taken.sem, q - 1)
                    else:
                        pe.wait_ge(taken.sem, 7 + q)
                    project(8 + q, 6 + q % 2, gate_projected)

                for q in range(8):
                    pe.wait_ge(zT_ready.sem, 2 * (q % 2) + 2)
                    if q >= 4:
                        pe.wait_ge(taken.sem, q - 3)
                    project(q, 4 + q % 4, projected)
                for q in range(4):
                    project_gate(q)
                for c in range(DI):
                    low_rank(c)
                project_gate(4)
                for r in range(8):
                    raise_delta(r)
                    if r in (3, 5, 7):
                        project_gate(5 + (r - 3) // 2)
                pe.wait_ge(gate_taken.sem, 8)
                pe.wait_ge(delta_biased.sem, 8)
                pe.wait_ge(low_ready.sem, 4)
                for c in range(DI):
                    for half in range(HALVES):
                        last = pe.matmul(bank[:, 2 * c + half, :], skip_diag[:, c, :],
                                         xs[:, c, half * BANK:(half + 1) * BANK], start=True, stop=False,
                                         skip_group_check=True)
                    last.then_inc(summed.sem, 1)
                with pe.Fori(0, D_STATE) as s:
                    for c in range(DI):
                        pe.wait_ge(weighted.sem, DI + s * DI + c + 2)
                        for half in range(HALVES):
                            last = pe.matmul(bank[:, 2 * c + half, :], k.ident[:],
                                             h[:, c, half * BANK:(half + 1) * BANK], start=False, stop=False,
                                             skip_group_check=True)
                        last.then_inc(summed.sem, 1)
                pe.wait_ge(gated.sem, DI)
                for j in range(TILES):
                    for c in range(DI):
                        last = pe.matmul(bank[:, j, 0:DM], xs[:, c, j * P:(j + 1) * P], w_out[:, c, :],
                                         start=(c == 0), stop=(c == DI - 1))
                    last.then_inc(out_summed.sem, 1)

            @block.sync
            def _(sp):
                sp.wait_ge(low_ready.sem, 4)
                sp.dma_start(bc_dram, bc).then_inc(bc_stored.sem, 16)
                sp.wait_ge(bc_stored.sem, 16)
                with sp.Fori(0, D_STATE // 2) as pair:
                    for r in range(2):
                        row = pair * 2 + r
                        sp.wait_ge(weighted.sem, row * DI + 1)
                        sp.dma_start(b_row[:, r, :], bc_dram[bass.ds(row, 1), :].broadcast_to([P, SEQ])).then_inc(b_loaded[r].sem, 16)
                        sp.dma_start(c_row[:, r, :], bc_dram[bass.ds(row + D_STATE, 1), :].broadcast_to([P, SEQ])).then_inc(c_loaded[r].sem, 16)
            block_ctx.close()
            signal.clear()



CTX = 77
HOPS = 2
MASKED = -3.4028234663852886e38


def memory_stage(k):
    nc, d = k.nc, k.dram
    with ExitStack() as ctx:
        def sb(name, shape, dt=F32):
            return ctx.enter_context(nc.sbuf_tensor(name, shape, dt))

        context = sb("context", [CTX, BATCH, DM])
        contextT = sb("contextT", [P, DK, BATCH, CTX])
        w_hop = sb("w_hop", [P, HOPS, DK, DM])
        w_context = sb("w_context", [P, HOPS, DK, BATCH, CTX])
        mask_in = sb("mask_in", [P, BATCH, CTX], I32)
        keep = sb("keep", [P, BATCH, CTX])
        fill = sb("fill", [P, BATCH, CTX])
        n = NormBuffers(sb, "memory")
        u = sb("u", [P, TILES, DM])
        uT = sb("uT", [P, DK, SEQ])
        logits = sb("logits", [P, TILES, CTX])
        most = sb("most", [P, TILES])
        total = sb("total", [P, TILES])
        scale = sb("scale", [P, TILES])
        weightT = sb("weightT", [CTX, TILES, P])
        bank = ctx.enter_context(nc.psum_tensor("memory_psum", [P, 8, BANK], F32))

        with Prologue(nc) as pre:
            loaded = pre.semaphore("memory_loaded")
            turned = pre.semaphore("memory_turned")
            contextT_ready = pre.semaphore("memory_contextT_ready")
            folded = pre.semaphore("memory_folded")
            kept = pre.semaphore("memory_kept")
            block = pre.block()

            @block.sync
            def _(sp):
                sp.dma_start(context[:], d["ctx_1024"].rearrange("b l d -> l b d")).then_inc(loaded, 16)
                for i, name in enumerate(("L0_xattn_W0", "L0_xattn_W1")):
                    sp.dma_start(w_hop[:, i], d[name].rearrange("(c p) n -> p c n", p=P)).then_inc(loaded, 16)
                mask = d["mask_BxS2_if1"].rearrange("(o b) l -> o (b l)", o=1)
                sp.dma_start(mask_in[:].rearrange("p b l -> p (b l)"),
                             mask.broadcast_to([P, BATCH * CTX])).then_inc(loaded, 16)
                sp.wait_ge(loaded, 64)

            @block.tensor
            def _(pe):
                pe.wait_ge(loaded, 64)
                for b in range(BATCH):
                    for c in range(DK):
                        last = pe.transpose(bank[:, c, b * P:b * P + CTX], context[:, b, c * P:(c + 1) * P],
                                            k.ident[0:CTX, 0:CTX])
                last.then_inc(turned, 1)
                pe.wait_ge(contextT_ready, 1)
                for i in range(HOPS):
                    for m in range(DK):
                        for c in range(DK):
                            last = pe.matmul(bank[:, 2 + i * DK + m, 0:BATCH * CTX],
                                             w_hop[:, i, c, m * P:(m + 1) * P],
                                             contextT[:, c].rearrange("p b l -> p (b l)"),
                                             start=(c == 0), stop=(c == DK - 1))
                last.then_inc(folded, 1)

            @block.vector
            def _(dve):
                dve.wait_ge(loaded, 64)
                dve.tensor_scalar(keep[:], mask_in[:], 0, None, ALU.not_equal).then_inc(kept, 1)
                dve.wait_ge(kept, 1)
                dve.tensor_scalar(fill[:], keep[:], 1.0, -MASKED, ALU.subtract, ALU.mult)
                dve.wait_ge(turned, 1)
                for c in range(DK):
                    last = dve.tensor_copy(contextT[:, c],
                                           bank[:, c, :].rearrange("p (b l) -> p b l", l=P)[:, :, 0:CTX])
                last.then_inc(contextT_ready, 1)
                dve.wait_ge(folded, 1)
                for i in range(HOPS):
                    for m in range(DK):
                        last = dve.tensor_copy(w_context[:, i, m].rearrange("p b l -> p (b l)"),
                                               bank[:, 2 + i * DK + m, 0:BATCH * CTX])
                last.then_inc(kept, 1)
                dve.wait_ge(kept, 2)

        with ExitStack() as run, nc.Fori(0, BATCH) as b:
            signal = BatchSignals(run, nc, "memory_")
            chain = Chain(signal("chain"))
            moments_ready = signal("moments_ready")
            std_ready = signal("std_ready")
            u_ready = signal("u_ready")
            turned = signal("turned")
            uT_ready = signal("uT_ready")
            scored = signal("scored")
            shifted = signal("shifted")
            exp_taken = signal("exp_taken")
            weight_turned = signal("weight_turned")
            weightT_ready = signal("weightT_ready")
            read = signal("read")
            added = signal("added")
            block_ctx = ExitStack()
            block = block_ctx.enter_context(nc.Block())

            @block.vector
            def _(dve):
                norm_on_vector(dve, n, lambda j: k.X[:, b * TILES + j, :], u, chain, std_ready,
                               moments_ready, u_ready)
                for i in range(HOPS):
                    for half in range(HALVES):
                        js = slice(half * 4, half * 4 + 4)
                        psum = bank[:, 4 + half, :].rearrange("p (j l) -> p j l", l=P)[:, :, 0:CTX]
                        dve.wait_ge(scored.sem, i * HALVES + half + 1)
                        chain.link(dve, dve.tensor_tensor(logits[:, js], psum,
                                                          keep[:, bass.ds(b, 1), :].broadcast_to([P, 4, CTX]), ALU.mult))
                        chain.link(dve, dve.tensor_tensor(logits[:, js], logits[:, js],
                                                          fill[:, bass.ds(b, 1), :].broadcast_to([P, 4, CTX]), ALU.add))
                        chain.link(dve, dve.tensor_reduce(most[:, js], logits[:, js], AXIS.X, ALU.max))
                        dve.tensor_tensor(logits[:, js], logits[:, js],
                                          most[:, js].unsqueeze(2).broadcast_to([P, 4, CTX]),
                                          ALU.subtract).then_inc(shifted.sem, 1)
                    for half in range(HALVES):
                        js = slice(half * 4, half * 4 + 4)
                        dve.wait_ge(exp_taken.sem, i * HALVES + half + 1)
                        chain.link(dve, dve.tensor_reduce(total[:, js], logits[:, js], AXIS.X, ALU.add))
                        chain.link(dve, dve.reciprocal(scale[:, js], total[:, js]))
                    for j in range(TILES):
                        dve.wait_ge(read.sem, i * TILES // 2 + j // 2 + 1)
                        dve.scalar_tensor_tensor(out=u[:, j, :], in0=bank[:, j // 2, (j % 2) * DM:(j % 2 + 1) * DM],
                                                 scalar=scale[:, j:j + 1], in1=u[:, j, :], op0=ALU.mult,
                                                 op1=ALU.add).then_inc(u_ready.sem, 1)
                for j in range(TILES):
                    dve.wait_ge(u_ready.sem, HOPS * TILES + j + 1)
                    dve.tensor_tensor(k.X[:, b * TILES + j, :], k.X[:, b * TILES + j, :], u[:, j, :],
                                      ALU.add).then_inc(added.sem, 1)
                dve.wait_ge(added.sem, TILES)

            @block.scalar
            def _(act):
                roots_on_scalar(act, n, moments_ready, std_ready)
                for i in range(HOPS):
                    for q in range(4):
                        act.wait_ge(turned.sem, i * 4 + q + 1)
                        act.copy(columns_of(uT, q), bank[:, q, :]).then_inc(uT_ready.sem, 1)
                    for half in range(HALVES):
                        js = slice(half * 4, half * 4 + 4)
                        act.wait_ge(shifted.sem, i * HALVES + half + 1)
                        act.activation(logits[:, js], logits[:, js], ACT.Exp).then_inc(exp_taken.sem, 1)
                    for half in range(HALVES):
                        act.wait_ge(weight_turned.sem, i * HALVES + half + 1)
                        act.copy(weightT[:, half * 4:half * 4 + 4, :],
                                 bank[0:CTX, 6 + half, :].rearrange("p (j l) -> p j l", l=P)).then_inc(weightT_ready.sem, 1)

            @block.tensor
            def _(pe):
                for i in range(HOPS):
                    transpose_on_tensor(pe, k, u, bank, u_ready, i * TILES, turned)
                    for half in range(HALVES):
                        pe.wait_ge(uT_ready.sem, i * 4 + 2 * half + 2)
                        for j in range(half * 4, half * 4 + 4):
                            for c in range(DK):
                                last = pe.matmul(bank[:, 4 + half, (j % 4) * P:(j % 4) * P + CTX],
                                                 uT[:, c, j * P:(j + 1) * P],
                                                 w_context[:, i, c, bass.ds(b, 1), :].rearrange("p o l -> p (o l)"),
                                                 start=(c == 0), stop=(c == DK - 1))
                        last.then_inc(scored.sem, 1)
                    for half in range(HALVES):
                        pe.wait_ge(exp_taken.sem, i * HALVES + half + 1)
                        for j in range(half * 4, half * 4 + 4):
                            last = pe.transpose(bank[0:CTX, 6 + half, (j % 4) * P:(j % 4 + 1) * P],
                                                logits[:, j, :], k.ident[:])
                        last.then_inc(weight_turned.sem, 1)
                    for half in range(HALVES):
                        pe.wait_ge(weightT_ready.sem, i * HALVES + half + 1)
                        for j in range(half * 4, half * 4 + 4):
                            last = pe.matmul(bank[:, j // 2, (j % 2) * DM:(j % 2 + 1) * DM], weightT[:, j, :],
                                             context[:, bass.ds(b, 1), :].rearrange("p o l -> p (o l)"),
                                             start=True, stop=True)
                            if j % 2:
                                last.then_inc(read.sem, 1)

            block_ctx.close()
            signal.clear()



FF = 1024
HEADS, KEYS, TOP = 4, 64, 8
EXPERTS = 1024
ROWS = EXPERTS // KEYS
KW = 64
SIDES = 2
FC = FF // P
EC = EXPERTS // P


def expert_plan():
    def weights(j, heads):
        return ([("choose", j)] if 0 in heads else []) + [("head", j, h) for h in heads]

    plan = []
    for q in range(FC):
        plan += weights(q // HEADS, [q % HEADS]) + [("piece", q)]
    for j in range(TILES):
        plan += [("turn", j)]
        if j < TILES // 2:
            plan += weights(j + 2, [0]) + [("piece", FC + 2 * j)] + weights(j + 2, range(1, HEADS))
            plan += [("out", j), ("piece", FC + 2 * j + 1)]
        else:
            plan += [("out", j)] + (weights(j + 2, range(HEADS)) if j + 2 < TILES else [])
    return plan


def expert_stage(k):
    nc, d = k.nc, k.dram
    with ExitStack() as ctx:
        def sb(name, shape, dt=F32):
            return ctx.enter_context(nc.sbuf_tensor(name, shape, dt))

        w_sim = sb("w_sim", [P, DK, SIDES * HEADS * KEYS])
        downT = sb("downT", [P, DK, EXPERTS])
        up = sb("up", [P, EC, DM])
        w_g = sb("w_g", [P, DK, FF])
        w_u = sb("w_u", [P, DK, FF])
        w_d = sb("w_d", [P, FC, DM])
        b_g = sb("b_g", [P, FC])
        b_u = sb("b_u", [P, FC])
        b_d = sb("b_d", [1, DM])
        n = NormBuffers(sb, "expert")
        y = sb("y", [P, TILES, DM])
        yT = sb("yT", [P, DK, SEQ])
        sims = sb("sims", [P, TILES, SIDES * HEADS * KEYS])
        hitT = sb("hitT", [P, EC, SEQ])
        innerT = sb("innerT", [P, FC, SEQ])
        gate = sb("ffn_gate", [P, BANK])
        best = sb("best", [P, SIDES, HEADS, TOP])
        pairs = sb("pairs", [P, HEADS, TOP, TOP])
        score = sb("score", [P, HEADS, TOP])
        escore = sb("escore", [P, HEADS, TOP])
        neg_most = sb("neg_most", [P, 2, HEADS])
        total = sb("expert_total", [P, HEADS])
        inv_total = sb("inv_total", [P, HEADS])
        given = sb("given", [P, 2])
        table = sb("table", [P, 2, ROWS, KEYS])
        picked = sb("picked", [P, 2, ROWS, KEYS])
        weight = sb("weight", [P, 2, EXPERTS])
        mixedT = y[:].rearrange("p (r e) t -> p r (e t)", r=2)
        bank = ctx.enter_context(nc.psum_tensor("expert_psum", [P, 8, BANK], F32))

        with Prologue(nc) as pre:
            loaded = pre.semaphore("expert_loaded")
            folded = pre.semaphore("expert_folded")
            kept = pre.semaphore("expert_kept")
            w_q = hitT[0:KW, 0:2, :].rearrange("p a (s d) -> p (a s) d", d=DM)
            keys = hitT[0:KW, 2, 0:SIDES * HEADS * KEYS].rearrange("p (s h e) -> p s h e", s=SIDES, h=HEADS)
            block = pre.block()
            loads = [
                (w_q[:], d["L0_ffn_Wq"].rearrange("(s n) d -> n s d", n=KW)),
                (keys[:], d["L0_ffn_keys"]),
                (downT[:], d["L0_ffn_down_embed"].rearrange("(c p) n -> p c n", p=P)),
                (up[:], d["L0_ffn_up_embed"].rearrange("(c p) n -> p c n", p=P)),
                (w_g[:], d["L0_ffn_Wg"].rearrange("(c p) n -> p c n", p=P)),
                (w_u[:], d["L0_ffn_Wu"].rearrange("(c p) n -> p c n", p=P)),
                (w_d[:], d["L0_ffn_Wd"].rearrange("(c p) n -> p c n", p=P)),
                (b_g[:], d["L0_ffn_bg"].rearrange("(c p) -> p c", p=P)),
                (b_u[:], d["L0_ffn_bu"].rearrange("(c p) -> p c", p=P)),
                (b_d[:], d["L0_ffn_bd"].rearrange("(o n) -> o n", o=1)),
            ]

            @block.sync
            def _(sp):
                for dst, src in loads:
                    sp.dma_start(dst, src, allow_slow_non_contiguous=True).then_inc(loaded, 16)
                sp.wait_ge(loaded, 16 * len(loads))

            @block.tensor
            def _(pe):
                pe.wait_ge(loaded, 16 * len(loads))
                for m in range(DK):
                    for s in range(SIDES * HEADS):
                        last = pe.matmul(bank[:, m, s * KEYS:(s + 1) * KEYS], w_q[:, s, m * P:(m + 1) * P],
                                         keys[:, s // HEADS, s % HEADS, :], start=True, stop=True)
                last.then_inc(folded, 1)

            @block.vector
            def _(dve):
                dve.wait_ge(folded, 1)
                for m in range(DK):
                    dve.tensor_copy(w_sim[:, m, :], bank[:, m, :]).then_inc(kept, 1)
                dve.wait_ge(kept, DK)

        with ExitStack() as run, nc.Fori(0, BATCH) as b:
            signal = BatchSignals(run, nc, "expert_")
            chain = Chain(signal("chain"))
            moments_ready = signal("moments_ready")
            std_ready = signal("std_ready")
            normed = signal("normed")
            turned = signal("turned")
            yT_ready = signal("yT_ready")
            compared = signal("compared")
            sims_ready = signal("sims_ready")
            hit = signal("hit")
            hitT_ready = signal("hitT_ready")
            gate_done = signal("gate_done")
            up_done = signal("up_done")
            gate_ready = signal("gate_ready")
            innerT_ready = signal("innerT_ready")
            most_ready = signal("most_ready")
            score_shifted = signal("score_shifted")
            escore_ready = signal("escore_ready")
            table_ready = signal("table_ready")
            exp_ready = signal("exp_ready")
            picked_ready = signal("picked_ready")
            head_added = signal("head_added")
            weight_ready = signal("weight_ready")
            weight_turned = signal("weight_turned")
            mixed = signal("mixed")
            out_summed = signal("out_summed")
            added = signal("added")
            block_ctx = ExitStack()
            block = block_ctx.enter_context(nc.Block())

            @block.vector
            def _(dve):
                norm_on_vector(dve, n, lambda j: k.X[:, b * TILES + j, :], y, chain, std_ready,
                               moments_ready, normed)

                def gate_up(q):
                    half, m = divmod(q, FC)
                    dve.wait_ge(up_done.sem, q + 1)
                    dve.wait_ge(gate_ready.sem, q + 1)
                    dve.scalar_tensor_tensor(out=innerT[:, m, half * BANK:(half + 1) * BANK], in0=bank[:, 7, :],
                                             scalar=b_u[:, m:m + 1], in1=gate[:], op0=ALU.add,
                                             op1=ALU.mult).then_inc(innerT_ready.sem, 1)

                def choose(j):
                    dve.wait_ge(sims_ready.sem, j + 1)
                    sim = sims[:, j, :].rearrange("p (s h e) -> p s h e", s=SIDES, h=HEADS)
                    for s in range(SIDES):
                        for h in range(HEADS):
                            last = dve.max(best[:, s, h, :], sim[:, s, h, :])
                    chain.link(dve, last)
                    chain.link(dve, dve.tensor_tensor(
                        pairs[:], best[:, 0].unsqueeze(3).broadcast_to([P, HEADS, TOP, TOP]),
                        best[:, 1].unsqueeze(2).broadcast_to([P, HEADS, TOP, TOP]), ALU.add))
                    if j >= 1:
                        dve.wait_ge(escore_ready.sem, j)
                    for h in range(HEADS):
                        last = dve.max(score[:, h, :], pairs[:, h].rearrange("p a b -> p (a b)"))
                    chain.link(dve, last)
                    if j >= 2:
                        dve.wait_ge(exp_ready.sem, HEADS * (j - 1))
                    dve.tensor_scalar(neg_most[:, j % 2, :], score[:, :, 0], -1.0, None,
                                      ALU.mult).then_inc(most_ready.sem, 1)
                    dve.tensor_tensor(escore[:], score[:], score[:, :, 0:1].broadcast_to([P, HEADS, TOP]),
                                      ALU.subtract).then_inc(score_shifted.sem, 1)

                def weigh(j, h):
                    t = j * HEADS + h
                    if h == 0:
                        dve.wait_ge(escore_ready.sem, j + 1)
                        chain.link(dve, dve.tensor_reduce(total[:], escore[:], AXIS.X, ALU.add))
                        chain.link(dve, dve.reciprocal(inv_total[:], total[:]))
                        if j >= 2:
                            dve.wait_ge(weight_turned.sem, j - 1)
                    w = weight[:, j % 2, :]
                    e = picked[:, t % 2].rearrange("p r e -> p (r e)")
                    dve.wait_ge(exp_ready.sem, t + 1)
                    dve.scalar_tensor_tensor(out=e, in0=table[:, t % 2].rearrange("p r e -> p (r e)"),
                                             scalar=score[:, h, TOP - 1:TOP], in1=e, op0=ALU.is_ge,
                                             op1=ALU.mult).then_inc(picked_ready.sem, 1)
                    dve.wait_ge(picked_ready.sem, t + 1)
                    if h == 0:
                        last = dve.tensor_scalar(w, e, inv_total[:, 0:1], None, ALU.mult)
                    elif h < HEADS - 1:
                        last = dve.scalar_tensor_tensor(out=w, in0=e, scalar=inv_total[:, h:h + 1], in1=w,
                                                        op0=ALU.mult, op1=ALU.add)
                    else:
                        last = dve.scalar_tensor_tensor(out=w, in0=e, scalar=inv_total[:, h:h + 1], in1=w,
                                                        op0=ALU.mult, op1=ALU.add, accum_out=given[:, 0:1])
                    last.then_inc(head_added.sem, 1)
                    dve.wait_ge(head_added.sem, t + 1)
                    if h == HEADS - 1:
                        chain.link(dve, dve.tensor_scalar(given[:, 1:2], given[:, 0:1], -1.0, float(HEADS),
                                                          ALU.mult, ALU.add))
                        dve.tensor_tensor(w[:, EXPERTS - 1:], w[:, EXPERTS - 1:], given[:, 1:2],
                                          ALU.add).then_inc(weight_ready.sem, 1)

                def mix(j):
                    dve.wait_ge(weight_turned.sem, j + 1)
                    dve.wait_ge(hitT_ready.sem, FC * (1 + j // 4))
                    if j >= 2:
                        dve.wait_ge(out_summed.sem, j - 1)
                    dve.tensor_tensor(mixedT[:, j % 2].rearrange("p (e t) -> p e t", t=P),
                                      bank[:, 2:4, :].rearrange("p a (e t) -> p (a e) t", t=P),
                                      hitT[:, :, j * P:(j + 1) * P], ALU.mult).then_inc(mixed.sem, 1)

                def add_out(j):
                    dve.wait_ge(out_summed.sem, j + 1)
                    dve.tensor_tensor(k.X[:, b * TILES + j, :], k.X[:, b * TILES + j, :], bank[:, j % 2, 0:DM],
                                      ALU.add).then_inc(added.sem, 1)

                for what, *at in expert_plan():
                    if what == "choose":
                        choose(*at)
                    elif what == "head":
                        weigh(*at)
                    elif what == "piece":
                        gate_up(*at)
                    elif what == "turn":
                        mix(*at)
                        if at[0] >= 1:
                            add_out(at[0] - 1)
                add_out(TILES - 1)
                dve.wait_ge(added.sem, TILES)

            @block.gpsimd
            def _(pool):
                for j in range(TILES):
                    pool.wait_ge(sims_ready.sem, j + 1)
                    sim = sims[:, j, :].rearrange("p (s h e) -> p s h e", s=SIDES, h=HEADS)
                    for h in range(HEADS):
                        t = j * HEADS + h
                        if t >= 2:
                            pool.wait_ge(picked_ready.sem, t - 1)
                        pool.tensor_tensor(table[:, t % 2], sim[:, 0, h, 0:ROWS].unsqueeze(2).broadcast_to([P, ROWS, KEYS]),
                                           sim[:, 1, h:h + 1, :].broadcast_to([P, ROWS, KEYS]),
                                           ALU.add).then_inc(table_ready.sem, 1)

            @block.scalar
            def _(act):
                roots_on_scalar(act, n, moments_ready, std_ready)
                for q in range(4):
                    act.wait_ge(turned.sem, q + 1)
                    act.copy(columns_of(yT, q), bank[:, q, :]).then_inc(yT_ready.sem, 1)
                for j in range(TILES):
                    act.wait_ge(compared.sem, j + 1)
                    act.copy(sims[:, j, :], bank[:, 4 + j % 4, :]).then_inc(sims_ready.sem, 1)
                for what, *at in expert_plan():
                    if what == "piece":
                        q = at[0]
                        half, m = divmod(q, FC)
                        act.wait_ge(hit.sem, q + 1)
                        act.activation(hitT[:, m, half * BANK:(half + 1) * BANK], bank[:, 4 + q % 2, :],
                                       ACT.Silu).then_inc(hitT_ready.sem, 1)
                        act.wait_ge(gate_done.sem, q + 1)
                        if q >= 1:
                            act.wait_ge(innerT_ready.sem, q)
                        act.activation(gate[:], bank[:, 6, :], ACT.Silu, bias=b_g[:, m:m + 1]).then_inc(gate_ready.sem, 1)
                    elif what == "choose":
                        j = at[0]
                        act.wait_ge(score_shifted.sem, j + 1)
                        act.activation(escore[:], escore[:], ACT.Exp).then_inc(escore_ready.sem, 1)
                    elif what == "head":
                        j, h = at
                        t = j * HEADS + h
                        act.wait_ge(most_ready.sem, j + 1)
                        act.wait_ge(table_ready.sem, t + 1)
                        if t >= 2:
                            act.wait_ge(head_added.sem, t - 1)
                        act.activation(picked[:, t % 2], table[:, t % 2], ACT.Exp,
                                       bias=neg_most[:, j % 2, h:h + 1]).then_inc(exp_ready.sem, 1)

            @block.tensor
            def _(pe):
                transpose_on_tensor(pe, k, y, bank, normed, 0, turned)
                for j in range(TILES):
                    pe.wait_ge(yT_ready.sem, 2 if j < 4 else 4)
                    if j >= 4:
                        pe.wait_ge(sims_ready.sem, j - 3)
                    for c in range(DK):
                        last = pe.matmul(bank[:, 4 + j % 4, :], yT[:, c, j * P:(j + 1) * P], w_sim[:, c, :],
                                         start=(c == 0), stop=(c == DK - 1))
                    last.then_inc(compared.sem, 1)
                pe.wait_ge(sims_ready.sem, TILES)

                def piece(q):
                    half, m = divmod(q, FC)
                    cols = slice(half * BANK, (half + 1) * BANK)
                    for w, slot, done, taken, lag in ((downT, 4 + q % 2, hit, hitT_ready, 2),
                                                      (w_g, 6, gate_done, gate_ready, 1),
                                                      (w_u, 7, up_done, innerT_ready, 1)):
                        if q >= lag:
                            pe.wait_ge(taken.sem, q - lag + 1)
                        for c in range(DK):
                            last = pe.matmul(bank[:, slot, :], w[:, c, m * P:(m + 1) * P], yT[:, c, cols],
                                             start=(c == 0), stop=(c == DK - 1))
                        last.then_inc(done.sem, 1)

                def turn(j):
                    pe.wait_ge(weight_ready.sem, j + 1)
                    if j >= 1:
                        pe.wait_ge(mixed.sem, j)
                    for e in range(EC):
                        last = pe.transpose(bank[:, 2 + e // 4, (e % 4) * P:(e % 4 + 1) * P],
                                            weight[:, j % 2, e * P:(e + 1) * P], k.ident[:])
                    last.then_inc(weight_turned.sem, 1)

                def out_of(j):
                    out = bank[:, j % 2, 0:DM]
                    if j >= 2:
                        pe.wait_ge(added.sem, j - 1)
                    pe.matmul(out, k.ones[0:1, :], b_d[:], start=True, stop=False)
                    pe.wait_ge(innerT_ready.sem, FC * (1 + j // 4))
                    for c in range(FC):
                        pe.matmul(out, innerT[:, c, j * P:(j + 1) * P], w_d[:, c, :], start=False, stop=False)
                    pe.wait_ge(mixed.sem, j + 1)
                    for c in range(EC):
                        last = pe.matmul(out, mixedT[:, j % 2, c * P:(c + 1) * P], up[:, c, :], start=False,
                                         stop=(c == EC - 1))
                    last.then_inc(out_summed.sem, 1)

                for what, *at in expert_plan():
                    if what == "piece":
                        piece(*at)
                    elif what == "turn":
                        turn(*at)
                    elif what == "out":
                        out_of(*at)

            block_ctx.close()
            signal.clear()



FILTER = 4
LOW1, LOW2 = SEQ // 2, SEQ // 4
HEAD_W = 16
ATTN_EPS = 1e-6


def wavelet_stage(k):
    nc, d = k.nc, k.dram
    with ExitStack() as ctx:
        def sb(name, shape, dt=F32):
            return ctx.enter_context(nc.sbuf_tensor(name, shape, dt))

        filters = sb("filters", [P, 4, DK, FILTER])
        even = sb("even", [P, 2, DK, 3])
        odd = sb("odd", [P, 2, DK, 2])
        high_diag = sb("high_diag", [P, DK, FILTER, P])
        even_diag = sb("even_diag", [P, DK, 3, P])
        odd_diag = sb("odd_diag", [P, DK, 2, P])
        gamma = sb("gamma", [P, DM])
        beta = sb("beta", [P, DM])
        heads = sb("heads", [P, P])
        n = NormBuffers(sb, "wavelet")
        n2 = NormBuffers(sb, "wavelet2")
        y = sb("wavelet_y", [P, TILES, DM])
        yT = sb("wavelet_yT", [P, DK, SEQ + 3])
        low1 = sb("low1", [P, DK, LOW1 + 3])
        high1 = sb("high1", [P, DK, LOW1 + 2])
        low2 = sb("low2", [P, DK, LOW2])
        high2 = sb("high2", [P, DK, LOW2 + 2])
        below = sb("below", [P, DK, LOW2])
        qT = sb("qT", [P, DK, LOW2])
        v_tokens = sb("v_tokens", [P, 2, DM])
        k_tokens = sb("k_tokens", [P, 2, DM])
        kv = sb("kv", [P, DK, P])
        z_column = sb("z_column", [P, DK])
        z_heads = sb("z_heads", [P, DK, P])
        den = sb("den", [P, DK, LOW2])
        attended = sb("attended", [P, DK, LOW2 + 2])
        back2 = sb("back2", [P, DK, LOW1 + 2])
        back1 = sb("back1", [P, DK, SEQ])
        bank = ctx.enter_context(nc.psum_tensor("wavelet_psum", [P, 8, BANK], F32))

        with Prologue(nc) as pre:
            loaded = pre.semaphore("wavelet_loaded")
            masked = pre.semaphore("wavelet_masked")
            combined = pre.semaphore("wavelet_combined")
            block = pre.block()

            @block.sync
            def _(sp):
                for i, name in enumerate(("h_filter", "g_filter", "h_synth", "g_synth")):
                    for c in range(DK):
                        sp.dma_start(filters[:, i, c, :], d["L1_attn_" + name][:, c * P:(c + 1) * P].rearrange("f p -> p f"),
                                     allow_slow_non_contiguous=True).then_inc(loaded, 16)
                for dst, name in ((gamma, "norm_gamma"), (beta, "norm_beta")):
                    row = d["L1_attn_" + name].rearrange("(o n) -> o n", o=1)
                    sp.dma_start(dst[:], row.broadcast_to([P, DM])).then_inc(loaded, 16)
                sp.wait_ge(loaded, 160)

            @block.gpsimd
            def _(pool):
                blocks = heads[:].rearrange("p (a r) -> p a r", r=HEAD_W)
                pool.affine_select(out=blocks, in_=k.ones[:].rearrange("p (a r) -> p a r", r=HEAD_W),
                                   compare_op=ALU.is_ge, fill=0.0, base=0, pattern=[[-HEAD_W, P // HEAD_W], [0, HEAD_W]],
                                   channel_multiplier=1).then_inc(masked, 1)
                pool.wait_ge(masked, 1)
                pool.affine_select(out=blocks, in_=blocks, compare_op=ALU.is_ge, fill=0.0, base=HEAD_W - 1,
                                   pattern=[[HEAD_W, P // HEAD_W], [0, HEAD_W]],
                                   channel_multiplier=-1).then_inc(masked, 1)
                pool.wait_ge(masked, 2)

            @block.vector
            def _(dve):
                dve.wait_ge(loaded, 160)
                f = filters[:, 2:4]
                dve.tensor_copy(even[:, :, :, 0:1], f[:, :, :, 0:1])
                dve.tensor_tensor(even[:, :, :, 1:2], f[:, :, :, 1:2], f[:, :, :, 2:3], ALU.add)
                dve.tensor_copy(even[:, :, :, 2:3], f[:, :, :, 3:4])
                dve.tensor_tensor(odd[:, :, :, 0:1], f[:, :, :, 0:1], f[:, :, :, 1:2], ALU.add)
                dve.tensor_tensor(odd[:, :, :, 1:2], f[:, :, :, 2:3], f[:, :, :, 3:4], ALU.add).then_inc(combined, 1)
                dve.wait_ge(combined, 1)
                for c in range(DK):
                    for diag, taps in ((high_diag, filters[:, 1, c]), (even_diag, even[:, 1, c]), (odd_diag, odd[:, 1, c])):
                        for t in range(diag.shape[2]):
                            dve.tensor_scalar(diag[:, c, t, :], k.ident[:], taps[:, t:t + 1], None, ALU.mult)
                for t, w in ((yT, SEQ), (low1, LOW1), (high1, LOW1), (high2, LOW2), (attended, LOW2), (back2, LOW1)):
                    for c in range(DK):
                        dve.memset(t[:, c, 0:1], 0.0)
                        last = dve.memset(t[:, c, w + 1:], 0.0)
                last.then_inc(combined, 1)
                dve.wait_ge(combined, 2)

        with ExitStack() as run, nc.Fori(0, BATCH) as b:
            signal = BatchSignals(run, nc, "wavelet_")
            chain = Chain(signal("chain"))
            moments_ready = signal("moments_ready")
            std_ready = signal("std_ready")
            normed = signal("normed")
            turned = signal("turned")
            yT_ready = signal("yT_ready")
            tapped = signal("tapped")
            high_done = signal("high_done")
            high_ready = signal("high_ready")
            high_back = signal("high_back")
            below_ready = signal("below_ready")
            exp_taken = signal("exp_taken")
            q_ready = signal("q_ready")
            tokens_turned = signal("tokens_turned")
            tokens_ready = signal("tokens_ready")
            kv_done = signal("kv_done")
            kv_ready = signal("kv_ready")
            num_den = signal("num_den")
            back_turned = signal("back_turned")
            moments2_ready = signal("moments2_ready")
            std2_ready = signal("std2_ready")
            normed2 = signal("normed2")
            scaled = signal("scaled")
            shifted = signal("shifted")
            added = signal("added")
            block_ctx = ExitStack()
            block = block_ctx.enter_context(nc.Block())

            @block.vector
            def _(dve):
                norm_on_vector(dve, n, lambda j: k.X[:, b * TILES + j, :], y, chain, std_ready,
                               moments_ready, normed)
                count = [0]

                def filter_all(outputs):
                    last_of = {}
                    for i in range(max(len(taps) for _, _, taps in outputs)):
                        for o, (out, start, taps) in enumerate(outputs):
                            if i >= len(taps):
                                continue
                            tap, source = taps[i]
                            if i:
                                dve.wait_ge(tapped.sem, last_of[o])
                            acc = out if i else start
                            if acc is None:
                                ins = dve.tensor_scalar(out, source, tap, None, ALU.mult)
                            else:
                                ins = dve.scalar_tensor_tensor(out=out, in0=source, scalar=tap, in1=acc,
                                                               op0=ALU.mult, op1=ALU.add)
                            ins.then_inc(tapped.sem, 1)
                            count[0] += 1
                            last_of[o] = count[0]
                    dve.wait_ge(tapped.sem, count[0])

                def analysis(source, low, length):
                    filter_all([(low[c], None, [(filters[:, 0, c, t:t + 1], source[:, c, t:t + 2 * length - 1:2])
                                                for t in range(FILTER)]) for c in range(DK)])

                def synthesis(source, out, start, length):
                    outputs = []
                    for c in range(DK):
                        for parity, taps in ((0, even), (1, odd)):
                            outputs.append((out[c][:, parity:2 * length:2], start[c][:, parity:2 * length:2],
                                            [(taps[:, 0, c, t:t + 1], source[:, c, t + parity:t + parity + length])
                                             for t in range(3 - parity)]))
                    filter_all(outputs)

                dve.wait_ge(yT_ready.sem, 4)
                analysis(yT, [low1[:, c, 1:1 + LOW1] for c in range(DK)], LOW1)
                analysis(low1, [low2[:, c, :] for c in range(DK)], LOW2)
                dve.tensor_scalar(below[:], low2[:], 0.0, None, ALU.min).then_inc(below_ready.sem, 1)
                dve.wait_ge(exp_taken.sem, 1)
                for c in range(DK):
                    dve.scalar_tensor_tensor(out=qT[:, c, :], in0=low2[:, c, :], scalar=0.0, in1=below[:, c, :],
                                             op0=ALU.max, op1=ALU.add).then_inc(q_ready.sem, 1)
                dve.wait_ge(tokens_turned.sem, 2)
                dve.tensor_copy(v_tokens[:].rearrange("p i n -> p (i n)"), bank[:, 4, :]).then_inc(tokens_ready.sem, 1)
                dve.tensor_copy(k_tokens[:].rearrange("p i n -> p (i n)"), bank[:, 5, :]).then_inc(tokens_ready.sem, 1)
                dve.wait_ge(kv_done.sem, 2)
                chain.link(dve, dve.tensor_copy(z_column[:], bank[:, 7, 0:DK]))
                for c in range(DK):
                    dve.tensor_tensor(kv[:, c, :], bank[:, 6, c * P:(c + 1) * P], heads[:], ALU.mult)
                    dve.tensor_scalar(z_heads[:, c, :], heads[:], z_column[:, c:c + 1], None,
                                      ALU.mult).then_inc(kv_ready.sem, 1)
                dve.wait_ge(num_den.sem, 2)
                chain.link(dve, dve.tensor_scalar(den[:].rearrange("p c t -> p (c t)"), bank[:, 5, :], ATTN_EPS, None,
                                                  ALU.add))
                chain.link(dve, dve.reciprocal(den[:], den[:]))
                chain.link(dve, dve.tensor_tensor(attended[:, :, 1:1 + LOW2],
                                                  bank[:, 4, :].rearrange("p (c t) -> p c t", c=DK), den[:], ALU.mult))
                dve.wait_ge(high_back.sem, 2 + 1)
                synthesis(attended, [back2[:, c, 1:1 + LOW1] for c in range(DK)],
                          [bank[:, 6 + c, :] for c in range(DK)], LOW2)
                dve.wait_ge(high_back.sem, 2 * DK + 1)
                synthesis(back2, [back1[:, c, :] for c in range(DK)],
                          [bank[:, 2 * c:2 * c + 2, :].rearrange("p a n -> p (a n)") for c in range(DK)], LOW1)
                dve.wait_ge(back_turned.sem, 4)
                norm_on_vector(dve, n2, lambda j: bank[:, j // 2, (j % 2) * DM:(j % 2 + 1) * DM], y, chain, std2_ready,
                               moments2_ready, normed2)
                dve.wait_ge(normed2.sem, TILES)
                ys = y[:, TILES // 2:, :]
                for row, op in ((gamma, ALU.mult), (beta, ALU.add)):
                    chain.link(dve, dve.tensor_tensor(ys, ys, row[:].unsqueeze(1).broadcast_to([P, TILES // 2, DM]), op))
                for half in (1, 0):
                    js = bass.ds(b * TILES + half * 4, 4)
                    if half == 0:
                        dve.wait_ge(shifted.sem, 1)
                    dve.tensor_tensor(k.X[:, js, :], k.X[:, js, :], y[:, half * 4:half * 4 + 4, :],
                                      ALU.add).then_inc(added.sem, 1)
                dve.wait_ge(added.sem, HALVES)

            @block.gpsimd
            def _(pool):
                ys = y[:, 0:TILES // 2, :]
                pool.wait_ge(normed2.sem, TILES // 2)
                pool.tensor_tensor(ys, ys, gamma[:].unsqueeze(1).broadcast_to([P, TILES // 2, DM]),
                                   ALU.mult).then_inc(scaled.sem, 1)
                pool.wait_ge(scaled.sem, 1)
                pool.tensor_tensor(ys, ys, beta[:].unsqueeze(1).broadcast_to([P, TILES // 2, DM]),
                                   ALU.add).then_inc(shifted.sem, 1)

            @block.scalar
            def _(act):
                roots_on_scalar(act, n, moments_ready, std_ready)
                for q in range(4):
                    act.wait_ge(turned.sem, q + 1)
                    act.copy(columns_of(yT, q, pad=1), bank[:, q, :]).then_inc(yT_ready.sem, 1)
                for c in range(DK):
                    act.wait_ge(high_done.sem, c + 1)
                    act.copy(high1[:, c, 1:1 + LOW1], bank[:, 6 + c, :]).then_inc(high_ready.sem, 1)
                act.wait_ge(high_done.sem, DK + 1)
                act.copy(high2[:, :, 1:1 + LOW2], bank[:, 4, :].rearrange("p (c t) -> p c t", c=DK)).then_inc(high_ready.sem, 1)
                act.wait_ge(below_ready.sem, 1)
                act.activation(below[:], below[:], ACT.Exp).then_inc(exp_taken.sem, 1)
                roots_on_scalar(act, n2, moments2_ready, std2_ready)

            @block.tensor
            def _(pe):
                transpose_on_tensor(pe, k, y, bank, normed, 0, turned)

                def high_back_1(c, half):
                    out = bank[:, 2 * c + half, :]
                    pe.matmul(out, k.ident[:], yT[:, c, 1 + half * BANK:1 + (half + 1) * BANK], start=True, stop=False,
                              skip_group_check=True)
                    first = half * BANK // 2
                    for parity, diag in ((0, even_diag), (1, odd_diag)):
                        for t in range(3 - parity):
                            at = t + parity + first
                            last = pe.matmul(out[:, parity::2], diag[:, c, t, :], high1[:, c, at:at + BANK // 2],
                                             start=False, stop=(parity == 1 and t == 1), skip_group_check=True)
                    last.then_inc(high_back.sem, 1)

                pe.wait_ge(yT_ready.sem, 4)
                for c in range(DK):
                    for t in range(FILTER):
                        last = pe.matmul(bank[:, 6 + c, :], high_diag[:, c, t, :], yT[:, c, t:t + 2 * LOW1 - 1:2],
                                         start=(t == 0), stop=(t == FILTER - 1))
                    last.then_inc(high_done.sem, 1)
                pe.wait_ge(tapped.sem, DK * FILTER)
                for c in range(DK):
                    for t in range(FILTER):
                        last = pe.matmul(bank[:, 4, c * LOW2:(c + 1) * LOW2], high_diag[:, c, t, :],
                                         low1[:, c, t:t + 2 * LOW2 - 1:2], start=(t == 0), stop=(t == FILTER - 1))
                last.then_inc(high_done.sem, 1)
                pe.wait_ge(high_ready.sem, DK)
                high_back_1(0, 0)
                for source, slot in ((low2, 4), (qT, 5)):
                    pe.wait_ge(q_ready.sem, DK)
                    pe.wait_ge(high_ready.sem, DK + 1)
                    for i in range(2):
                        for c in range(DK):
                            last = pe.transpose(bank[:, slot, (i * DK + c) * P:(i * DK + c + 1) * P],
                                                source[:, c, i * P:(i + 1) * P], k.ident[:])
                    last.then_inc(tokens_turned.sem, 1)
                pe.wait_ge(tokens_ready.sem, 2)
                for c in range(DK):
                    for i in range(2):
                        last = pe.matmul(bank[:, 6, c * P:(c + 1) * P], k_tokens[:, i, c * P:(c + 1) * P],
                                         v_tokens[:, i, c * P:(c + 1) * P], start=(i == 0), stop=(i == 1))
                last.then_inc(kv_done.sem, 1)
                for c in range(DK):
                    for i in range(2):
                        last = pe.matmul(bank[:, 7, c:c + 1], k_tokens[:, i, c * P:(c + 1) * P], k.ones[:, 0:1],
                                         start=(i == 0), stop=(i == 1))
                last.then_inc(kv_done.sem, 1)
                high_back_1(0, 1)
                pe.wait_ge(kv_ready.sem, DK)
                for w, slot in ((kv, 4), (z_heads, 5)):
                    for c in range(DK):
                        last = pe.matmul(bank[:, slot, c * LOW2:(c + 1) * LOW2], w[:, c, :], qT[:, c, :],
                                         start=True, stop=True)
                    last.then_inc(num_den.sem, 1)
                for c in range(DK):
                    for parity, diag in ((0, even_diag), (1, odd_diag)):
                        for t in range(3 - parity):
                            last = pe.matmul(bank[:, 6 + c, parity::2], diag[:, c, t, :],
                                             high2[:, c, t + parity:t + parity + LOW2], start=(t == 0),
                                             stop=(t == 2 - parity), skip_group_check=True)
                last.then_inc(high_back.sem, 1)
                for half in range(HALVES):
                    high_back_1(1, half)
                pe.wait_ge(tapped.sem, WAVELET_TAPS)
                for j in range(TILES):
                    for c in range(DK):
                        last = pe.transpose(bank[:, j // 2, ((j % 2) * DK + c) * P:((j % 2) * DK + c + 1) * P],
                                            back1[:, c, j * P:(j + 1) * P], k.ident[:])
                    if j % 2:
                        last.then_inc(back_turned.sem, 1)

            block_ctx.close()
            signal.clear()


WAVELET_TAPS = 2 * (DK * FILTER) + 2 * (DK * 5)



A_HEADS, A_W = 16, 64
INNER = A_HEADS * A_W
KEYS_ALL = SEQ + CTX
KT = TILES + 1
PAIRS = A_HEADS // 2
GROUP = 4
TP = 2 * TILES
GP = TP // GROUP
PIECES = 7
CTX_PIECE = 4
FIRST_BANKS = (4, 5, 6, 3, 2, 7, 1)
CHUNKS = 2 * GROUP + 1
CTX_CHUNK = 2
QK_STACKED, V_STACKED = 6 * 16, 2 * 16
RING = 2 * GROUP
F16 = mybir.dt.float16

BANK7 = []
for _g in range(GP):
    _t = GROUP * _g
    if _g:
        BANK7 += [(_t, "end", "piece", 2 * _g - 1)]
    BANK7 += [(_t + 1, "end", "values", _g - 1), (_t + 2, "middle", "out", 2 * _g - 2),
              (_t + 3, "early", "out", 2 * _g - 1), (_t + 3, "end", "piece", 2 * _g)]
BANK7_LAST = [(TP, "end", "values", GP - 1), (TP, "end", "out", TP // 2 - 2), (TP, "end", "out", TP // 2 - 1)]


def chunk_of(t, u):
    g, r = divmod(t, GROUP)
    if t == TP:
        return GP * CHUNKS
    return g * CHUNKS + 2 * r + u + (r > 0)


def counts_for(first_pair, t, u):
    return 2 if first_pair and (t, u) == (0, 1) else 1


def bank7_uses(first_pair, last_pair):
    uses = [u for u in BANK7 if not (first_pair and u[3] < 0) and not (last_pair and u[2] == "piece")]
    return uses + (BANK7_LAST if last_pair else [])


def attention_stage(k):
    nc, d = k.nc, k.dram
    with ExitStack() as ctx:
        def sb(name, shape, dt=F32):
            return ctx.enter_context(nc.sbuf_tensor(name, shape, dt))

        media = sb("media", [CTX, BATCH, DM])
        mediaT = sb("mediaT", [P, DK, BATCH, CTX])
        m_stats = sb("m_stats", [CTX, BATCH, 6])
        m_moments = sb("m_moments", [CTX, BATCH, 2])
        m_std = sb("m_std", [CTX, BATCH])
        m_rstd = sb("m_rstd", [CTX, BATCH])
        m_eps = sb("m_eps", [CTX, 1])
        ln = sb("ln", [P, 4, DK])
        n = NormBuffers(sb, "attention")
        n2 = NormBuffers(sb, "attention2")
        z = sb("attention_z", [P, TILES, DM])
        zT = sb("attention_zT", [P, DK, KEYS_ALL])
        w_q = sb("attention_w_q", [P, DK, P])
        w_k = sb("attention_w_k", [P, DK, P])
        w_v = sb("attention_w_v", [P, DK, P])
        w_o = sb("attention_w_o", [P, 2, DM])
        q_new = sb("q_new", [P, 2, SEQ], BF16)
        k_new = sb("k_new", [P, 2, KEYS_ALL], BF16)
        v_new = sb("v_new", [P, KT, 2, P], BF16)
        q_stack = sb("q_stack", [P, 2, SEQ], BF16)
        k_high = sb("k_high", [P, 2, KEYS_ALL], BF16)
        k_low = sb("k_low", [P, 2, KEYS_ALL], BF16)
        v_cols = sb("v_cols", [P, 2, KT, P], BF16)
        neg_max = sb("neg_max", [P, TP])
        den = sb("attention_den", [P, TP])
        inv_den = sb("inv_den", [P, TP])
        numer = sb("numer", [P, RING, KEYS_ALL])
        nT_high = sb("nT_high", [P, 2, KT, GROUP * P], F16)
        nT_low = sb("nT_low", [P, 2, KT, GROUP * P], F16)
        values = sb("values", [P, 2, GROUP * P])
        bank = ctx.enter_context(nc.psum_tensor("attention_psum", [P, 8, BANK], F32))
        logits_flat = bank[:, 0:5, :].rearrange("p a b -> p (a b)")
        ODD = 3 * BANK - CTX

        def logits(t):
            return logits_flat[:, ODD:ODD + KEYS_ALL] if t % 2 else logits_flat[:, 0:KEYS_ALL]

        def logits_z(t, half):
            return bank[:, (3 if t % 2 else 0) + half, :]

        def logits_ctx(t):
            return bank[:, 2, BANK - CTX:] if t % 2 else bank[:, 2, 0:CTX]

        def z_at(t):
            return CTX if t % 2 else 0

        def ctx_at(t):
            return 0 if t % 2 else SEQ

        with Prologue(nc) as pre:
            loaded = pre.semaphore("attention_loaded")
            m_done = pre.semaphore("media_done")
            m_var = pre.semaphore("media_var")
            m_root = pre.semaphore("media_root")
            m_turned = pre.semaphore("media_turned")
            block = pre.block()

            @block.sync
            def _(sp):
                sp.dma_start(media[:], d["ctx_1024"].rearrange("b l d -> l b d")).then_inc(loaded, 16)
                for i, name in enumerate(("m_g", "m_b", "l_g", "l_b")):
                    sp.dma_start(ln[:, i, :], d["L1_xattn_ln_" + name].rearrange("(c p) -> p c", p=P),
                                 allow_slow_non_contiguous=True).then_inc(loaded, 16)
                sp.wait_ge(loaded, 80)

            @block.vector
            def _(dve):
                dve.memset(m_eps[:], LN_EPS)
                dve.wait_ge(loaded, 80)
                for b in range(BATCH):
                    last = dve.bn_stats(m_stats[:, b, :], media[:, b, :])
                last.then_inc(m_done, 1)
                dve.wait_ge(m_done, 1)
                for b in range(BATCH):
                    last = dve.bn_aggr(m_moments[:, b, :], m_stats[:, b, :])
                last.then_inc(m_var, 1)
                dve.wait_ge(m_root, 1)
                dve.reciprocal(m_rstd[:], m_std[:]).then_inc(m_done, 1)
                dve.wait_ge(m_done, 2)
                for b in range(BATCH):
                    last = dve.tensor_scalar(media[:, b, :], media[:, b, :], m_moments[:, b, 0:1], m_rstd[:, b:b + 1],
                                             ALU.subtract, ALU.mult)
                last.then_inc(m_done, 1)
                dve.wait_ge(m_turned, 1)
                for c in range(DK):
                    last = dve.tensor_scalar(mediaT[:, c], bank[:, c, :].rearrange("p (b l) -> p b l", l=P)[:, :, 0:CTX],
                                             ln[:, 0, c:c + 1], ln[:, 1, c:c + 1], ALU.mult, ALU.add)
                last.then_inc(m_done, 1)
                dve.wait_ge(m_done, 4)

            @block.scalar
            def _(act):
                act.wait_ge(m_var, 1)
                act.activation(m_std[:], m_moments[:, :, 1], ACT.Sqrt, bias=m_eps[:, 0:1]).then_inc(m_root, 1)

            @block.tensor
            def _(pe):
                pe.wait_ge(m_done, 3)
                for b in range(BATCH):
                    for c in range(DK):
                        last = pe.transpose(bank[:, c, b * P:b * P + CTX], media[:, b, c * P:(c + 1) * P],
                                            k.ident[0:CTX, 0:CTX])
                last.then_inc(m_turned, 1)

        with ExitStack() as run, nc.Fori(0, BATCH) as b:
            signal = BatchSignals(run, nc, "attention_")
            chain = Chain(signal("chain"))
            moments_ready = signal("moments_ready")
            std_ready = signal("std_ready")
            normed = signal("normed")
            moments2_ready = signal("moments2_ready")
            std2_ready = signal("std2_ready")
            normed2 = signal("normed2")
            turned = signal("turned")
            zT_ready = signal("zT_ready")
            w_loaded = signal("w_loaded")
            wo_loaded = [signal("wo_loaded_a"), signal("wo_loaded_b")]
            piece_done = signal("piece_done")
            piece_high = signal("piece_high")
            piece_low = signal("piece_low")
            qk_stacked = [signal("qk_stacked_a"), signal("qk_stacked_b")]
            v_stacked = [signal("v_stacked_a"), signal("v_stacked_b")]
            scored = signal("scored")
            maxed = signal("maxed")
            numer_ready = signal("numer_ready")
            n_turned = signal("n_turned")
            n_high = signal("n_high")
            n_low = signal("n_low")
            values_done = signal("values_done")
            values_ready = signal("values_ready")
            den_ready = signal("den_ready")
            out_done = signal("out_done")
            added = signal("added")
            copied = signal("copied")
            block_ctx = ExitStack()
            block = block_ctx.enter_context(nc.Block())

            def numer_part(t, kt):
                if kt == TILES:
                    return numer[:, t % RING, ctx_at(t):ctx_at(t) + CTX]
                return numer[:, t % RING, z_at(t) + kt * P:z_at(t) + (kt + 1) * P]

            def parts_of(i, at=7):
                tiles = bank[:, at, :].rearrange("p (t a w) -> p t a w", a=2, w=A_W)
                if i == CTX_PIECE:
                    return [("k", SEQ, CTX, bank[:, at, 0:CTX]), ("v", TILES, 1, tiles[0:CTX, 1:2])]
                if i < CTX_PIECE:
                    return [("qk"[i // 2], i % 2 * BANK, BANK, bank[:, at, :])]
                return [("v", (i - CTX_PIECE - 1) * 4, 4, tiles)]

            def new_v(first, count, part):
                rows = CTX if first == TILES else P
                return v_new[0:rows, first:first + count, :, part * A_W:(part + 1) * A_W]

            def over_pairs(engine, body):
                body(0, True, False)
                with engine.Fori(1, PAIRS - 1) as pair:
                    body(pair, False, False)
                body(PAIRS - 1, False, True)

            @block.tensor
            def _(pe):
                transpose_on_tensor(pe, k, z, bank, normed2, 0, turned)

                def piece(i, at=7):
                    for kind, first, count, _ in parts_of(i):
                        if kind == "v":
                            for kt in range(first, first + count):
                                rows = CTX if kt == TILES else P
                                cols = P if kt == TILES else (kt - first) * P
                                for c in range(DK):
                                    last = pe.matmul(bank[0:rows, at, cols:cols + P], zT[:, c, kt * P:kt * P + rows],
                                                     w_v[:, c, :], start=(c == 0), stop=(c == DK - 1))
                        else:
                            w = w_q if kind == "q" else w_k
                            for c in range(DK):
                                last = pe.matmul(bank[:, at, 0:count], w[:, c, :], zT[:, c, first:first + count],
                                                 start=(c == 0), stop=(c == DK - 1))
                    last.then_inc(piece_done.sem, 1)

                pe.wait_ge(zT_ready.sem, 4)
                pe.wait_ge(copied.sem, 1)
                pe.wait_ge(w_loaded.sem, 48)
                for i in range(PIECES):
                    piece(i, FIRST_BANKS[i])
                pe.wait_ge(piece_low.sem, PIECES)

                def score_z(pair, t):
                    a, i = divmod(t % TP, TILES)
                    if i == 0:
                        pe.wait_ge(qk_stacked[a].sem, pair * QK_STACKED + (1 + t // TP) * QK_STACKED)
                    pe.wait_ge(numer_ready.sem, pair * TP + t + 1)
                    for half in range(HALVES):
                        for part, kx in enumerate((k_high, k_low)):
                            pe.matmul(logits_z(t, half), q_stack[:, a, i * P:(i + 1) * P],
                                      kx[:, a, half * BANK:(half + 1) * BANK], start=(part == 0), stop=(part == 1))

                def score_ctx(pair, t):
                    a, i = divmod(t % TP, TILES)
                    pe.wait_ge(numer_ready.sem, pair * TP + t + 2)
                    for part, kx in enumerate((k_high, k_low)):
                        last = pe.matmul(logits_ctx(t), q_stack[:, a, i * P:(i + 1) * P], kx[:, a, SEQ:],
                                         start=(part == 0), stop=(part == 1))
                    last.then_inc(scored.sem, 1)

                score_z(0, 0)
                score_ctx(0, 0)
                score_z(0, 1)

                def body(pair, first, last_pair):
                    uses = bank7_uses(first, last_pair)

                    def free_bank7(at):
                        if at == 0:
                            pe.wait_ge(piece_low.sem, pair * PIECES + PIECES)
                            return
                        _, _, before, m = uses[at - 1]
                        if before == "piece":
                            pe.wait_ge(piece_low.sem, pair * PIECES + PIECES + m + 1)
                        elif before == "out":
                            pe.wait_ge(added.sem, pair * (TP // 2) + m + 2)
                        else:
                            pe.wait_ge(values_ready.sem, pair * GP + m + 1)

                    def turn(t, u):
                        chunk = chunk_of(t, u)
                        if u == 0:
                            pe.wait_ge(numer_ready.sem, pair * TP + t + 3)
                        pe.wait_ge(n_low.sem, pair * GP * CHUNKS + chunk + 1)
                        out = bank[:, 5 + chunk % 2, :]
                        for s in range(GROUP):
                            if u == CTX_CHUNK:
                                last = pe.transpose(out[0:CTX, s * P:(s + 1) * P], numer_part(t - GROUP + s, TILES), k.ident[:])
                            else:
                                last = pe.transpose(out[:, s * P:(s + 1) * P], numer_part(t, 4 * u + s), k.ident[:])
                        last.then_inc(n_turned.sem, counts_for(first, t, u))

                    def values_of(g):
                        a = g % GP // (GP // 2)
                        if g in (0, GP // 2):
                            pe.wait_ge(v_stacked[a].sem, pair * V_STACKED + V_STACKED)
                        pe.wait_ge(n_low.sem, pair * GP * CHUNKS + chunk_of((g + 1) * GROUP, CTX_CHUNK) + 3)
                        for kt in range(KT):
                            rows = CTX if kt == TILES else P
                            for part, nx in enumerate((nT_high, nT_low)):
                                last = pe.matmul(bank[:, 7, :], v_cols[0:rows, a, kt, :], nx[0:rows, g % 2, kt, :],
                                                 start=(kt == 0 and part == 0), stop=(kt == KT - 1 and part == 1))
                        last.then_inc(values_done.sem, 1)

                    def out_of(i):
                        g, r = divmod(i, 2)
                        a = g % GP // (GP // 2)
                        if i in (0, GP):
                            pe.wait_ge(wo_loaded[a].sem, pair * 32 + 32)
                        pe.wait_ge(values_ready.sem, pair * GP + g + 1)
                        for s in range(2):
                            last = pe.matmul(bank[:, 7, s * DM:(s + 1) * DM],
                                             values[:, g % 2, (2 * r + s) * P:(2 * r + s + 1) * P], w_o[:, a, :],
                                             start=True, stop=True)
                        last.then_inc(out_done.sem, 1)

                    def use_bank7(t, slot):
                        for at, (when, where, use, i) in enumerate(uses):
                            if (when, where) != (t, slot):
                                continue
                            free_bank7(at)
                            if use == "piece":
                                if i == 0:
                                    pe.wait_ge(w_loaded.sem, pair * 48 + 96)
                                piece(i)
                            elif use == "values":
                                values_of(i)
                            else:
                                out_of(i)

                    ahead = TP if last_pair else TP + 2
                    for t in range(TP):
                        if t + 1 < ahead:
                            score_ctx(pair, t + 1)
                        turn(t, 0)
                        use_bank7(t, "early")
                        if t % GROUP != 1:
                            turn(t, 1)
                        use_bank7(t, "middle")
                        if t + 2 < ahead:
                            score_z(pair, t + 2)
                        if t % GROUP == 1:
                            turn(t, 1)
                        use_bank7(t, "end")
                        if t % GROUP == 0 and not (first and t == 0):
                            turn(t, CTX_CHUNK)
                    if last_pair:
                        turn(TP, CTX_CHUNK)
                        use_bank7(TP, "end")

                over_pairs(pe, body)

            def split_high(act, i, scale_q, at=7):
                for kind, first, count, psum in parts_of(i, at):
                    if kind == "q":
                        last = act.activation(q_new[:, 0, first:first + count], psum, ACT.Copy, scale=scale_q)
                    elif kind == "k":
                        last = act.copy(k_new[:, 0, first:first + count], psum)
                    else:
                        last = act.copy(new_v(first, count, 0), psum)
                last.then_inc(piece_high.sem, 1)

            def split_low(dve, i, scale_q, at=7):
                for kind, first, count, psum in parts_of(i, at):
                    if kind == "q":
                        q = q_new[:, :, first:first + count]
                        last = dve.scalar_tensor_tensor(out=q[:, 1], in0=psum, scalar=scale_q, in1=q[:, 0],
                                                        op0=ALU.mult, op1=ALU.subtract)
                    elif kind == "k":
                        keys = k_new[:, :, first:first + count]
                        last = dve.tensor_tensor(keys[:, 1], psum, keys[:, 0], ALU.subtract)
                    else:
                        last = dve.tensor_tensor(new_v(first, count, 1), psum, new_v(first, count, 0), ALU.subtract)
                last.then_inc(piece_low.sem, 1)

            SCALE = float(A_W) ** -0.5

            @block.scalar
            def _(act):
                roots_on_scalar(act, n, moments_ready, std_ready)
                roots_on_scalar(act, n2, moments2_ready, std2_ready)
                for q in range(4):
                    c = q % DK
                    act.wait_ge(turned.sem, q + 1)
                    act.activation(columns_of(zT, q), bank[:, q, :], ACT.Identity, scale=ln[:, 2, c:c + 1],
                                   bias=ln[:, 3, c:c + 1]).then_inc(zT_ready.sem, 1)
                for i in range(PIECES):
                    act.wait_ge(piece_done.sem, i + 1)
                    split_high(act, i, SCALE, FIRST_BANKS[i])

                def exps(pair, t):
                    act.wait_ge(maxed.sem, pair * TP + t + 1)
                    act.activation(numer[:, t % RING, :], logits(t), ACT.Exp, bias=neg_max[:, t % TP:t % TP + 1],
                                   accum_out=den[:, t % TP:t % TP + 1]).then_inc(numer_ready.sem, 1)

                exps(0, 0)

                def body(pair, first, last_pair):
                    uses = bank7_uses(first, last_pair)

                    def high(t, u):
                        g, r = divmod(t, GROUP)
                        chunk = chunk_of(t, u)
                        act.wait_ge(n_turned.sem, pair * GP * CHUNKS + chunk + 1)
                        if r == 0 and u == 0:
                            act.wait_ge(values_done.sem, pair * GP + g + 1)
                        src = bank[:, 5 + chunk % 2, :].rearrange("p (s q) -> p s q", q=P)
                        if u < 2:
                            dst = nT_high[:, g % 2, 4 * u:4 * u + 4, r * P:(r + 1) * P]
                        else:
                            dst, src = nT_high[0:CTX, (g - 1) % 2, TILES, :], bank[0:CTX, 5 + chunk % 2, :]
                        act.copy(dst, src).then_inc(n_high.sem, counts_for(first, t, u))

                    def use_bank7(t, slot):
                        for when, where, use, i in uses:
                            if (when, where) != (t, slot):
                                continue
                            if use == "piece":
                                act.wait_ge(piece_done.sem, pair * PIECES + PIECES + i + 1)
                                if i == 0:
                                    for done in qk_stacked:
                                        act.wait_ge(done.sem, pair * QK_STACKED + QK_STACKED)
                                if i == CTX_PIECE:
                                    for done in v_stacked:
                                        act.wait_ge(done.sem, pair * V_STACKED + V_STACKED)
                                split_high(act, i, SCALE)
                            elif use == "values":
                                act.wait_ge(values_done.sem, pair * GP + i + 3)
                                act.copy(values[:, i % 2, :], bank[:, 7, :]).then_inc(values_ready.sem, 1)

                    for t in range(TP):
                        high(t, 0)
                        if t % GROUP != 1:
                            high(t, 1)
                        if t + 1 < TP or not last_pair:
                            exps(pair, t + 1)
                        if t % GROUP == 1:
                            high(t, 1)
                        use_bank7(t, "end")
                        if t % GROUP == 0 and not (first and t == 0):
                            high(t, CTX_CHUNK)
                    if last_pair:
                        high(TP, CTX_CHUNK)
                        use_bank7(TP, "end")

                over_pairs(act, body)

            @block.vector
            def _(dve):
                dve.sem_inc(numer_ready.sem, 2)
                dve.sem_inc(n_low.sem, 2)
                dve.sem_inc(values_done.sem, 2)
                dve.sem_inc(added.sem, 1)
                dve.tensor_copy(zT[:, :, SEQ:].rearrange("p c (o l) -> p c o l", o=1),
                                mediaT[:, :, bass.ds(b, 1), :]).then_inc(copied.sem, 1)
                norm_on_vector(dve, n, lambda j: k.X[:, b * TILES + j, :], z, chain, std_ready, moments_ready, normed)
                dve.wait_ge(normed.sem, TILES)
                norm_on_vector(dve, n2, lambda j: z[:, j, :], z, chain, std2_ready, moments2_ready, normed2)
                for i in range(PIECES):
                    dve.wait_ge(piece_high.sem, i + 1)
                    split_low(dve, i, SCALE, FIRST_BANKS[i])

                def maximum(pair, t):
                    dve.wait_ge(scored.sem, pair * TP + t + 1)
                    dve.tensor_reduce(neg_max[:, t % TP:t % TP + 1], logits(t), AXIS.X, ALU.max,
                                      negate=True).then_inc(maxed.sem, 1)

                maximum(0, 0)

                def body(pair, first, last_pair):
                    uses = bank7_uses(first, last_pair)

                    def low(t, u):
                        g, r = divmod(t, GROUP)
                        chunk = chunk_of(t, u)
                        dve.wait_ge(n_high.sem, pair * GP * CHUNKS + chunk + 1)
                        src = bank[:, 5 + chunk % 2, :].rearrange("p (s q) -> p s q", q=P)
                        if u < 2:
                            at = (slice(None), g % 2, slice(4 * u, 4 * u + 4), slice(r * P, (r + 1) * P))
                        else:
                            at, src = (slice(0, CTX), (g - 1) % 2, TILES, slice(None)), bank[0:CTX, 5 + chunk % 2, :]
                        dve.tensor_tensor(nT_low[at], src, nT_high[at],
                                          ALU.subtract).then_inc(n_low.sem, counts_for(first, t, u))

                    def add_out(i):
                        g, r = divmod(i, 2)
                        first_tile = g % GP * GROUP
                        cols = slice(first_tile, first_tile + GROUP)
                        if r == 0:
                            dve.reciprocal(inv_den[:, cols], den[:, cols]).then_inc(den_ready.sem, 1)
                        dve.wait_ge(out_done.sem, pair * (TP // 2) + i + 1)
                        dve.wait_ge(den_ready.sem, pair * GP + g + 1)
                        for s in range(2):
                            tile = first_tile + 2 * r + s
                            x = k.X[:, b * TILES + tile % TILES, :]
                            last = dve.scalar_tensor_tensor(out=x, in0=bank[:, 7, s * DM:(s + 1) * DM],
                                                            scalar=inv_den[:, tile:tile + 1], in1=x,
                                                            op0=ALU.mult, op1=ALU.add)
                        last.then_inc(added.sem, 1)

                    def use_bank7(t, slot):
                        for when, where, use, i in uses:
                            if (when, where) != (t, slot):
                                continue
                            if use == "piece":
                                dve.wait_ge(piece_high.sem, pair * PIECES + PIECES + i + 1)
                                split_low(dve, i, SCALE)
                            elif use == "out":
                                add_out(i)

                    for t in range(TP):
                        if t + 1 < TP or not last_pair:
                            maximum(pair, t + 1)
                        use_bank7(t, "early")
                        low(t, 0)
                        use_bank7(t, "middle")
                        low(t, 1)
                        use_bank7(t, "end")
                        if t % GROUP == 0 and not (first and t == 0):
                            low(t, CTX_CHUNK)
                    if last_pair:
                        low(TP, CTX_CHUNK)
                        use_bank7(TP, "end")

                over_pairs(dve, body)
                dve.wait_ge(added.sem, PAIRS * TP // 2 + 1)

            @block.sync
            def _(sp):
                heads_of = {"q": d["L1_xattn_Wq"], "k": d["L1_xattn_Wkv"][:, 0:INNER], "v": d["L1_xattn_Wkv"][:, INNER:]}
                w_rows = {x: w.rearrange("(c p) n -> p c n", p=P) for x, w in heads_of.items()}

                def load_weights(pair):
                    for dst, x in ((w_q, "q"), (w_k, "k"), (w_v, "v")):
                        sp.dma_start(dst[:], w_rows[x][:, :, bass.ds(pair * P, P)]).then_inc(w_loaded.sem, 16)

                def load_out_weights(pair, a):
                    for half in range(2):
                        sp.dma_start(w_o[half * A_W:(half + 1) * A_W, a, :],
                                     d["L1_xattn_Wout"][bass.ds(pair * P + a * A_W, A_W), :]).then_inc(wo_loaded[a].sem, 16)

                def stack_qk(a):
                    rows = slice(a * A_W, (a + 1) * A_W)
                    upper, lower = slice(0, A_W), slice(A_W, P)
                    for dst, src in ((q_stack[upper, a, :], q_new[rows, 0, :]), (q_stack[lower, a, :], q_new[rows, 1, :]),
                                     (k_high[upper, a, :], k_new[rows, 0, :]), (k_high[lower, a, :], k_new[rows, 0, :]),
                                     (k_low[upper, a, :], k_new[rows, 1, :]), (k_low[lower, a, :], k_new[rows, 1, :])):
                        sp.dma_start(dst, src).then_inc(qk_stacked[a].sem, 16)

                def stack_v(a):
                    sp.dma_start(v_cols[:, a, 0:TILES], v_new[:, 0:TILES, a, :]).then_inc(v_stacked[a].sem, 16)
                    sp.dma_start(v_cols[0:CTX, a, TILES], v_new[0:CTX, TILES, a, :]).then_inc(v_stacked[a].sem, 16)

                load_weights(0)
                load_out_weights(0, 0)
                sp.wait_ge(piece_low.sem, CTX_PIECE + 1)
                for a in range(2):
                    stack_qk(a)

                def body(pair, first, last_pair):
                    if not last_pair:
                        sp.wait_ge(piece_done.sem, pair * PIECES + PIECES)
                        load_weights(pair + 1)
                    sp.wait_ge(piece_low.sem, pair * PIECES + PIECES)
                    stack_v(0)
                    if not first:
                        sp.wait_ge(values_done.sem, pair * GP + 2)
                    stack_v(1)
                    if not first:
                        sp.wait_ge(added.sem, pair * (TP // 2) + 1)
                    load_out_weights(pair, 1)
                    if not last_pair:
                        sp.wait_ge(piece_low.sem, pair * PIECES + PIECES + CTX_PIECE + 1)
                        stack_qk(0)
                        sp.wait_ge(added.sem, pair * (TP // 2) + 1 + TP // 4)
                        load_out_weights(pair + 1, 0)
                        sp.wait_ge(scored.sem, pair * TP + TP)
                        stack_qk(1)

                over_pairs(sp, body)

            block_ctx.close()
            signal.clear()



FP8_MAX = 448.0
FP8_LEAST_NORMAL = 2.0 ** -6
EXPONENT_BITS = 0x7F800000
ROUNDER = 1.5 * 2.0 ** 20
UNITS = BATCH * TILES // 4


def round_to_fp8(dve, v, c, out, chain):
    chain.link(dve, dve.tensor_scalar(c.bitcast(I32), v.bitcast(I32), EXPONENT_BITS, None, ALU.bitwise_and))
    chain.link(dve, dve.tensor_scalar(c, c, FP8_LEAST_NORMAL, ROUNDER, ALU.max, ALU.mult))
    chain.link(dve, dve.scalar_tensor_tensor(out=v, in0=v, scalar=-FP8_MAX, in1=c, op0=ALU.max, op1=ALU.add))
    return dve.tensor_tensor(out, v, c, ALU.subtract)


def quantized_stage(k):
    nc, d = k.nc, k.dram
    with ExitStack() as ctx:
        def sb(name, shape, dt=F32):
            return ctx.enter_context(nc.sbuf_tensor(name, shape, dt))

        stats = sb("quant_stats", [P, BATCH * TILES, 6])
        moments = sb("quant_moments", [P, BATCH * TILES, 2])
        std = sb("quant_std", [P, BATCH * TILES])
        rstd = sb("quant_rstd", [P, BATCH * TILES])
        eps = sb("quant_eps", [P, 1])
        y = sb("quant_y", [P, BATCH * TILES, DM])
        w = sb("quant_w", [P, DK * DM])
        w_round = sb("w_round", [P, DK * DM])
        w_fp8 = sb("w_fp8", [P, DK, DM], BF16)
        bias = sb("quant_bias", [P, DM])
        tops = sb("tops", [P, BATCH])
        top = sb("top", [P, 2])
        top_row = sb("top_row", [2, 1])
        top_diag = sb("top_diag", [2, 2])
        scale = sb("quant_scale", [P, 2])
        inverse = sb("inverse", [P, 2])
        inverse_both = sb("inverse_both", [P, 1])
        v = sb("quant_v", [P, 2, 4 * DM])
        c = sb("quant_c", [P, 2, 4 * DM])
        x_fp8 = sb("x_fp8", [P, TILES, DM])
        xT_fp8 = sb("xT_fp8", [P, DK, SEQ], BF16)
        out = sb("quant_out", [P, 2, 2, DM], BF16)
        bank = ctx.enter_context(nc.psum_tensor("quant_psum", [P, 8, BANK], F32))

        with Prologue(nc) as pre:
            chain = Chain(pre.counter("quant_norm_chain"))
            moments_ready = pre.semaphore("quant_moments_ready")
            std_ready = pre.semaphore("quant_std_ready")
            rstd_ready = pre.semaphore("quant_rstd_ready")
            pool_normed = pre.semaphore("quant_pool_normed")
            block = pre.block()

            def norm_tile(engine, g):
                return engine.tensor_scalar(y[:, g, :], k.X[:, g, :], moments[:, g, 0:1], rstd[:, g:g + 1],
                                            ALU.subtract, ALU.mult)

            @block.vector
            def _(dve):
                dve.memset(eps[:], LN_EPS)
                for g in range(BATCH * TILES):
                    last = dve.bn_stats(stats[:, g, :], k.X[:, g, :])
                chain.link(dve, last)
                for g in range(BATCH * TILES):
                    last = dve.bn_aggr(moments[:, g, :], stats[:, g, :])
                last.then_inc(moments_ready, 1)
                dve.wait_ge(std_ready, 1)
                dve.reciprocal(rstd[:], std[:]).then_inc(rstd_ready, 1)
                dve.wait_ge(rstd_ready, 1)
                for g in range(BATCH * TILES):
                    if g % 4 != 3:
                        last = norm_tile(dve, g)
                chain.link(dve, last)
                dve.wait_ge(pool_normed, 1)
                chain.link(dve, dve.tensor_reduce(tops[:], y[:].rearrange("p (b j) n -> p b (j n)", b=BATCH), AXIS.X,
                                                  ALU.max, apply_absolute_value=True))

            @block.gpsimd
            def _(pool):
                pool.wait_ge(rstd_ready, 1)
                for g in range(3, BATCH * TILES, 4):
                    last = norm_tile(pool, g)
                last.then_inc(pool_normed, 1)

            @block.scalar
            def _(act):
                act.wait_ge(moments_ready, 1)
                act.activation(std[:], moments[:, :, 1], ACT.Sqrt, bias=eps[:, 0:1]).then_inc(std_ready, 1)

        with Prologue(nc) as pre:
            loaded = pre.semaphore("quant_loaded")
            top_ready = pre.semaphore("top_ready")
            top_turned = pre.semaphore("top_turned")
            diag_ready = pre.semaphore("diag_ready")
            top_spread = pre.semaphore("top_spread")
            chain = Chain(pre.counter("quant_scale_chain"))
            block = pre.block()

            @block.sync
            def _(sp):
                sp.dma_start(w[:].rearrange("p (c n) -> p c n", c=DK),
                             d["L1_ffn_weight"].rearrange("(c p) n -> p c n", p=P)).then_inc(loaded, 16)
                row = d["L1_ffn_bias"].rearrange("(o n) -> o n", o=1)
                sp.dma_start(bias[:], row.broadcast_to([P, DM])).then_inc(loaded, 16)
                sp.wait_ge(loaded, 32)

            @block.vector
            def _(dve):
                dve.tensor_reduce(top[:, 0:1], tops[:], AXIS.X, ALU.max)
                dve.wait_ge(loaded, 32)
                dve.tensor_reduce(top[:, 1:2], w[:], AXIS.X, ALU.max,
                                  apply_absolute_value=True).then_inc(top_ready, 1)
                dve.wait_ge(top_turned, 1)
                chain.link(dve, dve.tensor_reduce(top_row[:], bank[0:2, 0, 0:P], AXIS.X, ALU.max))
                dve.tensor_scalar(top_diag[:], k.ident[0:2, 0:2], top_row[:], None, ALU.mult).then_inc(diag_ready, 1)
                dve.wait_ge(top_spread, 1)
                chain.link(dve, dve.tensor_scalar(scale[:], bank[:, 1, 0:2], 1e-12, None, ALU.max))
                chain.link(dve, dve.reciprocal(scale[:], scale[:]))
                chain.link(dve, dve.tensor_scalar(scale[:], scale[:], FP8_MAX, FP8_MAX, ALU.mult, ALU.min))
                chain.link(dve, dve.reciprocal(inverse[:], scale[:]))
                dve.tensor_tensor(inverse_both[:], inverse[:, 0:1], inverse[:, 1:2], ALU.mult)
                chain.link(dve, dve.tensor_scalar(w[:], w[:], scale[:, 1:2], FP8_MAX, ALU.mult, ALU.min))
                chain.link(dve, round_to_fp8(dve, w[:], w_round[:], w_fp8[:].rearrange("p c n -> p (c n)"), chain))

            @block.tensor
            def _(pe):
                pe.wait_ge(top_ready, 1)
                pe.transpose(bank[0:2, 0, 0:P], top[:], k.ident[:]).then_inc(top_turned, 1)
                pe.wait_ge(diag_ready, 1)
                pe.matmul(bank[:, 1, 0:2], k.ones[0:2, :], top_diag[:], start=True, stop=True).then_inc(top_spread, 1)

        with Prologue(nc) as pre:
            chain = Chain(pre.counter("quant_chain"))
            scaled = pre.semaphore("quant_scaled")
            v_ready = pre.semaphore("quant_v_ready")
            rounded = pre.semaphore("quant_rounded")
            turned = pre.semaphore("quant_turned")
            xT_ready = pre.semaphore("quant_xT_ready")
            multiplied = pre.semaphore("quant_multiplied")
            out_ready = pre.semaphore("quant_out_ready")
            added = pre.semaphore("quant_added")
            block = pre.block()

            def columns(u, i):
                return xT_fp8[:, i, u % 2 * BANK:(u % 2 + 1) * BANK]

            @block.gpsimd
            def _(pool):
                for u in range(UNITS):
                    pool.wait_ge(scaled, u + 1)
                    pool.tensor_scalar(v[:, u % 2, :], v[:, u % 2, :], FP8_MAX, None, ALU.min).then_inc(v_ready, 1)

            @block.vector
            def _(dve):
                def add_out(u):
                    for pair in range(2):
                        m = 2 * u + pair
                        dve.wait_ge(multiplied, m + 1)
                        for i in range(2):
                            dve.scalar_tensor_tensor(out=out[:, pair, i, :],
                                                     in0=bank[:, 4 + m % 4, i * DM:(i + 1) * DM],
                                                     scalar=inverse_both[:], in1=bias[:], op0=ALU.mult,
                                                     op1=ALU.add).then_inc(out_ready, 1)
                        dve.wait_ge(out_ready, 2 * m + 2)
                        x = k.X[:, 2 * m:2 * m + 2, :]
                        dve.tensor_tensor(x, x, out[:, pair], ALU.add).then_inc(added, 1)
                        dve.wait_ge(added, m + 1)

                for u in range(UNITS):
                    dve.wait_ge(v_ready, u + 1)
                    if u >= 2:
                        dve.wait_ge(turned, DK * (u - 1))
                    tiles = x_fp8[:, u % 2 * 4:u % 2 * 4 + 4, :].rearrange("p j n -> p (j n)")
                    round_to_fp8(dve, v[:, u % 2, :], c[:, u % 2, :], tiles, chain).then_inc(rounded, 1)
                    if u:
                        add_out(u - 1)
                add_out(UNITS - 1)

            @block.scalar
            def _(act):
                for u in range(UNITS + 1):
                    if u < UNITS:
                        if u >= 2:
                            act.wait_ge(rounded, u - 1)
                        act.mul(v[:, u % 2, :], y[:, 4 * u:4 * u + 4, :].rearrange("p j n -> p (j n)"),
                                scale[:, 0:1]).then_inc(scaled, 1)
                    if u:
                        for i in range(DK):
                            act.wait_ge(turned, DK * (u - 1) + i + 1)
                            if u >= 3:
                                act.wait_ge(multiplied, 2 * (u - 2))
                            act.copy(columns(u - 1, i), bank[:, (u - 1) % 2 * DK + i, :]).then_inc(xT_ready, 1)

            @block.tensor
            def _(pe):
                def multiply(u):
                    pe.wait_ge(xT_ready, DK * (u + 1))
                    if u >= 2:
                        pe.wait_ge(added, 2 * (u - 1))
                    for j in range(4):
                        for i in range(DK):
                            last = pe.matmul(bank[:, 4 + (2 * u + j // 2) % 4, (j % 2) * DM:(j % 2 + 1) * DM],
                                             columns(u, i)[:, j * P:(j + 1) * P], w_fp8[:, i, :],
                                             start=(i == 0), stop=(i == DK - 1))
                        if j % 2:
                            last.then_inc(multiplied, 1)

                for u in range(UNITS):
                    pe.wait_ge(rounded, u + 1)
                    if u >= 2:
                        pe.wait_ge(xT_ready, DK * (u - 1))
                    for i in range(DK):
                        for j in range(4):
                            last = pe.transpose(bank[:, u % 2 * DK + i, j * P:(j + 1) * P],
                                                x_fp8[:, u % 2 * 4 + j, i * P:(i + 1) * P], k.ident[:])
                        last.then_inc(turned, 1)
                    if u:
                        multiply(u - 1)
                multiply(UNITS - 1)


def decoder(nc, dram):
    with ExitStack() as ctx:
        k = Kernel(nc, ctx, dram)
        load_residual(k)
        for stage in (mamba_stage, memory_stage, expert_stage, wavelet_stage, attention_stage, quantized_stage):
            stage(k)
        store_residual(k)



TRANSPOSED = ("L0_attn_W_in", "L0_attn_W_x", "L0_attn_W_dt", "L0_attn_W_out", "L0_ffn_Wq", "L0_ffn_down_embed",
              "L1_ffn_weight")


def kernel(**inputs):
    import numpy as np
    import concourse.bacc as bacc
    from concourse.bass_utils import run_bass_kernel_spmd

    nc = bacc.Bacc("TRN2", target_bir_lowering=False, num_devices=1)
    arrays, dram = {}, {}
    for name, value in inputs.items():
        a = np.asarray(value)
        if name in TRANSPOSED:
            a = a.T
        if name == "L0_ffn_keys":
            a = a.transpose(3, 2, 0, 1)
        a = np.ascontiguousarray(a)
        arrays[f"in_{name}"] = a
        dram[name] = nc.dram_tensor(f"in_{name}", a.shape, mybir.dt.from_np(a.dtype), kind="ExternalInput").ap()
    dram["out"] = nc.dram_tensor("out_x", (BATCH, SEQ, DM), F32, kind="ExternalOutput").ap()
    decoder(nc, dram)
    result = run_bass_kernel_spmd(nc, [arrays], core_ids=[0])
    return result.results[0]["out_x"]
```
